# Optimizing a Trainium2 kernel written in Bass

```python
import numpy as np
import jax
import jax.numpy as jnp

def _softmax(x, axis=-1):
    return jax.nn.softmax(x, axis=axis)

def _gelu(x):
    return jax.nn.gelu(x, approximate=True)

def _silu(x):
    return jax.nn.silu(x)

def _sigmoid(x):
    return jax.nn.sigmoid(x)

def _layernorm(x, axis=-1, eps=1e-05):
    m = jnp.mean(x, axis=axis, keepdims=True)
    v = jnp.var(x, axis=axis, keepdims=True)
    return (x - m) / jnp.sqrt(v + eps)

def _scatter_add(tgt, idx, src, axis=0):
    return tgt.at[idx].add(src)

def _segment_sum(src, seg, n):
    return jax.ops.segment_sum(src, seg, n)
kernel_name = 'mk_rec_standalone_d1_rec_r8_c5f4e7'

def setup_inputs(seed: int=0):
    np.random.seed(seed)
    _w = jnp.asarray

    def _rec_inputs():
        import jax
        import jax.numpy as jnp
        _rk = jax.random.key(seed)
        r_strength = jax.random.uniform(jax.random.fold_in(_rk, 1), (1024, 4, 4), jnp.float32, 0.0, 0.999994)
        r_x = 7.22013e-05 + 1.00017 * jax.random.normal(jax.random.fold_in(_rk, 2), (1024, 256), jnp.float32)
        return (r_strength, r_x)
    r_strength, r_x = _rec_inputs()

    def _L0_rec_setup():
        import jax, jax.numpy as jnp
        import numpy as np
        B, IN, HID, D, N, OUT = (512, 256, 256, 512, 4, 512)
        H = 8
        HD = D // H

        def _ln(x, g, b):
            m = x.mean(-1, keepdims=True)
            v = ((x - m) ** 2).mean(-1, keepdims=True)
            return (x - m) / jnp.sqrt(v + 1e-05) * g + b
        key = jax.random.key(seed)
        ks = jax.random.split(key, 32)

        def nrm(k, shape, scale=0.02):
            return jax.random.normal(k, shape, jnp.float32) * scale
        inp = {}
        inp['x'] = jax.random.normal(ks[0], (B, IN), jnp.float32)
        inp['strength'] = jax.random.uniform(ks[1], (B, N, N), jnp.float32)
        for t, i in (('er', 2), ('ei', 4)):
            inp[t + '_W1'] = nrm(ks[i], (HID, IN))
            inp[t + '_b1'] = jnp.zeros((HID,), jnp.float32)
            inp[t + '_g1'] = jnp.ones((HID,), jnp.float32)
            inp[t + '_be1'] = jnp.zeros((HID,), jnp.float32)
            inp[t + '_W2'] = nrm(ks[i + 1], (N * D, HID))
            inp[t + '_b2'] = jnp.zeros((N * D,), jnp.float32)
        names = ['Wq_r', 'Wq_i', 'Wk_r', 'Wk_i', 'Wv_r', 'Wv_i', 'Wo_r', 'Wo_i']
        for j, nm in enumerate(names):
            inp[nm] = nrm(ks[6 + j], (D, D))
            inp['b' + nm[1:]] = jnp.zeros((D,), jnp.float32)
        inp['int_Wr'] = jnp.tile(jnp.eye(D, dtype=jnp.float32)[None], (N, 1, 1))
        inp['int_Wi'] = jnp.zeros((N, D, D), jnp.float32)
        inp['meas_Mr'] = nrm(ks[20], (OUT, D), 1.0 / np.sqrt(D))
        inp['meas_Mi'] = nrm(ks[21], (OUT, D), 1.0 / np.sqrt(D))
        inp['post_W'] = nrm(ks[22], (OUT, OUT))
        inp['post_b'] = jnp.zeros((OUT,), jnp.float32)
        inp['post_g'] = jnp.ones((OUT,), jnp.float32)
        inp['post_be'] = jnp.zeros((OUT,), jnp.float32)
        return inp
    _L0_rec_all = _L0_rec_setup()
    _L0_rec_in = {k: v for k, v in _L0_rec_all.items() if k in ('er_W1', 'er_b1', 'er_g1', 'er_be1', 'er_W2', 'er_b2', 'ei_W1', 'ei_b1', 'ei_g1', 'ei_be1', 'ei_W2', 'ei_b2', 'Wq_r', 'bq_r', 'Wq_i', 'bq_i', 'Wk_r', 'bk_r', 'Wk_i', 'bk_i', 'Wv_r', 'bv_r', 'Wv_i', 'bv_i', 'Wo_r', 'bo_r', 'Wo_i', 'bo_i', 'int_Wr', 'int_Wi', 'meas_Mr', 'meas_Mi', 'post_W', 'post_b', 'post_g', 'post_be')}
    del _L0_rec_all
    return {'r_strength': r_strength, 'r_x': r_x, 'L0_rec_er_W1': _L0_rec_in['er_W1'], 'L0_rec_er_b1': _L0_rec_in['er_b1'], 'L0_rec_er_g1': _L0_rec_in['er_g1'], 'L0_rec_er_be1': _L0_rec_in['er_be1'], 'L0_rec_er_W2': _L0_rec_in['er_W2'], 'L0_rec_er_b2': _L0_rec_in['er_b2'], 'L0_rec_ei_W1': _L0_rec_in['ei_W1'], 'L0_rec_ei_b1': _L0_rec_in['ei_b1'], 'L0_rec_ei_g1': _L0_rec_in['ei_g1'], 'L0_rec_ei_be1': _L0_rec_in['ei_be1'], 'L0_rec_ei_W2': _L0_rec_in['ei_W2'], 'L0_rec_ei_b2': _L0_rec_in['ei_b2'], 'L0_rec_Wq_r': _L0_rec_in['Wq_r'], 'L0_rec_bq_r': _L0_rec_in['bq_r'], 'L0_rec_Wq_i': _L0_rec_in['Wq_i'], 'L0_rec_bq_i': _L0_rec_in['bq_i'], 'L0_rec_Wk_r': _L0_rec_in['Wk_r'], 'L0_rec_bk_r': _L0_rec_in['bk_r'], 'L0_rec_Wk_i': _L0_rec_in['Wk_i'], 'L0_rec_bk_i': _L0_rec_in['bk_i'], 'L0_rec_Wv_r': _L0_rec_in['Wv_r'], 'L0_rec_bv_r': _L0_rec_in['bv_r'], 'L0_rec_Wv_i': _L0_rec_in['Wv_i'], 'L0_rec_bv_i': _L0_rec_in['bv_i'], 'L0_rec_Wo_r': _L0_rec_in['Wo_r'], 'L0_rec_bo_r': _L0_rec_in['bo_r'], 'L0_rec_Wo_i': _L0_rec_in['Wo_i'], 'L0_rec_bo_i': _L0_rec_in['bo_i'], 'L0_rec_int_Wr': _L0_rec_in['int_Wr'], 'L0_rec_int_Wi': _L0_rec_in['int_Wi'], 'L0_rec_meas_Mr': _L0_rec_in['meas_Mr'], 'L0_rec_meas_Mi': _L0_rec_in['meas_Mi'], 'L0_rec_post_W': _L0_rec_in['post_W'], 'L0_rec_post_b': _L0_rec_in['post_b'], 'L0_rec_post_g': _L0_rec_in['post_g'], 'L0_rec_post_be': _L0_rec_in['post_be']}

def reference(r_strength, r_x, L0_rec_er_W1, L0_rec_er_b1, L0_rec_er_g1, L0_rec_er_be1, L0_rec_er_W2, L0_rec_er_b2, L0_rec_ei_W1, L0_rec_ei_b1, L0_rec_ei_g1, L0_rec_ei_be1, L0_rec_ei_W2, L0_rec_ei_b2, L0_rec_Wq_r, L0_rec_bq_r, L0_rec_Wq_i, L0_rec_bq_i, L0_rec_Wk_r, L0_rec_bk_r, L0_rec_Wk_i, L0_rec_bk_i, L0_rec_Wv_r, L0_rec_bv_r, L0_rec_Wv_i, L0_rec_bv_i, L0_rec_Wo_r, L0_rec_bo_r, L0_rec_Wo_i, L0_rec_bo_i, L0_rec_int_Wr, L0_rec_int_Wi, L0_rec_meas_Mr, L0_rec_meas_Mi, L0_rec_post_W, L0_rec_post_b, L0_rec_post_g, L0_rec_post_be):
    import jax
    import jax.numpy as jnp

    def _L0_rec_ref(x, strength, er_W1, er_b1, er_g1, er_be1, er_W2, er_b2, ei_W1, ei_b1, ei_g1, ei_be1, ei_W2, ei_b2, Wq_r, bq_r, Wq_i, bq_i, Wk_r, bk_r, Wk_i, bk_i, Wv_r, bv_r, Wv_i, bv_i, Wo_r, bo_r, Wo_i, bo_i, int_Wr, int_Wi, meas_Mr, meas_Mi, post_W, post_b, post_g, post_be):
        import jax, jax.numpy as jnp
        import numpy as np
        B, IN, HID, D, N, OUT = (512, 256, 256, 512, 4, 512)
        H = 8
        HD = D // H

        def _ln(x, g, b):
            m = x.mean(-1, keepdims=True)
            v = ((x - m) ** 2).mean(-1, keepdims=True)
            return (x - m) / jnp.sqrt(v + 1e-05) * g + b
        Bsz = x.shape[0]

        def enc(W1, b1, g, be, W2, b2):
            h = jax.nn.gelu(_ln(x @ W1.T + b1, g, be), approximate=False)
            return (h @ W2.T + b2).reshape(Bsz, N, D)
        sr = enc(er_W1, er_b1, er_g1, er_be1, er_W2, er_b2)
        si = enc(ei_W1, ei_b1, ei_g1, ei_be1, ei_W2, ei_b2)

        def heads(t):
            return t.reshape(Bsz, N, H, HD).transpose(0, 2, 1, 3)
        qr = heads(sr @ Wq_r.T + bq_r)
        qi = heads(si @ Wq_i.T + bq_i)
        kr = heads(sr @ Wk_r.T + bk_r)
        ki = heads(si @ Wk_i.T + bk_i)
        vr = heads(sr @ Wv_r.T + bv_r)
        vi = heads(si @ Wv_i.T + bv_i)
        ar = jnp.einsum('bhnd,bhmd->bhnm', qr, kr) + jnp.einsum('bhnd,bhmd->bhnm', qi, ki)
        ai = jnp.einsum('bhnd,bhmd->bhnm', qi, kr) - jnp.einsum('bhnd,bhmd->bhnm', qr, ki)
        mag = jnp.sqrt(ar ** 2 + ai ** 2 + 1e-08) * HD ** (-0.5)
        w = jax.nn.softmax(mag, axis=-1)
        out_r = jnp.einsum('bhnm,bhmd->bhnd', w, vr).transpose(0, 2, 1, 3).reshape(Bsz, N, D)
        out_i = jnp.einsum('bhnm,bhmd->bhnd', w, vi).transpose(0, 2, 1, 3).reshape(Bsz, N, D)
        attn_r = out_r @ Wo_r.T + bo_r
        attn_i = out_i @ Wo_i.T + bo_i
        R = jnp.einsum('bnd,ned->bne', attn_r, int_Wr) - jnp.einsum('bnd,ned->bne', attn_i, int_Wi)
        I = jnp.einsum('bnd,ned->bne', attn_r, int_Wi) + jnp.einsum('bnd,ned->bne', attn_i, int_Wr)
        Ri, Ii = (R[:, :, None, :], I[:, :, None, :])
        Rj, Ij = (R[:, None, :, :], I[:, None, :, :])
        phase = jnp.arctan2(Ii * Rj - Ri * Ij, Ri * Rj + Ii * Ij)
        f = jnp.cos(phase) * strength[..., None]
        sup_r = jnp.einsum('bijd,bjd->bd', f, R)
        sup_i = jnp.einsum('bijd,bjd->bd', f, I)
        norm = jnp.sqrt(jnp.sum(sup_r ** 2 + sup_i ** 2, axis=-1, keepdims=True) + 1e-08)
        sup_r = sup_r / norm
        sup_i = sup_i / norm
        mr = sup_r @ meas_Mr.T - sup_i @ meas_Mi.T
        mi = sup_r @ meas_Mi.T + sup_i @ meas_Mr.T
        amp = jnp.sqrt(mr ** 2 + mi ** 2)
        out = jax.nn.gelu(_ln(amp @ post_W.T + post_b, post_g, post_be), approximate=False)
        return out
    y = _L0_rec_ref(r_x, r_strength, L0_rec_er_W1, L0_rec_er_b1, L0_rec_er_g1, L0_rec_er_be1, L0_rec_er_W2, L0_rec_er_b2, L0_rec_ei_W1, L0_rec_ei_b1, L0_rec_ei_g1, L0_rec_ei_be1, L0_rec_ei_W2, L0_rec_ei_b2, L0_rec_Wq_r, L0_rec_bq_r, L0_rec_Wq_i, L0_rec_bq_i, L0_rec_Wk_r, L0_rec_bk_r, L0_rec_Wk_i, L0_rec_bk_i, L0_rec_Wv_r, L0_rec_bv_r, L0_rec_Wv_i, L0_rec_bv_i, L0_rec_Wo_r, L0_rec_bo_r, L0_rec_Wo_i, L0_rec_bo_i, L0_rec_int_Wr, L0_rec_int_Wi, L0_rec_meas_Mr, L0_rec_meas_Mi, L0_rec_post_W, L0_rec_post_b, L0_rec_post_g, L0_rec_post_be)
    return y

_drawn_inputs = setup_inputs


def setup_inputs(seed=0):
    import zlib

    import numpy as np

    out = dict(_drawn_inputs(seed))
    spreads = {'L0_rec_er_b1': (0.0, 0.661),
     'L0_rec_er_g1': (1.0, 0.6),
     'L0_rec_er_be1': (0.0, 0.8),
     'L0_rec_er_b2': (0.0, 0.503),
     'L0_rec_ei_b1': (0.0, 0.656),
     'L0_rec_ei_g1': (1.0, 0.6),
     'L0_rec_ei_be1': (0.0, 0.8),
     'L0_rec_ei_b2': (0.0, 0.516),
     'L0_rec_bq_r': (0.0, 0.8),
     'L0_rec_bq_i': (0.0, 0.8),
     'L0_rec_bk_r': (0.0, 0.8),
     'L0_rec_bk_i': (0.0, 0.8),
     'L0_rec_bv_r': (0.0, 0.1),
     'L0_rec_bv_i': (0.0, 0.1),
     'L0_rec_bo_r': (0.0, 0.1),
     'L0_rec_bo_i': (0.0, 0.1),
     'L0_rec_int_Wi': (0.0, 0.1),
     'L0_rec_post_b': (0.0, 0.1),
     'L0_rec_post_g': (1.0, 0.2),
     'L0_rec_post_be': (0.0, 0.1)}
    factors = {'L0_rec_Wq_r': 8.0, 'L0_rec_Wq_i': 8.0, 'L0_rec_Wk_r': 8.0, 'L0_rec_Wk_i': 8.0}
    for name, (base, spread) in spreads.items():
        noise = np.random.default_rng([zlib.crc32(name.encode()), seed]).standard_normal(out[name].shape)
        drawn = base * np.exp(spread * noise) if base else spread * noise
        out[name] = jnp.asarray(drawn.astype(out[name].dtype))
    for name, factor in factors.items():
        out[name] = (out[name] * factor).astype(out[name].dtype)
    return out
```

```python
from contextlib import ExitStack

import concourse.bass as bass
from concourse import mybir

P = 128
BANK = 512
NB = 8

F32 = mybir.dt.float32
F32R = mybir.dt.float32r
ACT = mybir.ActivationFunctionType
ALU = mybir.AluOpType
AX_X = mybir.AxisListType.X

B, IN, HID, D, N, OUT, H = 1024, 256, 256, 512, 4, 512, 8
HD = D // H
TILES = B // P
KI = IN // P
KH = HID // P
KD = D // P
HC = P // HD
TQ = 256
NQ = B // TQ
G = TQ // 32
GH = G * HC
EPS_LN = 1e-5
EPS = 1e-8
RI = 2


class Ring:

    def __init__(self, readers):
        self.readers = readers
        self.per = {r: readers.count(r) for r in set(readers)}

    def nth(self, j):
        return self.readers[:j].count(self.readers[j])

    def bank(self, j):
        return j % NB

    def filled(self, j, it):
        return it * len(self.readers) + j + 1

    def before(self, j, it):
        if j >= NB:
            r = self.readers[j - NB]
            return r, it * self.per[r] + self.nth(j - NB) + 1 + self.per[r]
        last = max(k for k in range(len(self.readers)) if k % NB == j)
        r = self.readers[last]
        return r, it * self.per[r] + self.nth(last) + 1


def three(nc, out, lhs, rhs, first, last):
    (lh, ll), (rh, rl) = lhs, rhs
    nc.tensor.matmul(out, lh, rh, start=first, stop=False)
    nc.tensor.matmul(out, lh, rl, start=False, stop=False)
    return nc.tensor.matmul(out, ll, rh, start=False, stop=last)


def wait_apart(eng, sem, count):
    eng.wait_ge(sem, 1)
    eng.wait_ge(sem, count)


def f32(ap):
    return ap.bitcast(F32)


def stage_encode(nc, const, hT, w2, banks, x, w1, b1, g1, be1, W2, bias_rows, biasT):
    with ExitStack() as ctx:
        E = ctx.enter_context
        sb = lambda name, shape, dt=F32: E(nc.sbuf_tensor(name, shape, dt))
        sem = lambda name: E(nc.semaphore(name))
        x_rows = sb("x_rows", [P, TILES, IN])
        xT = [sb(f"xT_{s}", [P, KI, B], F32R) for s in ("hi", "lo")]
        w1_rows = sb("w1_rows", [P, RI, KH, IN])
        w1T = [sb(f"w1T_{s}", [P, KI, RI, HID], F32R) for s in ("hi", "lo")]
        h = sb("h_rows", [P, TILES, RI, HID])
        w2f = sb("w2_rows", [P, RI, N * KD, HID])
        b1b = sb("b1_bcast", [P, RI, HID])
        g1b = sb("g1_bcast", [P, RI, HID])
        be1b = sb("be1_bcast", [P, RI, HID])
        brows = sb("bias_rows", [P, P])
        stats = sb("ln_stats", [P, TILES * RI, 6])
        mv = sb("ln_mean_var", [P, TILES * RI, 2])
        std = sb("ln_std", [P, TILES * RI])
        rstd = sb("ln_rstd", [P, TILES * RI])
        eps = sb("eps_ln", [P, 1])

        s_x, s_w1, s_w2, s_brow, s_vec = (sem(n) for n in ("x_in", "w1_in", "w2_in", "bias_rows_in", "ln_vectors_in"))
        s_id0, s_id, s_mask = sem("identity_zeroed"), sem("identity_ready"), sem("mask_ready")
        filled = sem("a_filled")
        freed = {"act": sem("a_freed_act"), "dve": sem("a_freed_dve")}
        s_hi = sem("a_hi_ready")
        s_w2hi = sem("w2_hi_ready")
        s_std = sem("ln_std_ready")
        s_ln, s_h, s_eps, s_step = sem("ln_rows_ready"), sem("h_rows_ready"), sem("eps_ready"), sem("a_dve_step")

        XJ = [(k, q) for k in range(KI) for q in range(TILES // 4)]
        HJ = [(ri, k, q) for ri in range(RI) for k in range(KH) for q in range(TILES // 4)]
        n_x, n_w1, n_h = len(XJ), RI, TILES
        first_h = n_x + n_w1 + 1
        first_hT = first_h + n_h
        ring = Ring(["dve"] * (first_hT + len(HJ)))

        block = E(nc.Block())

        @block.sync
        def _(sp):
            sp.dma_start(x_rows[:], x.rearrange("(t p) f -> p t f", p=P)).then_inc(s_x, 16)
            for ri in range(RI):
                sp.dma_start(w1_rows[:, ri], w1[ri].rearrange("(k p) f -> p k f", p=P)).then_inc(s_w1, 16)
            row = 0
            for v in bias_rows:
                n = v.shape[0] // P
                sp.dma_start(brows[row:row + n, :], v.rearrange("(r p) -> r p", p=P)).then_inc(s_brow, 16)
                row += n
            for t, v in ((b1b, b1), (g1b, g1), (be1b, be1)):
                for ri in range(RI):
                    sp.dma_start(t[:, ri], v[ri].partition_broadcast(P)).then_inc(s_vec, 16)
            for ri in range(RI):
                sp.dma_start(w2f[:, ri], W2[ri].rearrange("(k p) f -> p k f", p=P)).then_inc(s_w2, 16)

        @block.gpsimd
        def _(pool):
            nc.gpsimd.memset(const.ident[:], 0.0).then_inc(s_id0, 1)
            pool.wait_ge(s_id0, 1)
            nc.gpsimd.affine_select(out=const.ident[:], in_=const.ident[:], compare_op=ALU.not_equal, fill=1.0,
                                    base=0, pattern=[[-1, P]], channel_multiplier=1).then_inc(s_id, 1)
            for ri in range(RI):
                pool.wait_ge(s_w2hi, ri + 1)
                nc.gpsimd.tensor_tensor(w2[1][:, ri], w2f[:, ri], f32(w2[0][:, ri]), ALU.subtract)

        @block.tensor
        def _(pe):
            def take(j):
                if j >= NB:
                    pe.wait_ge(freed["dve"], j - NB + 1)
                return banks[ring.bank(j)]

            pe.wait_ge(s_id, 1)
            pe.wait_ge(s_x, 16)
            for j, (k, q) in enumerate(XJ):
                ps = take(j)
                for t in range(4):
                    mm = nc.tensor.transpose(ps[:, t * P:(t + 1) * P], x_rows[:, 4 * q + t, k * P:(k + 1) * P],
                                             const.ident[:])
                mm.then_inc(filled, 1)
            pe.wait_ge(s_w1, 16 * RI)
            for ri in range(RI):
                ps = take(n_x + ri)
                for k in range(KI):
                    for m in range(KH):
                        mm = nc.tensor.transpose(ps[:, (k * KH + m) * P:(k * KH + m + 1) * P],
                                                 w1_rows[:, ri, m, k * P:(k + 1) * P], const.ident[:])
                mm.then_inc(filled, 1)
            pe.wait_ge(s_brow, 16 * len(bias_rows))
            ps = take(n_x + n_w1)
            nrow = biasT.shape[1]
            nc.tensor.transpose(ps[:, 0:nrow], brows[0:nrow, :], const.ident[0:nrow, 0:nrow]).then_inc(filled, 1)
            pe.wait_ge(freed["dve"], n_x + n_w1)
            for t in range(TILES):
                ps = take(first_h + t)
                for k in range(KI):
                    mm = three(nc, ps[:], [v[:, k, t * P:(t + 1) * P] for v in xT],
                               [v[:, k].rearrange("p r f -> p (r f)") for v in w1T], k == 0, k == KI - 1)
                mm.then_inc(filled, 1)
            pe.wait_ge(s_h, TILES)
            for j, (ri, k, q) in enumerate(HJ):
                ps = take(first_hT + j)
                for t in range(4):
                    mm = nc.tensor.transpose(ps[:, t * P:(t + 1) * P], h[:, 4 * q + t, ri, k * P:(k + 1) * P],
                                             const.ident[:])
                mm.then_inc(filled, 1)

        @block.scalar
        def _(act):
            for j, (k, q) in enumerate(XJ):
                act.wait_ge(filled, j + 1)
                nc.scalar.activation(xT[0][:, k, q * BANK:(q + 1) * BANK], banks[ring.bank(j)][:],
                                     ACT.Identity).then_inc(s_hi, 1)
            for ri in range(RI):
                act.wait_ge(filled, n_x + ri + 1)
                nc.scalar.activation(w1T[0][:, :, ri, :],
                                     banks[ring.bank(n_x + ri)][:].rearrange("p (k f) -> p k f", k=KI),
                                     ACT.Identity).then_inc(s_hi, 1)
            act.wait_ge(s_w2, 16 * RI)
            for ri in range(RI):
                nc.scalar.activation(w2[0][:, ri], w2f[:, ri], ACT.Identity).then_inc(s_w2hi, 1)
            act.wait_ge(s_eps, 1)
            act.wait_ge(s_ln, 1)
            nc.scalar.activation(std[:], mv[:, :, 1], ACT.Sqrt, bias=eps[:]).then_inc(s_std, 1)
            for t in range(TILES):
                act.wait_ge(s_ln, t + 2)
                nc.scalar.activation(h[:, t], h[:, t], ACT.Gelu).then_inc(s_h, 1)
            for j, (ri, k, q) in enumerate(HJ):
                jj = first_hT + j
                act.wait_ge(filled, jj + 1)
                nc.scalar.activation(hT[0][:, ri, k, q * BANK:(q + 1) * BANK], banks[ring.bank(jj)][:],
                                     ACT.Identity).then_inc(s_hi, 1)

        @block.vector
        def _(dve):
            steps = [0]

            def link(ins):
                steps[0] += 1
                ins.then_inc(s_step, 1)
                dve.wait_ge(s_step, steps[0])

            link(nc.vector.memset(eps[:], EPS_LN))
            nc.vector.memset(const.zero[:], 0.0)
            nc.vector.memset(const.eps[:], EPS).then_inc(s_eps, 1)
            for j, (k, q) in enumerate(XJ):
                dve.wait_ge(s_hi, j + 1)
                cols = slice(q * BANK, (q + 1) * BANK)
                nc.vector.tensor_tensor(xT[1][:, k, cols], banks[ring.bank(j)][:], f32(xT[0][:, k, cols]),
                                        ALU.subtract).then_inc(freed["dve"], 1)
            for ri in range(RI):
                dve.wait_ge(s_hi, n_x + ri + 1)
                nc.vector.tensor_tensor(w1T[1][:, :, ri, :],
                                        banks[ring.bank(n_x + ri)][:].rearrange("p (k f) -> p k f", k=KI),
                                        f32(w1T[0][:, :, ri, :]), ALU.subtract).then_inc(freed["dve"], 1)
            dve.wait_ge(filled, n_x + n_w1 + 1)
            nc.vector.tensor_copy(biasT[:], banks[ring.bank(n_x + n_w1)][:, 0:biasT.shape[1]]).then_inc(freed["dve"], 1)
            dve.wait_ge(s_id, 1)
            nc.vector.tensor_reduce(const.mask[:], const.ident[:].rearrange("p (n t) -> p t n", t=32), AX_X, ALU.add)
            dve.wait_ge(s_vec, 16 * 6)
            for t in range(TILES):
                dve.wait_ge(filled, first_h + t + 1)
                link(nc.vector.tensor_tensor(h[:, t].rearrange("p r f -> p (r f)"), banks[ring.bank(first_h + t)][:],
                                             b1b[:].rearrange("p r f -> p (r f)"), ALU.add))
                nc.vector.bn_stats(stats[:, RI * t, :], h[:, t, 0]).then_inc(freed["dve"], 1)
                link(nc.vector.bn_stats(stats[:, RI * t + 1, :], h[:, t, 1]))
                nc.vector.bn_aggr(mv[:, RI * t, :], stats[:, RI * t, :])
                ins = nc.vector.bn_aggr(mv[:, RI * t + 1, :], stats[:, RI * t + 1, :])
            ins.then_inc(s_ln, 1)
            dve.wait_ge(s_std, 1)
            link(nc.vector.reciprocal(rstd[:], std[:]))
            for t in range(TILES):
                for ri in range(RI):
                    i = RI * t + ri
                    ins = nc.vector.tensor_scalar(h[:, t, ri], h[:, t, ri], mv[:, i, 0:1], rstd[:, i:i + 1],
                                                  ALU.subtract, ALU.mult)
                link(ins)
                link(nc.vector.tensor_tensor(h[:, t], h[:, t], g1b[:], ALU.mult))
                nc.vector.tensor_tensor(h[:, t], h[:, t], be1b[:], ALU.add).then_inc(s_ln, 1)
            for j, (ri, k, q) in enumerate(HJ):
                jj = first_hT + j
                dve.wait_ge(s_hi, n_x + n_w1 + j + 1)
                cols = slice(q * BANK, (q + 1) * BANK)
                nc.vector.tensor_tensor(hT[1][:, ri, k, cols], banks[ring.bank(jj)][:], f32(hT[0][:, ri, k, cols]),
                                        ALU.subtract).then_inc(freed["dve"], 1)


NP = 3
FOLD = NP * P


def stage_fold(nc, const, w2, banks, proj, biasT, bias_cols, c_dram):
    with ExitStack() as ctx:
        E = ctx.enter_context
        sb = lambda name, shape, dt=F32: E(nc.sbuf_tensor(name, shape, dt))
        sem = lambda name: E(nc.semaphore(name))
        rows = sb("proj_rows", [P, RI * NP, D])
        wT = [sb(f"projT_{s}", [P, RI, KD, FOLD], F32R) for s in ("hi", "lo")]
        b2T = [sb(f"b2T_{s}", [P, RI * N * KD], F32R) for s in ("hi", "lo")]
        stage = sb("fold_out", [P, RI, N * KH, FOLD])

        s_rows = sem("proj_rows_in")
        s_stored = [sem(f"folded_stored_{ri}") for ri in range(RI)]
        filled = sem("f_filled")
        freed = {"act": sem("f_freed_act"), "dve": sem("f_freed_dve")}
        s_hi, s_b2, s_b2hi = sem("f_hi_ready"), sem("b2_split"), sem("b2_hi_ready")

        n_t = RI * NP
        FJ = [(ri, n, kh) for ri in range(RI) for n in range(N) for kh in range(KH)]
        ring = Ring(["dve"] * (n_t + 1) + ["act"] * len(FJ))
        n_j = len(ring.readers)
        per = ring.per

        def load(sp, c):
            for i in range(n_t):
                sp.dma_start(rows[:, i, :], proj[i // NP][i % NP][bass.ds(c * P, P), :]).then_inc(s_rows, 16)

        block = E(nc.Block())

        @block.sync
        def _(sp):
            def store(c):
                half = N * KH
                for ri in range(RI):
                    wait_apart(sp, freed["act"], (c + 1) * per["act"] + (ri + 1) * half)
                    sp.dma_start(c_dram[bass.ds(c, 1), :, ri].rearrange("a p k f -> (a p) k f"),
                                 stage[:, ri]).then_inc(s_stored[ri], 16)

            load(sp, 0)
            with sp.Fori(0, KD - 1) as c:
                wait_apart(sp, filled, ring.filled(n_t - 1, c))
                load(sp, c + 1)
                store(c)
            store(KD - 1)
            for ri in range(RI):
                sp.wait_ge(s_stored[ri], 16 * (KD + 1))

        @block.tensor
        def _(pe):
            with pe.Fori(0, KD) as c:
                def take(j):
                    r, v = ring.before(j, c)
                    pe.wait_ge(freed[r], v)
                    return banks[ring.bank(j)]

                pe.wait_ge(s_rows, (c + 1) * 16 * n_t)
                for i in range(n_t):
                    ps = take(i)
                    for k in range(KD):
                        mm = nc.tensor.transpose(ps[:, k * P:(k + 1) * P], rows[:, i, k * P:(k + 1) * P],
                                                 const.ident[:])
                    mm.then_inc(filled, 1)
                ps = take(n_t)
                pe.wait_ge(s_b2, 1)
                pe.wait_ge(freed["dve"], c * per["dve"] + per["dve"] + n_t)
                for i in range(n_t):
                    ri, pr = i // NP, i % NP
                    for k in range(KD):
                        cols = slice(ri * N * KD + k, (ri + 1) * N * KD, KD)
                        mm = three(nc, ps[:, i * N:(i + 1) * N],
                                   [w[:, ri, k, pr * P:(pr + 1) * P] for w in wT], [b[:, cols] for b in b2T],
                                   k == 0, k == KD - 1)
                mm.then_inc(filled, 1)
                for j, (ri, n, kh) in enumerate(FJ):
                    ps = take(n_t + 1 + j)
                    for k in range(KD):
                        mm = three(nc, ps[:, 0:FOLD],
                                   [w[:, ri, n * KD + k, kh * P:(kh + 1) * P] for w in w2],
                                   [w[:, ri, k] for w in wT], k == 0, k == KD - 1)
                    mm.then_inc(filled, 1)

        def out_slot(j):
            ri, n, kh = FJ[j]
            return ri, stage[:, ri, n * KH + kh, :]

        @block.scalar
        def _(act):
            nc.scalar.activation(b2T[0][:], biasT[:, 0:RI * N * KD], ACT.Identity).then_inc(s_b2hi, 1)
            nc.scalar.activation(const.scratch[:, 0:1], const.eps[:], ACT.Identity).then_inc(freed["act"], per["act"])
            with act.Fori(0, KD) as c:
                for i in range(n_t):
                    ri, pr = i // NP, i % NP
                    act.wait_ge(filled, ring.filled(i, c))
                    if i == 0:
                        act.wait_ge(freed["dve"], (c + 1) * per["dve"])
                    nc.scalar.activation(wT[0][:, ri, :, pr * P:(pr + 1) * P],
                                         banks[ring.bank(i)][:].rearrange("p (k f) -> p k f", k=KD),
                                         ACT.Identity).then_inc(s_hi, 1)
                for j, (ri, n, kh) in enumerate(FJ):
                    jj = n_t + 1 + j
                    if n == 0 and kh == 0:
                        act.wait_ge(s_stored[ri], (c + 1) * 16)
                    act.wait_ge(filled, ring.filled(jj, c))
                    nc.scalar.activation(stage[:, ri, n * KH + kh, :], banks[ring.bank(jj)][:, 0:FOLD],
                                         ACT.Identity).then_inc(freed["act"], 1)

        @block.vector
        def _(dve):
            dve.wait_ge(s_b2hi, 1)
            nc.vector.tensor_tensor(b2T[1][:], biasT[:, 0:RI * N * KD], f32(b2T[0][:]), ALU.subtract).then_inc(s_b2, 1)
            nc.vector.memset(const.scratch[:, 1:2], 0.0).then_inc(freed["dve"], per["dve"])
            for ri in range(RI):
                nc.vector.memset(const.scratch[:, 2 + ri:3 + ri], 0.0).then_inc(s_stored[ri], 16)
            with dve.Fori(0, KD) as c:
                for i in range(n_t):
                    ri, pr = i // NP, i % NP
                    dve.wait_ge(s_hi, c * n_t + i + 1)
                    cols = slice(pr * P, (pr + 1) * P)
                    nc.vector.tensor_tensor(wT[1][:, ri, :, cols], banks[ring.bank(i)][:].rearrange("p (k f) -> p k f", k=KD),
                                            f32(wT[0][:, ri, :, cols]), ALU.subtract).then_inc(freed["dve"], 1)
                dve.wait_ge(filled, ring.filled(n_t, c))
                own = biasT[:, RI * N * KD:RI * N * KD + n_t * KD].rearrange("p (i c) -> p i c", c=KD)[:, :, bass.ds(c, 1)]
                nc.vector.tensor_tensor(bias_cols[:, bass.ds(c, 1)].rearrange("p a i n -> p (a i) n"),
                                        banks[ring.bank(n_t)][:, 0:n_t * N].rearrange("p (i n) -> p i n", n=N),
                                        own.to_broadcast([P, n_t, N]), ALU.add).then_inc(freed["dve"], 1)


def stage_attend(nc, const, hT, banks, bias_cols, c_dram, o_dram):
    with ExitStack() as ctx:
        E = ctx.enter_context
        sb = lambda name, shape, dt=F32: E(nc.sbuf_tensor(name, shape, dt))
        pair = lambda name, shape: [sb(f"{name}_{s}", shape, F32R) for s in ("hi", "lo")]
        sem = lambda name: E(nc.semaphore(name))
        SLOTS = 4
        KI_, KR_, NKI_ = 0, 1, 2
        fold_in = sb("fold_in", [P, SLOTS, KH * FOLD])
        fold = pair("fold", [P, RI, N, KH * FOLD])
        bias = sb("bias_chunk", [P, RI, NP, N])
        k_ = pair("k", [P, G, 3, P])
        q_ = pair("q", [P, RI, G, P])
        vT = sb("vT", [P, RI, G, P])
        v_ = pair("v", [P, G, HC, RI, HD])
        sq = sb("squares", [P, 2, GH // 2, 2, P])
        mag2 = sb("masked_mag2", [P, GH // 2, P])
        magc = sb("mag2", [P, GH, N])
        root = sb("magnitude", [P, GH, N])
        top = sb("row_max", [P, GH])
        dif = sb("minus_max", [P, GH, N])
        ex = sb("exps", [P, GH, N])
        den = sb("exp_sum", [P, GH])
        rden = sb("exp_sum_inverse", [P, GH])
        w = sb("weights", [P, GH, N])
        wt = sb("weights_turned", [P, GH, N])
        wt_ = pair("weights_split", [P, GH, N])
        wT = pair("wT", [P, GH, P])
        oT = sb("oT", [P, HC, N, TQ])

        s_in = [sem(f"fold_in_{i}") for i in range(SLOTS)]
        s_fhi, s_flo, s_bias = sem("fold_hi_ready"), sem("fold_lo_ready"), sem("bias_ready")
        filled = sem("b_filled")
        freed = {"act": sem("b_freed_act"), "dve": sem("b_freed_dve")}
        s_hi, s_nki, s_sq = sem("b_hi_ready"), sem("minus_ki_ready"), sem("squares_ready")
        s_sum, s_msk = sem("mag2_summed"), sem("mag2_masked")
        s_mag, s_root, s_top, s_dif = sem("mag2_ready"), sem("magnitude_ready"), sem("max_ready"), sem("minus_max_ready")
        s_ex, s_den, s_rden, s_w, s_wt = (sem(n) for n in ("exps_ready", "exp_sum_ready", "inverse_ready", "weights_ready", "weights_turned_ready"))
        s_wthi, s_wtlo, s_wThi, s_wTlo = (sem(n) for n in ("weights_hi_ready", "weights_lo_ready", "wT_hi_ready", "wT_lo_ready"))
        s_out = sem("oT_stored")

        STEPS = KD * NQ
        VJ = [(ri, n) for ri in range(RI) for n in range(N)]
        KJ = [(ri, n) for ri in (1, 0) for n in range(N)]
        QJ = VJ
        OJ = [(h, gq) for h in range(HC) for gq in range(G // 4)]
        TJ = range(G // 2)
        SJ = range(GH // 2)
        kinds = (["act"] * len(VJ) + ["dve"] * len(KJ) + ["dve"] * len(QJ) + ["dve"] * len(OJ)
                 + ["dve"] * len(TJ) + ["act"] * len(SJ))
        ring = Ring(kinds)
        per, n_j = ring.per, len(kinds)
        j_k = len(VJ)
        j_q = j_k + len(KJ)
        j_o = j_q + len(QJ)
        j_t = j_o + len(OJ)
        j_s = j_t + len(TJ)
        n_hi = len(KJ) + len(QJ) + len(TJ)
        HB = GH // 4
        done = lambda j, it, r: (it + 1) * per[r] + ring.nth(j) + 1

        block = E(nc.Block())

        @block.sync
        def _(sp):
            def store(it):
                wait_apart(sp, freed["dve"], done(j_t - 1, it, "dve"))
                sp.dma_start(o_dram[bass.ds(it, 1)].rearrange("a p h n t -> (a p) (h n t)"),
                             oT[:].rearrange("p h n t -> p (h n t)")).then_inc(s_out, 16)

            with sp.Fori(0, KD) as c:
                for i, (ri, n) in enumerate(VJ):
                    wait_apart(sp, s_flo, (c + 1) * len(VJ) + i + 1 - SLOTS)
                    sp.dma_start(fold_in[:, i % SLOTS], c_dram[bass.ds(c, 1), :, ri, KH * n:KH * n + KH, :]
                                 .rearrange("a p k f -> (a p) (k f)")).then_inc(s_in[i % SLOTS], 16)
                with sp.Fori(0, NQ) as q:
                    store(c * NQ + q)
            sp.wait_ge(freed["dve"], (STEPS + 1) * per["dve"] + len(OJ))
            sp.dma_start(o_dram[STEPS].rearrange("p h n t -> p (h n t)"),
                         oT[:].rearrange("p h n t -> p (h n t)")).then_inc(s_out, 16)
            sp.wait_ge(s_out, 16 * (STEPS + 2))

        @block.gpsimd
        def _(pool):
            def expand(it):
                pool.wait_ge(s_wtlo, it + 1)
                nc.gpsimd.tensor_tensor(wT[1][:].rearrange("p a (n t) -> p (a n) t", t=32),
                                        f32(wt_[1][:]).rearrange("p a n -> p (a n)").unsqueeze(2).to_broadcast([P, GH * N, 32]),
                                        const.mask[:].unsqueeze(1).to_broadcast([P, GH * N, 32]),
                                        ALU.mult).then_inc(s_wTlo, 1)

            with pool.Fori(0, KD) as c:
                with pool.Fori(0, NQ) as q:
                    it = c * NQ + q
                    expand(it)
                    pool.wait_ge(freed["dve"], done(j_k + N - 1, it, "dve"))
                    for s in range(2):
                        nc.gpsimd.tensor_tensor(k_[s][:, :, NKI_, :], const.zero[:].unsqueeze(2).to_broadcast([P, G, P]),
                                                f32(k_[s][:, :, KI_, :]), ALU.subtract).then_inc(s_nki, 1)
            expand(STEPS)

        @block.tensor
        def _(pe):
            def weighted_sum(it, j0, take):
                pe.wait_ge(s_wThi, it + 1)
                pe.wait_ge(s_wTlo, it + 1)
                for j, (h, gq) in enumerate(OJ):
                    ps = take(j0 + j)
                    for g4 in range(4):
                        g = 4 * gq + g4
                        lhs = [v[:, g, h].rearrange("p r d -> p (r d)") for v in v_]
                        rhs = [x[:, h * G + g, :] for x in wT]
                        mm = three(nc, ps[:, g4 * P:(g4 + 1) * P], lhs, rhs, True, True)
                    mm.then_inc(filled, 1)

            with pe.Fori(0, KD) as c:
                with pe.Fori(0, NQ) as q:
                    it = c * NQ + q
                    toks = bass.ds(q * TQ, TQ)

                    def take(j):
                        r, v = ring.before(j, it)
                        pe.wait_ge(freed[r], v)
                        return banks[ring.bank(j)]

                    for j0, pr, jobs in ((0, 2, VJ), (j_k, 1, KJ), (j_q, 0, QJ)):
                        for j, (ri, n) in enumerate(jobs):
                            if pr == 2:
                                pe.wait_ge(s_flo, (c + 1) * len(VJ) + j + 1)
                            ps = take(j0 + j)
                            for kh in range(KH):
                                f0 = kh * FOLD + pr * P
                                mm = three(nc, ps[:, 0:TQ], [f[:, ri, n, f0:f0 + P] for f in fold],
                                           [x[:, ri, kh, toks] for x in hT], kh == 0, kh == KH - 1)
                            mm.then_inc(filled, 1)
                    weighted_sum(it, j_o, take)
                    pe.wait_ge(freed["act"], done(j_k - 1, it, "act"))
                    for j in TJ:
                        ps = take(j_t + j)
                        for g2 in range(2):
                            for ri in range(RI):
                                o = (ri * 2 + g2) * P
                                mm = nc.tensor.transpose(ps[:, o:o + P], vT[:, ri, 2 * j + g2, :], const.ident[:])
                        mm.then_inc(filled, 1)
                    pe.wait_ge(freed["dve"], done(j_o - 1, it, "dve"))
                    pe.wait_ge(s_nki, 2 * it + 2)
                    for j in SJ:
                        ps = take(j_s + j)
                        for x in range(2):
                            gh = 2 * j + x
                            h, g = gh // G, gh % G
                            rows = slice(h * HD, (h + 1) * HD)
                            out = ps[:, x * 2 * P:(x + 1) * 2 * P]
                            for ri, ks in ((0, slice(KR_, NKI_ + 1)), (1, slice(KI_, KR_ + 1))):
                                mm = three(nc, out, [t[rows, ri, g, :] for t in q_],
                                           [t[rows, g, ks, :].rearrange("p s f -> p (s f)") for t in k_],
                                           ri == 0, ri == 1)
                        mm.then_inc(filled, 1)
            pe.wait_ge(freed["act"], (STEPS + 1) * per["act"])
            weighted_sum(STEPS, 0, lambda j: banks[j])

        @block.scalar
        def _(act):
            nc.scalar.activation(const.scratch[:, 0:1], const.eps[:], ACT.Identity).then_inc(freed["act"], per["act"])

            def magnitudes(it):
                act.wait_ge(s_mag, 2 * it + 2)
                nc.scalar.activation(root[:], magc[:], ACT.Sqrt, bias=const.eps[:]).then_inc(s_root, 1)

            def exponentials(it):
                act.wait_ge(s_dif, it + 1)
                nc.scalar.activation(ex[:], dif[:], ACT.Exp, scale=float(HD) ** -0.5).then_inc(s_ex, 1)

            with act.Fori(0, KD) as c:
                for i, (ri, n) in enumerate(VJ):
                    act.wait_ge(s_in[i % SLOTS], (c * (len(VJ) // SLOTS) + i // SLOTS + 1) * 16)
                    nc.scalar.activation(fold[0][:, ri, n], fold_in[:, i % SLOTS], ACT.Identity).then_inc(s_fhi, 1)
                act.wait_ge(s_bias, c + 1)
                with act.Fori(0, NQ) as q:
                    it = c * NQ + q
                    for j, (ri, n) in enumerate(VJ):
                        if j == 2:
                            magnitudes(it)
                        if j == 4:
                            exponentials(it)
                        act.wait_ge(filled, ring.filled(j, it))
                        nc.scalar.activation(vT[:, ri, :, n * 32:(n + 1) * 32],
                                             banks[ring.bank(j)][:, 0:TQ].rearrange("p (g t) -> p g t", t=32),
                                             ACT.Identity, bias=bias[:, ri, 2, n:n + 1]).then_inc(freed["act"], 1)
                    for j0, pr, jobs in ((j_k, 1, KJ), (j_q, 0, QJ)):
                        for j, (ri, n) in enumerate(jobs):
                            act.wait_ge(filled, ring.filled(j0 + j, it))
                            dst = k_[0][:, :, 1 - ri, :] if pr == 1 else q_[0][:, ri]
                            nc.scalar.activation(dst[:, :, n * 32:(n + 1) * 32],
                                                 banks[ring.bank(j0 + j)][:, 0:TQ].rearrange("p (g t) -> p g t", t=32),
                                                 ACT.Identity, bias=bias[:, ri, pr, n:n + 1]).then_inc(s_hi, 1)
                    for j in TJ:
                        act.wait_ge(filled, ring.filled(j_t + j, it))
                        nc.scalar.activation(v_[0][:, 2 * j:2 * j + 2].rearrange("p g h r d -> p r (g h) d"),
                                             banks[ring.bank(j_t + j)][:].rearrange("p (r a d) -> p r a d", r=RI, d=HD),
                                             ACT.Identity).then_inc(s_hi, 1)
                    for j in SJ:
                        act.wait_ge(filled, ring.filled(j_s + j, it))
                        nc.scalar.activation(sq[:, j // HB, 2 * (j % HB):2 * (j % HB) + 2].rearrange("p a r f -> p (a r f)"),
                                             banks[ring.bank(j_s + j)][:], ACT.Square).then_inc(freed["act"], 1)
            magnitudes(STEPS)
            exponentials(STEPS)

        @block.vector
        def _(dve):
            nc.vector.memset(const.scratch[:, 1:2], 0.0).then_inc(freed["dve"], per["dve"])
            nc.vector.memset(const.scratch[:, 2:3], 0.0).then_inc(s_flo, len(VJ))
            nc.vector.memset(const.scratch[:, 3:4], 0.0).then_inc(s_out, 16)
            nc.vector.memset(f32(v_[0][:]), 0.0)
            nc.vector.memset(f32(v_[1][:]), 0.0)
            nc.vector.memset(magc[:], 0.0).then_inc(s_mag, 2)

            def softmax_a(it):
                dve.wait_ge(s_root, it + 1)
                nc.vector.tensor_reduce(top[:], root[:], AX_X, ALU.max).then_inc(s_top, 1)
                dve.wait_ge(s_top, it + 1)
                nc.vector.tensor_tensor(dif[:], root[:], top[:].unsqueeze(2).to_broadcast([P, GH, N]),
                                        ALU.subtract).then_inc(s_dif, 1)

            def softmax_b(it):
                dve.wait_ge(s_ex, it + 1)
                nc.vector.tensor_reduce(den[:], ex[:], AX_X, ALU.add).then_inc(s_den, 1)
                dve.wait_ge(s_den, it + 1)
                nc.vector.reciprocal(rden[:], den[:]).then_inc(s_rden, 1)
                dve.wait_ge(s_rden, it + 1)
                nc.vector.tensor_tensor(w[:], ex[:], rden[:].unsqueeze(2).to_broadcast([P, GH, N]),
                                        ALU.mult).then_inc(s_w, 1)
                dve.wait_ge(s_w, it + 1)
                for n in range(N):
                    for m in range(N):
                        ins = nc.vector.tensor_copy(wt[m * 32:(m + 1) * 32, :, n], w[n * 32:(n + 1) * 32, :, m])
                        ins.then_inc(s_wt, 1)
                dve.wait_ge(s_wt, N * N * (it + 1))
                nc.vector.tensor_copy(wt_[0][:], wt[:]).then_inc(s_wthi, 1)
                dve.wait_ge(s_wthi, it + 1)
                nc.vector.tensor_tensor(wt_[1][:], wt[:], f32(wt_[0][:]), ALU.subtract).then_inc(s_wtlo, 1)
                nc.vector.tensor_tensor(wT[0][:].rearrange("p a (n t) -> p (a n) t", t=32),
                                        f32(wt_[0][:]).rearrange("p a n -> p (a n)").unsqueeze(2).to_broadcast([P, GH * N, 32]),
                                        const.mask[:].unsqueeze(1).to_broadcast([P, GH * N, 32]),
                                        ALU.mult).then_inc(s_wThi, 1)

            def outputs(j0, fill):
                for j, (h, gq) in enumerate(OJ):
                    dve.wait_ge(filled, fill + j + 1)
                    nc.vector.tensor_copy(oT[:, h, :, gq * BANK // N:(gq + 1) * BANK // N].rearrange("p n (g t) -> p g n t", t=32),
                                          banks[(j0 + j) % NB][:].rearrange("p (g n t) -> p g n t", n=N, t=32)
                                          ).then_inc(freed["dve"], 1)

            with dve.Fori(0, KD) as c:
                nc.vector.tensor_copy(bias[:].rearrange("p r a n -> p (r a) n"),
                                      bias_cols[:, bass.ds(c, 1)].rearrange("p a i n -> p (a i) n")).then_inc(s_bias, 1)
                for i, (ri, n) in enumerate(VJ):
                    dve.wait_ge(s_fhi, c * len(VJ) + i + 1)
                    nc.vector.tensor_tensor(fold[1][:, ri, n], fold_in[:, i % SLOTS], f32(fold[0][:, ri, n]),
                                            ALU.subtract).then_inc(s_flo, 1)
                with dve.Fori(0, NQ) as q:
                    it = c * NQ + q
                    softmax_a(it)
                    softmax_b(it)
                    for i, (j0, pr, jobs) in enumerate(((j_k, 1, KJ), (j_q, 0, QJ))):
                        for j, (ri, n) in enumerate(jobs):
                            dve.wait_ge(s_hi, it * n_hi + i * len(KJ) + j + 1)
                            cols = slice(n * 32, (n + 1) * 32)
                            hi, lo = [k_[s][:, :, 1 - ri, cols] if pr == 1 else q_[s][:, ri, :, cols] for s in range(2)]
                            nc.vector.scalar_tensor_tensor(out=lo, in0=banks[ring.bank(j0 + j)][:, 0:TQ].rearrange("p (g t) -> p g t", t=32),
                                                           scalar=bias[:, ri, pr, n:n + 1], in1=f32(hi),
                                                           op0=ALU.add, op1=ALU.subtract).then_inc(freed["dve"], 1)
                    dve.wait_ge(s_out, (it + 1) * 16)
                    outputs(j_o, it * n_j + j_o)
                    for j in TJ:
                        dve.wait_ge(s_hi, it * n_hi + len(KJ) + len(QJ) + j + 1)
                        hi, lo = [v_[s][:, 2 * j:2 * j + 2].rearrange("p g h r d -> p r (g h) d") for s in range(2)]
                        nc.vector.tensor_tensor(lo, banks[ring.bank(j_t + j)][:].rearrange("p (r a d) -> p r a d", r=RI, d=HD),
                                                f32(hi), ALU.subtract).then_inc(freed["dve"], 1)
                    for b in range(2):
                        dve.wait_ge(freed["act"], done(j_s + (b + 1) * HB - 1, it, "act"))
                        dve.wait_ge(s_mag, 2 * it + b + 2)
                        nc.vector.tensor_tensor(mag2[:], sq[:, b, :, 0, :], sq[:, b, :, 1, :], ALU.add).then_inc(s_sum, 1)
                        dve.wait_ge(s_sum, 2 * it + b + 1)
                        m2 = mag2[:].rearrange("p a (n t) -> p (a n) t", t=32)
                        nc.vector.tensor_tensor(m2, m2, const.mask[:].unsqueeze(1).to_broadcast([P, GH * N // 2, 32]),
                                                ALU.mult).then_inc(s_msk, 1)
                        dve.wait_ge(s_msk, 2 * it + b + 1)
                        nc.vector.tensor_reduce(magc[:, b * GH // 2:(b + 1) * GH // 2].rearrange("p a n -> p (a n)"),
                                                m2, AX_X, ALU.add).then_inc(s_mag, 1)
            softmax_a(STEPS)
            softmax_b(STEPS)
            dve.wait_ge(s_out, (STEPS + 1) * 16)
            outputs(0, STEPS * n_j)


def at_least(eng, sem, count):
    if not isinstance(count, int) or count > 0:
        eng.wait_ge(sem, count)


def stage_interact(nc, const, banks, wo, int_r, int_i, bo_cols, o_dram, z_dram):
    with ExitStack() as ctx:
        E = ctx.enter_context
        sb = lambda name, shape, dt=F32: E(nc.sbuf_tensor(name, shape, dt))
        pair = lambda name, shape: [sb(f"{name}_{s}", shape, F32R) for s in ("hi", "lo")]
        sem = lambda name: E(nc.semaphore(name))
        TT = TQ // P
        rows = sb("int_rows", [P, 3, KD, D])
        woT = pair("woT", [P, RI, KD, D])
        wT = pair("intT", [P, 3, KD, D])
        o_in = sb("out_in", [P, RI, KD, TQ])
        o_ = pair("out", [P, RI, KD, TQ])
        a_f = sb("attn_f", [P, 2, 3, KD, TQ])
        a_ = pair("attn", [P, 3, KD, TQ])
        k1 = sb("k1", [P, TT, D])
        z = sb("z_out", [P, TT, RI, D])

        s_wo, s_int, s_oin = sem("wo_in"), sem("int_in"), sem("out_in_ready")
        s_sums = sem("int_sums_ready")
        s_tf, s_thi, s_tlo = sem("turn_filled"), sem("turn_hi"), sem("turn_lo")
        s_af, s_ahi0, s_as = sem("attn_filled"), sem("attn_evacuated"), sem("attn_sum_ready")
        s_ahi, s_alo = sem("attn_hi"), sem("attn_lo")
        s_ohi, s_olo = sem("out_hi"), sem("out_lo")
        s_zf, s_k1, s_z, s_st = sem("z_filled"), sem("k1_ready"), sem("z_ready"), sem("z_stored")

        STEPS = N * NQ
        WJ = [(ri, m) for ri in range(RI) for m in range(KD)]
        TJ = [(w, m) for w in range(3) for m in range(KD)]
        AJ = [(ri, m) for ri in range(RI) for m in range(KD)]
        ZB = 2
        n_t, n_a, n_z = len(TJ), len(AJ), 3 * TT
        SRC = (0, 1, 2)
        o_view = o_dram[1:].rearrange("(c q) p h n t -> q c p h n t", q=NQ)
        z_view = z_dram.rearrange("n (q k p) r d -> n q p k (r d)", p=P, k=TT)

        def turned(n):
            return len(WJ) + (n + 1) * n_t

        block = E(nc.Block())

        @block.sync
        def _(sp):
            def load_out(n, q):
                for ri in range(RI):
                    for hh in range(HC):
                        src = o_view[q, :, ri * HD:(ri + 1) * HD, hh, bass.ds(n, 1), :].rearrange("c p a t -> p (a c) t")
                        sp.dma_start(o_in[hh * HD:(hh + 1) * HD, ri], src).then_inc(s_oin, 16)

            def store(n, q):
                wait_apart(sp, s_z, RI * TT * (n * NQ + q + 1))
                sp.dma_start(z_view[bass.ds(n, 1), q].rearrange("a p k f -> (a p) k f"),
                             z[:].rearrange("p k r d -> p k (r d)")).then_inc(s_st, 16)

            def state(n, first, last):
                for q in range(NQ):
                    if not (last and q == NQ - 1):
                        wait_apart(sp, s_olo, n * NQ + q + 1)
                        load_out(n + (q + 1) // NQ, (q + 1) % NQ)
                    if not (first and q == 0):
                        store(n - (q == 0), (q - 1) % NQ)

            for ri in range(RI):
                sp.dma_start(rows[:, ri], wo[ri].rearrange("(m p) d -> p m d", p=P)).then_inc(s_wo, 16)
            load_out(0, 0)
            state(0, True, False)
            with sp.Fori(1, N - 1) as n:
                state(n, False, False)
            state(N - 1, False, True)
            store(N - 1, NQ - 1)
            sp.wait_ge(s_st, 16 * STEPS)

        @block.gpsimd
        def _(pool):
            def state(n):
                pool.wait_ge(s_tf, len(WJ) + n * n_t)
                for i, src in enumerate((int_r, int_i)):
                    pool.dma_start(rows[:, i], src[bass.ds(n, 1)].rearrange("a (m p) d -> p (a m) d", p=P)).then_inc(s_int, 16)
                pool.wait_ge(s_int, 32 * (n + 1))
                nc.gpsimd.tensor_tensor(rows[:, 2], rows[:, 0], rows[:, 1], ALU.add).then_inc(s_sums, 1)
                pool.wait_ge(s_sums, 2 * n + 1)
                nc.gpsimd.tensor_tensor(rows[:, 1], rows[:, 1], rows[:, 0], ALU.subtract).then_inc(s_sums, 1)

            state(0)
            with pool.Fori(1, N) as n:
                state(n)

        @block.tensor
        def _(pe):
            def turns(jobs, j0):
                for j, (w, m) in enumerate(jobs):
                    ps = banks[ZB + j % 6]
                    at_least(pe, s_tlo, j0 + j - 5)
                    for k in range(KD):
                        mm = nc.tensor.transpose(ps[:, k * P:(k + 1) * P], rows[:, w, m, k * P:(k + 1) * P],
                                                 const.ident[:])
                    mm.then_inc(s_tf, 1)

            def attn(n, q):
                s = n * NQ + q
                pe.wait_ge(s_olo, s + 1)
                for j, (ri, m) in enumerate(AJ):
                    ps = banks[j % ZB]
                    at_least(pe, s_ahi0, s * n_a + j - ZB + 1)
                    for k in range(KD):
                        mm = three(nc, ps[:, 0:TQ], [w[:, ri, k, m * P:(m + 1) * P] for w in woT],
                                   [o[:, ri, k] for o in o_], k == 0, k == KD - 1)
                    mm.then_inc(s_af, 1)

            def product(n, s):
                pe.wait_ge(s_alo, s + 1)
                pe.wait_ge(s_tlo, turned(n))
                at_least(pe, s_z, RI * TT * s)
                for t in range(TT):
                    for i in range(3):
                        ps = banks[ZB + 3 * t + i]
                        for k in range(KD):
                            mm = three(nc, ps[:], [a[:, i, k, t * P:(t + 1) * P] for a in a_],
                                       [w[:, i, k] for w in wT], k == 0, k == KD - 1)
                        mm.then_inc(s_zf, 1)

            def turn_state(n):
                pe.wait_ge(s_sums, 2 * n + 2)
                at_least(pe, s_z, RI * TT * NQ * n)
                turns(TJ, len(WJ) + n * n_t)

            pe.wait_ge(s_wo, 16 * RI)
            turns(WJ, 0)
            def state(n, first=False):
                for q in range(NQ):
                    attn(n, q)
                    if q:
                        product(n, n * NQ + q - 1)
                    elif not first:
                        product(n - 1, n * NQ - 1)
                    if q == 0:
                        turn_state(n)

            state(0, True)
            with pe.Fori(1, N - 1) as n:
                state(n)
            state(N - 1)
            product(N - 1, STEPS - 1)

        @block.scalar
        def _(act):
            def turns(jobs, j0, dst):
                for j, (w, m) in enumerate(jobs):
                    act.wait_ge(s_tf, j0 + j + 1)
                    nc.scalar.activation(dst[0][:, w, :, m * P:(m + 1) * P],
                                         banks[ZB + j % 6][:].rearrange("p (k f) -> p k f", k=KD),
                                         ACT.Identity).then_inc(s_thi, 1)

            def split_out(s):
                act.wait_ge(s_oin, 16 * RI * HC * (s + 1))
                nc.scalar.activation(o_[0][:], o_in[:], ACT.Identity).then_inc(s_ohi, 1)

            def attn(s, par):
                for j, (ri, m) in enumerate(AJ):
                    act.wait_ge(s_af, s * n_a + j + 1)
                    if j == 0:
                        at_least(act, s_alo, s - 1)
                    nc.scalar.activation(a_f[:, par, 1 + ri, m], banks[j % ZB][:, 0:TQ], ACT.Identity,
                                         bias=bo_cols[:, ri, m:m + 1]).then_inc(s_ahi0, 1)

            def split_attn(s, par):
                act.wait_ge(s_as, s + 1)
                at_least(act, s_zf, n_z * s)
                nc.scalar.activation(a_[0][:], a_f[:, par], ACT.Identity).then_inc(s_ahi, 1)

            def product(s):
                for t in range(TT):
                    act.wait_ge(s_zf, s * n_z + 3 * t + 1)
                    at_least(act, s_z, RI * TT * s)
                    nc.scalar.activation(k1[:, t], banks[ZB + 3 * t][:], ACT.Identity).then_inc(s_k1, 1)

            def state(n, first=False, last=False):
                for q in range(NQ):
                    s = n * NQ + q
                    attn(s, q % 2)
                    if not (last and q == NQ - 1):
                        split_out(s + 1)
                    if not (first and q == 0):
                        product(s - 1)
                    split_attn(s, q % 2)
                    if q == 0:
                        turns(TJ, len(WJ) + n * n_t, wT)

            turns(WJ, 0, woT)
            split_out(0)
            state(0, first=True)
            with act.Fori(1, N - 1) as n:
                state(n)
            state(N - 1, last=True)
            product(STEPS - 1)

        @block.vector
        def _(dve):
            def turns(jobs, j0, dst):
                for j, (w, m) in enumerate(jobs):
                    dve.wait_ge(s_thi, j0 + j + 1)
                    cols = slice(m * P, (m + 1) * P)
                    nc.vector.tensor_tensor(dst[1][:, w, :, cols], banks[ZB + j % 6][:].rearrange("p (k f) -> p k f", k=KD),
                                            f32(dst[0][:, w, :, cols]), ALU.subtract).then_inc(s_tlo, 1)

            def split_out(s):
                dve.wait_ge(s_ohi, s + 1)
                nc.vector.tensor_tensor(o_[1][:], o_in[:], f32(o_[0][:]), ALU.subtract).then_inc(s_olo, 1)

            def attn_sum(s, par):
                dve.wait_ge(s_ahi0, n_a * (s + 1))
                nc.vector.tensor_tensor(a_f[:, par, 0], a_f[:, par, 1], a_f[:, par, 2], ALU.add).then_inc(s_as, 1)

            def split_attn(s, par):
                dve.wait_ge(s_ahi, s + 1)
                nc.vector.tensor_tensor(a_[1][:], a_f[:, par], f32(a_[0][:]), ALU.subtract).then_inc(s_alo, 1)

            def product(s):
                for t in range(TT):
                    if t == 0:
                        at_least(dve, s_st, 16 * s)
                    dve.wait_ge(s_k1, s * TT + t + 1)
                    dve.wait_ge(s_zf, s * n_z + 3 * t + 2)
                    nc.vector.tensor_tensor(z[:, t, 1], k1[:, t], banks[ZB + 3 * t + 1][:], ALU.add).then_inc(s_z, 1)
                    dve.wait_ge(s_zf, s * n_z + 3 * t + 3)
                    nc.vector.tensor_tensor(z[:, t, 0], k1[:, t], banks[ZB + 3 * t + 2][:], ALU.subtract).then_inc(s_z, 1)

            def state(n, first=False, last=False):
                for q in range(NQ):
                    s = n * NQ + q
                    attn_sum(s, q % 2)
                    if not (last and q == NQ - 1):
                        split_out(s + 1)
                    if not (first and q == 0):
                        product(s - 1)
                    split_attn(s, q % 2)
                    if q == 0:
                        turns(TJ, len(WJ) + n * n_t, wT)

            turns(WJ, 0, woT)
            split_out(0)
            state(0, first=True)
            with dve.Fori(1, N - 1) as n:
                state(n)
            state(N - 1, last=True)
            product(STEPS - 1)


def stage_measure(nc, const, banks, strength, meas_r, meas_i, post_w, post_vectors, z_dram, out):
    TINY = 1e-17
    SHIFTS = ((1, 0, 3), (2, 3, 2), (3, 5, 1))
    PAIRS = [(i, i + d) for d, _, n in SHIFTS for i in range(n)]
    of = lambda i, j: PAIRS.index((min(i, j), max(i, j)))
    with ExitStack() as ctx:
        E = ctx.enter_context
        sb = lambda name, shape, dt=F32: E(nc.sbuf_tensor(name, shape, dt))
        pair = lambda name, shape: [sb(f"{name}_{s}", shape, F32R) for s in ("hi", "lo")]
        sem = lambda name: E(nc.semaphore(name))
        z = sb("z_in", [P, 2, N, RI, D])
        st = sb("strengths", [P, TILES, N, N])
        prod = sb("z_products", [P, len(PAIRS), RI, D])
        m2 = sb("z_mag2", [P, N, D])
        x = sb("z_dots", [P, len(PAIRS), D])
        den = sb("z_norms", [P, len(PAIRS), D])
        gain = sb("gains", [P, N, D])
        sup = sb("superposition", [P, RI, D])
        nrm2 = sb("norm2", [P, 1])
        nrm = sb("norm", [P, 1])
        rn = sb("norm_inverse", [P, 2])
        supT = pair("supT", [P, RI, KD, P])
        amp2 = sb("amp2", [P, RI, D])
        amp = sb("amp", [P, OUT])
        ampT = pair("ampT", [P, KD, P])
        mT = pair("measT", [P, 3, KD, OUT])
        pT = pair("postT", [P, KD, OUT])
        vec = sb("post_vectors", [P, 3, OUT])
        y = sb("y", [P, TILES, OUT])
        stats = sb("post_stats", [P, 6])
        mv = sb("post_mean_var", [P, 2])
        std = sb("post_std", [P, 1])
        rstd = sb("post_rstd", [P, 1])
        eps_ln = sb("eps_post", [P, 1])
        tiny2 = sb("tiny_squared", [P, 1])

        w_rows = [y[:, 0:KD], y[:, KD:2 * KD], gain[:]]
        w_dst = [[t[:, 0] for t in mT], [t[:, 1] for t in mT], [t[:] for t in pT]]
        TJ = [(w, m) for w in range(3) for m in range(KD)]

        s_w, s_st, s_vec, s_zin = sem("meas_rows_in"), sem("strength_in"), sem("post_vectors_in"), [sem(f"z_in_ready_{i}") for i in range(2)]
        s_eps = sem("d_constants_ready")
        s_tf, s_thi, s_tlo, s_neg = sem("d_turn_filled"), sem("d_turn_hi"), sem("d_turn_lo"), sem("minus_mi_ready")
        s_sq, s_m2, s_prod, s_x, s_mm = (sem(n) for n in ("z_squares", "z_mag2_ready", "z_prod_ready", "z_dots_ready", "z_mag2_products"))
        s_den, s_rec, s_cos, s_g0, s_g, s_gz, s_s2, s_sup = (sem(n) for n in ("z_norms_ready", "z_norms_inverse", "cosines_ready", "gains_begun", "gains_step", "weighted_z", "half_sums", "superposition_ready"))
        s_n2, s_n, s_rn = sem("norm2_ready"), sem("norm_ready"), sem("norm_inverse_ready")
        s_sf, s_shi, s_slo = sem("supT_filled"), sem("supT_hi"), sem("supT_lo")
        s_mf, s_a2, s_asum, s_amp = sem("meas_filled"), sem("amp_squares"), sem("amp2_ready"), sem("amp_ready")
        s_pf, s_phi, s_plo = sem("ampT_filled"), sem("ampT_hi"), sem("ampT_lo")
        s_yf, s_y, s_yst, s_var, s_std, s_rstd, s_yn, s_yg, s_yb = (sem(n) for n in ("post_filled", "y_rows", "y_stats", "y_variance", "y_std", "y_rstd", "y_normed", "y_scaled", "y_ready"))
        s_out, s_gelu = sem("out_stored"), sem("gelu_ready")
        B_SUP, B_M, B_AMP, B_Y = 0, 2, 4, 5

        block = E(nc.Block())

        @block.sync
        def _(sp):
            for w, src in zip(w_rows, (meas_r, meas_i, post_w)):
                sp.dma_start(w, src.rearrange("(m p) d -> p m d", p=P)).then_inc(s_w, 16)
            sp.dma_start(st[:], strength.rearrange("(t p) i j -> p t (i j)", p=P)
                         .rearrange("p t (i j) -> p t i j", i=N)).then_inc(s_st, 16)
            for i, v in enumerate(post_vectors):
                sp.dma_start(vec[:, i], v.partition_broadcast(P)).then_inc(s_vec, 16)

            def load(t, par):
                if not isinstance(t, int):
                    wait_apart(sp, s_gz, t - 1)
                sp.dma_start(z[:, par], z_dram[:, bass.ds(t * P, P)].rearrange("n p r d -> p n r d")).then_inc(s_zin[par], 16)

            load(0, 0)
            load(1, 1)
            with sp.Fori(0, (TILES - 2) // 2) as i:
                load(2 * i + 2, 0)
                load(2 * i + 3, 1)
            for t in range(TILES):
                wait_apart(sp, s_gelu, t + 1)
                sp.dma_start(out[t * P:(t + 1) * P, :], y[:, t]).then_inc(s_out, 16)
            sp.wait_ge(s_out, 16 * TILES)

        @block.gpsimd
        def _(pool):
            pool.wait_ge(s_tlo, 2 * KD)
            for s in range(2):
                nc.gpsimd.tensor_scalar(mT[s][:, 2], f32(mT[s][:, 1]), -1.0, None, ALU.mult).then_inc(s_neg, 1)

        @block.tensor
        def _(pe):
            pe.wait_ge(s_w, 16 * 3)
            for j, (w, m) in enumerate(TJ):
                ps = banks[j % NB]
                at_least(pe, s_tlo, j - NB + 1)
                for k in range(KD):
                    mm = nc.tensor.transpose(ps[:, k * P:(k + 1) * P], w_rows[w][:, m, k * P:(k + 1) * P], const.ident[:])
                mm.then_inc(s_tf, 1)
            pe.wait_ge(s_tlo, len(TJ))
            pe.wait_ge(s_neg, 2)

            with pe.Fori(0, TILES) as t:
                pe.wait_ge(s_sup, t + 1)
                for ri in range(RI):
                    for k in range(KD):
                        mm = nc.tensor.transpose(banks[B_SUP + ri][:, k * P:(k + 1) * P], sup[:, ri, k * P:(k + 1) * P],
                                                 const.ident[:])
                    mm.then_inc(s_sf, 1)
                pe.wait_ge(s_slo, RI * (t + 1))
                for o, ws in ((0, (0, 2)), (1, (1, 0))):
                    for ri in range(RI):
                        for k in range(KD):
                            mm = three(nc, banks[B_M + o][:], [s[:, ri, k] for s in supT], [m[:, ws[ri], k] for m in mT],
                                       ri == 0 and k == 0, ri == 1 and k == KD - 1)
                    mm.then_inc(s_mf, 1)
                pe.wait_ge(s_amp, t + 1)
                for k in range(KD):
                    mm = nc.tensor.transpose(banks[B_AMP][:, k * P:(k + 1) * P], amp[:, k * P:(k + 1) * P], const.ident[:])
                mm.then_inc(s_pf, 1)
                pe.wait_ge(s_plo, t + 1)
                for k in range(KD):
                    mm = three(nc, banks[B_Y][:], [a[:, k] for a in ampT], [w[:, k] for w in pT], k == 0, k == KD - 1)
                mm.then_inc(s_yf, 1)

        @block.scalar
        def _(act):
            for j, (w, m) in enumerate(TJ):
                act.wait_ge(s_tf, j + 1)
                nc.scalar.activation(w_dst[w][0][:, :, m * P:(m + 1) * P],
                                     banks[j % NB][:].rearrange("p (k f) -> p k f", k=KD), ACT.Identity).then_inc(s_thi, 1)
            act.wait_ge(s_eps, 2)
            act.wait_ge(s_st, 16)

            def squares(t, par, nth):
                act.wait_ge(s_zin[par], 16 * nth)
                at_least(act, s_sup, t)
                nc.scalar.activation(prod[:, 0:N], z[:, par], ACT.Square).then_inc(s_sq, 1)

            def norms(t):
                act.wait_ge(s_mm, len(SHIFTS) * (t + 1))
                nc.scalar.activation(den[:], den[:], ACT.Sqrt, bias=tiny2[:]).then_inc(s_den, 1)

            def begin_gains(t):
                act.wait_ge(s_cos, t + 1)
                for j in range(N):
                    i = (j + 1) % N
                    nc.scalar.activation(gain[:, j], x[:, of(i, j)], ACT.Identity, bias=cur(t, j, j),
                                         scale=cur(t, i, j)).then_inc(s_g0, 1)

            def cur(t, i, j):
                return st[:, bass.ds(t, 1), i, j]

            def norm(t):
                act.wait_ge(s_sup, t + 1)
                nc.scalar.activation(den[:, 0:RI], sup[:], ACT.Square, accum_out=nrm2[:]).then_inc(s_n2, 1)
                act.wait_ge(s_n2, t + 1)
                nc.scalar.activation(nrm[:], nrm2[:], ACT.Sqrt, bias=const.eps[:]).then_inc(s_n, 1)

            def supT_hi(t):
                for ri in range(RI):
                    act.wait_ge(s_sf, RI * t + ri + 1)
                    nc.scalar.activation(supT[0][:, ri].rearrange("p k f -> p (k f)"), banks[B_SUP + ri][:],
                                         ACT.Identity).then_inc(s_shi, 1)

            def amp_squares(t, par):
                act.wait_ge(s_rn, t + 1)
                at_least(act, s_yn, t)
                for o in range(2):
                    act.wait_ge(s_mf, 2 * t + o + 1)
                    nc.scalar.activation(amp2[:, o], banks[B_M + o][:], ACT.Square, scale=rn[:, par:par + 1]).then_inc(s_a2, 1)

            def amplitude(t):
                act.wait_ge(s_asum, t + 1)
                nc.scalar.activation(amp[:], amp2[:, 0], ACT.Sqrt).then_inc(s_amp, 1)

            def ampT_hi(t):
                act.wait_ge(s_pf, t + 1)
                nc.scalar.activation(ampT[0][:].rearrange("p k f -> p (k f)"), banks[B_AMP][:], ACT.Identity).then_inc(s_phi, 1)

            def deviation(t):
                act.wait_ge(s_var, t + 1)
                nc.scalar.activation(std[:], mv[:, 1:2], ACT.Sqrt, bias=eps_ln[:]).then_inc(s_std, 1)

            def body(t, par, nth, first=False, last=False):
                if not first:
                    supT_hi(t - 1)
                norms(t)
                if not first:
                    amp_squares(t - 1, 1 - par)
                begin_gains(t)
                if not first:
                    amplitude(t - 1)
                    ampT_hi(t - 1)
                if not last:
                    squares(t + 1, 1 - par, nth + par)
                norm(t)
                if not first:
                    deviation(t - 1)

            squares(0, 0, 1)
            body(0, 0, 1, first=True)
            with act.Fori(0, (TILES - 2) // 2) as i:
                body(2 * i + 1, 1, i + 1)
                body(2 * i + 2, 0, i + 2)
            body(TILES - 1, 1, TILES // 2, last=True)
            supT_hi(TILES - 1)
            amp_squares(TILES - 1, 1)
            amplitude(TILES - 1)
            ampT_hi(TILES - 1)
            deviation(TILES - 1)
            for t in range(TILES):
                act.wait_ge(s_yb, t + 1)
                nc.scalar.activation(y[:, t], y[:, t], ACT.Gelu).then_inc(s_gelu, 1)

        @block.vector
        def _(dve):
            nc.vector.memset(eps_ln[:], EPS_LN).then_inc(s_eps, 1)
            nc.vector.memset(tiny2[:], TINY * TINY).then_inc(s_eps, 1)
            for j, (w, m) in enumerate(TJ):
                dve.wait_ge(s_thi, j + 1)
                cols = slice(m * P, (m + 1) * P)
                nc.vector.tensor_tensor(w_dst[w][1][:, :, cols], banks[j % NB][:].rearrange("p (k f) -> p k f", k=KD),
                                        f32(w_dst[w][0][:, :, cols]), ALU.subtract).then_inc(s_tlo, 1)
            dve.wait_ge(s_st, 16)
            dve.wait_ge(s_vec, 16 * 3)

            def dots(t, par):
                zt = z[:, par]
                dve.wait_ge(s_sq, t + 1)
                nc.vector.tensor_tensor(m2[:], prod[:, 0:N, 0], prod[:, 0:N, 1], ALU.add).then_inc(s_m2, 1)
                dve.wait_ge(s_m2, t + 1)
                for d, p0, n in SHIFTS:
                    nc.vector.tensor_tensor(prod[:, p0:p0 + n], zt[:, 0:n], zt[:, d:d + n], ALU.mult).then_inc(s_prod, 1)
                at_least(dve, s_n2, t)
                for d, p0, n in SHIFTS:
                    nc.vector.tensor_tensor(den[:, p0:p0 + n], m2[:, 0:n], m2[:, d:d + n], ALU.mult).then_inc(s_mm, 1)
                dve.wait_ge(s_prod, len(SHIFTS) * (t + 1))
                at_least(dve, s_g0, N * t)
                nc.vector.scalar_tensor_tensor(out=x[:], in0=prod[:, :, 0], scalar=TINY, in1=prod[:, :, 1],
                                               op0=ALU.add, op1=ALU.add).then_inc(s_x, 1)

            def cosines(t):
                dve.wait_ge(s_den, t + 1)
                nc.vector.reciprocal(den[:], den[:]).then_inc(s_rec, 1)
                dve.wait_ge(s_rec, t + 1)
                dve.wait_ge(s_x, t + 1)
                nc.vector.tensor_tensor(x[:], x[:], den[:], ALU.mult).then_inc(s_cos, 1)

            def gains(t):
                dve.wait_ge(s_g0, N * (t + 1))
                for k in range(2, N):
                    for j in range(N):
                        i = (j + k) % N
                        nc.vector.scalar_tensor_tensor(out=gain[:, j], in0=x[:, of(i, j)], scalar=st[:, bass.ds(t, 1), i, j],
                                                       in1=gain[:, j], op0=ALU.mult, op1=ALU.add).then_inc(s_g, 1)
                    dve.wait_ge(s_g, (N - 2) * N * t + (k - 1) * N)

            def superpose(t, par):
                nc.vector.tensor_tensor(prod[:, 0:N], z[:, par], gain[:].unsqueeze(2).to_broadcast([P, N, RI, D]),
                                        ALU.mult).then_inc(s_gz, 1)
                dve.wait_ge(s_gz, t + 1)
                nc.vector.tensor_tensor(prod[:, 0:2], prod[:, 0:2], prod[:, 2:4], ALU.add).then_inc(s_s2, 1)
                dve.wait_ge(s_s2, t + 1)
                at_least(dve, s_sf, RI * t)
                at_least(dve, s_n2, t)
                nc.vector.tensor_tensor(sup[:], prod[:, 0], prod[:, 1], ALU.add).then_inc(s_sup, 1)

            def norm(t, par):
                dve.wait_ge(s_n, t + 1)
                nc.vector.reciprocal(rn[:, par:par + 1], nrm[:]).then_inc(s_rn, 1)

            def supT_lo(t):
                for ri in range(RI):
                    dve.wait_ge(s_shi, RI * t + ri + 1)
                    nc.vector.tensor_tensor(supT[1][:, ri].rearrange("p k f -> p (k f)"), banks[B_SUP + ri][:],
                                            f32(supT[0][:, ri]).rearrange("p k f -> p (k f)"), ALU.subtract).then_inc(s_slo, 1)

            def amp_sum(t):
                dve.wait_ge(s_a2, 2 * (t + 1))
                nc.vector.tensor_tensor(amp2[:, 0], amp2[:, 0], amp2[:, 1], ALU.add).then_inc(s_asum, 1)

            def ampT_lo(t):
                dve.wait_ge(s_phi, t + 1)
                nc.vector.tensor_tensor(ampT[1][:].rearrange("p k f -> p (k f)"), banks[B_AMP][:],
                                        f32(ampT[0][:]).rearrange("p k f -> p (k f)"), ALU.subtract).then_inc(s_plo, 1)

            raw = amp2[:, 1]

            def layer(t):
                yt = raw
                dve.wait_ge(s_yf, t + 1)
                nc.vector.tensor_tensor(yt, banks[B_Y][:], vec[:, 0], ALU.add).then_inc(s_y, 1)
                dve.wait_ge(s_y, t + 1)
                nc.vector.bn_stats(stats[:], yt).then_inc(s_yst, 1)
                wait_apart(dve, s_yst, t + 1)
                nc.vector.bn_aggr(mv[:], stats[:]).then_inc(s_var, 1)

            def layernorm(t):
                yt = y[:, bass.ds(t, 1)].rearrange("p a f -> p (a f)")
                dve.wait_ge(s_std, t + 1)
                nc.vector.reciprocal(rstd[:], std[:]).then_inc(s_rstd, 1)
                dve.wait_ge(s_rstd, t + 1)
                nc.vector.tensor_scalar(yt, raw, mv[:, 0:1], rstd[:], ALU.subtract, ALU.mult).then_inc(s_yn, 1)
                dve.wait_ge(s_yn, t + 1)
                nc.vector.tensor_tensor(yt, yt, vec[:, 1], ALU.mult).then_inc(s_yg, 1)
                dve.wait_ge(s_yg, t + 1)
                nc.vector.tensor_tensor(yt, yt, vec[:, 2], ALU.add).then_inc(s_yb, 1)

            def body(t, par, first=False):
                dots(t, par)
                if not first:
                    supT_lo(t - 1)
                cosines(t)
                if not first:
                    amp_sum(t - 1)
                gains(t)
                if not first:
                    ampT_lo(t - 1)
                superpose(t, par)
                if not first:
                    layer(t - 1)
                norm(t, par)
                if not first:
                    layernorm(t - 1)

            body(0, 0, first=True)
            with dve.Fori(0, (TILES - 2) // 2) as i:
                body(2 * i + 1, 1)
                body(2 * i + 2, 0)
            body(TILES - 1, 1)
            supT_lo(TILES - 1)
            amp_sum(TILES - 1)
            ampT_lo(TILES - 1)
            layer(TILES - 1)
            layernorm(TILES - 1)


def program(nc, t, out):
    w = lambda name: t["L0_rec_" + name]
    sides = ("r", "i")
    folded = nc.dram_tensor("folded_weights", (KD, P, RI, N * KH, FOLD), F32, kind="Internal").ap()
    attended = nc.dram_tensor("attended", (KD * NQ + 1, P, HC, N, TQ), F32, kind="Internal").ap()
    states = nc.dram_tensor("states", (N, B, RI, D), F32, kind="Internal").ap()
    bias_rows = [w(f"e{s}_b2") for s in sides] + [w(f"b{p}_{s}") for s in sides for p in "qkv"] + [w(f"bo_{s}") for s in sides]
    n_bias = sum(v.shape[0] for v in bias_rows) // P
    with ExitStack() as ctx:
        E = ctx.enter_context

        class const:
            ident = E(nc.sbuf_tensor("identity", [P, P], F32))
            mask = E(nc.sbuf_tensor("same_token", [P, 32], F32))
            eps = E(nc.sbuf_tensor("eps", [P, 1], F32))
            zero = E(nc.sbuf_tensor("zero", [P, 1], F32))
            scratch = E(nc.sbuf_tensor("scratch", [P, 8], F32))

        banks = [E(nc.psum_tensor(f"bank_{i}", [P, BANK], F32)) for i in range(NB)]
        biasT = E(nc.sbuf_tensor("biasT", [P, n_bias], F32))
        bias_cols = E(nc.sbuf_tensor("bias_cols", [P, KD, RI * NP, N], F32))
        with ExitStack() as attention:
            hT = [attention.enter_context(nc.sbuf_tensor(f"hT_{s}", [P, RI, KH, B], F32R)) for s in ("hi", "lo")]
            with ExitStack() as folding:
                w2 = [folding.enter_context(nc.sbuf_tensor(f"w2_{s}", [P, RI, N * KD, HID], F32R)) for s in ("hi", "lo")]
                both = lambda name: [w(f"e{s}_{name}") for s in sides]
                stage_encode(nc, const, hT, w2, banks, t["r_x"], both("W1"), both("b1"), both("g1"), both("be1"),
                             both("W2"), bias_rows, biasT)
                stage_fold(nc, const, w2, banks, [[w(f"W{p}_{s}") for p in "qkv"] for s in sides], biasT, bias_cols, folded)
            stage_attend(nc, const, hT, banks, bias_cols, folded, attended)
        bo_cols = biasT[:, n_bias - RI * KD:n_bias].rearrange("p (r m) -> p r m", r=RI)
        stage_interact(nc, const, banks, [w(f"Wo_{s}") for s in sides], w("int_Wr"), w("int_Wi"), bo_cols, attended, states)
        stage_measure(nc, const, banks, t["r_strength"], w("meas_Mr"), w("meas_Mi"), w("post_W"),
                      [w("post_b"), w("post_g"), w("post_be")], states, out)


_INS = ["r_strength", "r_x"] + ["L0_rec_" + n for n in (
    "er_W1", "er_b1", "er_g1", "er_be1", "er_W2", "er_b2", "ei_W1", "ei_b1", "ei_g1", "ei_be1", "ei_W2", "ei_b2",
    "Wq_r", "bq_r", "Wq_i", "bq_i", "Wk_r", "bk_r", "Wk_i", "bk_i", "Wv_r", "bv_r", "Wv_i", "bv_i",
    "Wo_r", "bo_r", "Wo_i", "bo_i", "int_Wr", "int_Wi", "meas_Mr", "meas_Mi", "post_W", "post_b", "post_g", "post_be")]


def kernel(**inputs):
    import numpy as np
    import concourse.bacc as bacc
    from concourse.bass_utils import run_bass_kernel_spmd

    nc = bacc.Bacc("TRN2", target_bir_lowering=False, num_devices=1)
    arrays = {f"in_{n}": np.ascontiguousarray(inputs[n]) for n in _INS}
    tensors = {n: nc.dram_tensor(f"in_{n}", arrays[f"in_{n}"].shape, F32, kind="ExternalInput").ap() for n in _INS}
    out = nc.dram_tensor("out", (B, OUT), F32, kind="ExternalOutput").ap()
    program(nc, tensors, out)
    return run_bass_kernel_spmd(nc, [arrays], core_ids=[0]).results[0]["out"]
```

```python
from contextlib import ExitStack

import concourse.bass as bass
from concourse import mybir

P = 128
BANK = 512
NB = 8

F32 = mybir.dt.float32
F32R = mybir.dt.float32r
ACT = mybir.ActivationFunctionType
ALU = mybir.AluOpType
AX_X = mybir.AxisListType.X

B, IN, HID, D, N, OUT, H = 1024, 256, 256, 512, 4, 512, 8
HD = D // H
TILES = B // P
KI = IN // P
KH = HID // P
KD = D // P
HC = P // HD
TQ = 256
NQ = B // TQ
G = TQ // 32
GH = G * HC
EPS_LN = 1e-5
EPS = 1e-8
RI = 2


class Ring:

    def __init__(self, readers):
        self.readers = readers
        self.per = {r: readers.count(r) for r in set(readers)}

    def nth(self, j):
        return self.readers[:j].count(self.readers[j])

    def bank(self, j):
        return j % NB

    def filled(self, j, it):
        return it * len(self.readers) + j + 1

    def before(self, j, it):
        if j >= NB:
            r = self.readers[j - NB]
            return r, it * self.per[r] + self.nth(j - NB) + 1 + self.per[r]
        last = max(k for k in range(len(self.readers)) if k % NB == j)
        r = self.readers[last]
        return r, it * self.per[r] + self.nth(last) + 1


def three(nc, out, lhs, rhs, first, last):
    (lh, ll), (rh, rl) = lhs, rhs
    nc.tensor.matmul(out, lh, rh, start=first, stop=False)
    nc.tensor.matmul(out, lh, rl, start=False, stop=False)
    return nc.tensor.matmul(out, ll, rh, start=False, stop=last)


def wait_apart(eng, sem, count):
    eng.wait_ge(sem, 1)
    eng.wait_ge(sem, count)


def f32(ap):
    return ap.bitcast(F32)


def stage_encode(nc, const, hT, w2, banks, x, w1, b1, g1, be1, W2, bias_rows, biasT):
    with ExitStack() as ctx:
        E = ctx.enter_context
        sb = lambda name, shape, dt=F32: E(nc.sbuf_tensor(name, shape, dt))
        sem = lambda name: E(nc.semaphore(name))
        x_rows = sb("x_rows", [P, TILES, IN])
        xT = [sb(f"xT_{s}", [P, KI, B], F32R) for s in ("hi", "lo")]
        w1_rows = sb("w1_rows", [P, RI, KH, IN])
        w1T = [sb(f"w1T_{s}", [P, KI, RI, HID], F32R) for s in ("hi", "lo")]
        h = sb("h_rows", [P, TILES, RI, HID])
        w2f = sb("w2_rows", [P, RI, N * KD, HID])
        b1b = sb("b1_bcast", [P, RI, HID])
        g1b = sb("g1_bcast", [P, RI, HID])
        be1b = sb("be1_bcast", [P, RI, HID])
        brows = sb("bias_rows", [P, P])
        stats = sb("ln_stats", [P, TILES * RI, 6])
        mv = sb("ln_mean_var", [P, TILES * RI, 2])
        std = sb("ln_std", [P, TILES * RI])
        rstd = sb("ln_rstd", [P, TILES * RI])
        eps = sb("eps_ln", [P, 1])

        s_x, s_w1, s_w2, s_brow, s_vec = (sem(n) for n in ("x_in", "w1_in", "w2_in", "bias_rows_in", "ln_vectors_in"))
        s_id0, s_id, s_mask = sem("identity_zeroed"), sem("identity_ready"), sem("mask_ready")
        filled = sem("a_filled")
        freed = {"act": sem("a_freed_act"), "dve": sem("a_freed_dve")}
        s_hi = sem("a_hi_ready")
        s_w2hi = sem("w2_hi_ready")
        s_std = sem("ln_std_ready")
        s_ln, s_h, s_eps, s_step = sem("ln_rows_ready"), sem("h_rows_ready"), sem("eps_ready"), sem("a_dve_step")

        XJ = [(k, q) for k in range(KI) for q in range(TILES // 4)]
        HJ = [(ri, k, q) for ri in range(RI) for k in range(KH) for q in range(TILES // 4)]
        n_x, n_w1, n_h = len(XJ), RI, TILES
        first_h = n_x + n_w1 + 1
        first_hT = first_h + n_h
        ring = Ring(["dve"] * (first_hT + len(HJ)))

        block = E(nc.Block())

        @block.sync
        def _(sp):
            sp.dma_start(x_rows[:], x.rearrange("(t p) f -> p t f", p=P)).then_inc(s_x, 16)
            for ri in range(RI):
                sp.dma_start(w1_rows[:, ri], w1[ri].rearrange("(k p) f -> p k f", p=P)).then_inc(s_w1, 16)
            row = 0
            for v in bias_rows:
                n = v.shape[0] // P
                sp.dma_start(brows[row:row + n, :], v.rearrange("(r p) -> r p", p=P)).then_inc(s_brow, 16)
                row += n
            for t, v in ((b1b, b1), (g1b, g1), (be1b, be1)):
                for ri in range(RI):
                    sp.dma_start(t[:, ri], v[ri].partition_broadcast(P)).then_inc(s_vec, 16)
            for ri in range(RI):
                sp.dma_start(w2f[:, ri], W2[ri].rearrange("(k p) f -> p k f", p=P)).then_inc(s_w2, 16)

        @block.gpsimd
        def _(pool):
            nc.gpsimd.memset(const.ident[:], 0.0).then_inc(s_id0, 1)
            pool.wait_ge(s_id0, 1)
            nc.gpsimd.affine_select(out=const.ident[:], in_=const.ident[:], compare_op=ALU.not_equal, fill=1.0,
                                    base=0, pattern=[[-1, P]], channel_multiplier=1).then_inc(s_id, 1)
            for ri in range(RI):
                pool.wait_ge(s_w2hi, ri + 1)
                nc.gpsimd.tensor_tensor(w2[1][:, ri], w2f[:, ri], f32(w2[0][:, ri]), ALU.subtract)

        @block.tensor
        def _(pe):
            def take(j):
                if j >= NB:
                    pe.wait_ge(freed["dve"], j - NB + 1)
                return banks[ring.bank(j)]

            pe.wait_ge(s_id, 1)
            pe.wait_ge(s_x, 16)
            for j, (k, q) in enumerate(XJ):
                ps = take(j)
                for t in range(4):
                    mm = nc.tensor.transpose(ps[:, t * P:(t + 1) * P], x_rows[:, 4 * q + t, k * P:(k + 1) * P],
                                             const.ident[:])
                mm.then_inc(filled, 1)
            pe.wait_ge(s_w1, 16 * RI)
            for ri in range(RI):
                ps = take(n_x + ri)
                for k in range(KI):
                    for m in range(KH):
                        mm = nc.tensor.transpose(ps[:, (k * KH + m) * P:(k * KH + m + 1) * P],
                                                 w1_rows[:, ri, m, k * P:(k + 1) * P], const.ident[:])
                mm.then_inc(filled, 1)
            pe.wait_ge(s_brow, 16 * len(bias_rows))
            ps = take(n_x + n_w1)
            nrow = biasT.shape[1]
            nc.tensor.transpose(ps[:, 0:nrow], brows[0:nrow, :], const.ident[0:nrow, 0:nrow]).then_inc(filled, 1)
            pe.wait_ge(freed["dve"], n_x + n_w1)
            for t in range(TILES):
                ps = take(first_h + t)
                for k in range(KI):
                    mm = three(nc, ps[:], [v[:, k, t * P:(t + 1) * P] for v in xT],
                               [v[:, k].rearrange("p r f -> p (r f)") for v in w1T], k == 0, k == KI - 1)
                mm.then_inc(filled, 1)
            pe.wait_ge(s_h, TILES)
            for j, (ri, k, q) in enumerate(HJ):
                ps = take(first_hT + j)
                for t in range(4):
                    mm = nc.tensor.transpose(ps[:, t * P:(t + 1) * P], h[:, 4 * q + t, ri, k * P:(k + 1) * P],
                                             const.ident[:])
                mm.then_inc(filled, 1)

        @block.scalar
        def _(act):
            for j, (k, q) in enumerate(XJ):
                act.wait_ge(filled, j + 1)
                nc.scalar.activation(xT[0][:, k, q * BANK:(q + 1) * BANK], banks[ring.bank(j)][:],
                                     ACT.Identity).then_inc(s_hi, 1)
            for ri in range(RI):
                act.wait_ge(filled, n_x + ri + 1)
                nc.scalar.activation(w1T[0][:, :, ri, :],
                                     banks[ring.bank(n_x + ri)][:].rearrange("p (k f) -> p k f", k=KI),
                                     ACT.Identity).then_inc(s_hi, 1)
            act.wait_ge(s_w2, 16 * RI)
            for ri in range(RI):
                nc.scalar.activation(w2[0][:, ri], w2f[:, ri], ACT.Identity).then_inc(s_w2hi, 1)
            act.wait_ge(s_eps, 1)
            act.wait_ge(s_ln, 1)
            nc.scalar.activation(std[:], mv[:, :, 1], ACT.Sqrt, bias=eps[:]).then_inc(s_std, 1)
            for t in range(TILES):
                act.wait_ge(s_ln, t + 2)
                nc.scalar.activation(h[:, t], h[:, t], ACT.Gelu).then_inc(s_h, 1)
            for j, (ri, k, q) in enumerate(HJ):
                jj = first_hT + j
                act.wait_ge(filled, jj + 1)
                nc.scalar.activation(hT[0][:, ri, k, q * BANK:(q + 1) * BANK], banks[ring.bank(jj)][:],
                                     ACT.Identity).then_inc(s_hi, 1)

        @block.vector
        def _(dve):
            steps = [0]

            def link(ins):
                steps[0] += 1
                ins.then_inc(s_step, 1)
                dve.wait_ge(s_step, steps[0])

            link(nc.vector.memset(eps[:], EPS_LN))
            nc.vector.memset(const.zero[:], 0.0)
            nc.vector.memset(const.eps[:], EPS).then_inc(s_eps, 1)
            for j, (k, q) in enumerate(XJ):
                dve.wait_ge(s_hi, j + 1)
                cols = slice(q * BANK, (q + 1) * BANK)
                nc.vector.tensor_tensor(xT[1][:, k, cols], banks[ring.bank(j)][:], f32(xT[0][:, k, cols]),
                                        ALU.subtract).then_inc(freed["dve"], 1)
            for ri in range(RI):
                dve.wait_ge(s_hi, n_x + ri + 1)
                nc.vector.tensor_tensor(w1T[1][:, :, ri, :],
                                        banks[ring.bank(n_x + ri)][:].rearrange("p (k f) -> p k f", k=KI),
                                        f32(w1T[0][:, :, ri, :]), ALU.subtract).then_inc(freed["dve"], 1)
            dve.wait_ge(filled, n_x + n_w1 + 1)
            nc.vector.tensor_copy(biasT[:], banks[ring.bank(n_x + n_w1)][:, 0:biasT.shape[1]]).then_inc(freed["dve"], 1)
            dve.wait_ge(s_id, 1)
            nc.vector.tensor_reduce(const.mask[:], const.ident[:].rearrange("p (n t) -> p t n", t=32), AX_X, ALU.add)
            dve.wait_ge(s_vec, 16 * 6)
            for t in range(TILES):
                dve.wait_ge(filled, first_h + t + 1)
                link(nc.vector.tensor_tensor(h[:, t].rearrange("p r f -> p (r f)"), banks[ring.bank(first_h + t)][:],
                                             b1b[:].rearrange("p r f -> p (r f)"), ALU.add))
                nc.vector.bn_stats(stats[:, RI * t, :], h[:, t, 0]).then_inc(freed["dve"], 1)
                link(nc.vector.bn_stats(stats[:, RI * t + 1, :], h[:, t, 1]))
                nc.vector.bn_aggr(mv[:, RI * t, :], stats[:, RI * t, :])
                ins = nc.vector.bn_aggr(mv[:, RI * t + 1, :], stats[:, RI * t + 1, :])
            ins.then_inc(s_ln, 1)
            dve.wait_ge(s_std, 1)
            link(nc.vector.reciprocal(rstd[:], std[:]))
            for t in range(TILES):
                for ri in range(RI):
                    i = RI * t + ri
                    ins = nc.vector.tensor_scalar(h[:, t, ri], h[:, t, ri], mv[:, i, 0:1], rstd[:, i:i + 1],
                                                  ALU.subtract, ALU.mult)
                link(ins)
                link(nc.vector.tensor_tensor(h[:, t], h[:, t], g1b[:], ALU.mult))
                nc.vector.tensor_tensor(h[:, t], h[:, t], be1b[:], ALU.add).then_inc(s_ln, 1)
            for j, (ri, k, q) in enumerate(HJ):
                jj = first_hT + j
                dve.wait_ge(s_hi, n_x + n_w1 + j + 1)
                cols = slice(q * BANK, (q + 1) * BANK)
                nc.vector.tensor_tensor(hT[1][:, ri, k, cols], banks[ring.bank(jj)][:], f32(hT[0][:, ri, k, cols]),
                                        ALU.subtract).then_inc(freed["dve"], 1)


NP = 3
FOLD = NP * P


def stage_fold(nc, const, w2, banks, proj, biasT, bias_cols, c_dram):
    with ExitStack() as ctx:
        E = ctx.enter_context
        sb = lambda name, shape, dt=F32: E(nc.sbuf_tensor(name, shape, dt))
        sem = lambda name: E(nc.semaphore(name))
        rows = sb("proj_rows", [P, RI * NP, D])
        wT = [sb(f"projT_{s}", [P, RI, KD, FOLD], F32R) for s in ("hi", "lo")]
        b2T = [sb(f"b2T_{s}", [P, RI * N * KD], F32R) for s in ("hi", "lo")]
        stage = sb("fold_out", [P, RI, N * KH, FOLD])

        s_rows = sem("proj_rows_in")
        s_stored = [sem(f"folded_stored_{ri}") for ri in range(RI)]
        filled = sem("f_filled")
        freed = {"act": sem("f_freed_act"), "dve": sem("f_freed_dve")}
        s_hi, s_b2, s_b2hi = sem("f_hi_ready"), sem("b2_split"), sem("b2_hi_ready")

        n_t = RI * NP
        FJ = [(ri, n, kh) for ri in range(RI) for n in range(N) for kh in range(KH)]
        ring = Ring(["dve"] * (n_t + 1) + ["act"] * len(FJ))
        n_j = len(ring.readers)
        per = ring.per

        def load(sp, c):
            for i in range(n_t):
                sp.dma_start(rows[:, i, :], proj[i // NP][i % NP][bass.ds(c * P, P), :]).then_inc(s_rows, 16)

        block = E(nc.Block())

        @block.sync
        def _(sp):
            def store(c):
                half = N * KH
                for ri in range(RI):
                    wait_apart(sp, freed["act"], (c + 1) * per["act"] + (ri + 1) * half)
                    sp.dma_start(c_dram[bass.ds(c, 1), :, ri].rearrange("a p k f -> (a p) k f"),
                                 stage[:, ri]).then_inc(s_stored[ri], 16)

            load(sp, 0)
            with sp.Fori(0, KD - 1) as c:
                wait_apart(sp, filled, ring.filled(n_t - 1, c))
                load(sp, c + 1)
                store(c)
            store(KD - 1)
            for ri in range(RI):
                sp.wait_ge(s_stored[ri], 16 * (KD + 1))

        @block.tensor
        def _(pe):
            with pe.Fori(0, KD) as c:
                def take(j):
                    r, v = ring.before(j, c)
                    pe.wait_ge(freed[r], v)
                    return banks[ring.bank(j)]

                pe.wait_ge(s_rows, (c + 1) * 16 * n_t)
                for i in range(n_t):
                    ps = take(i)
                    for k in range(KD):
                        mm = nc.tensor.transpose(ps[:, k * P:(k + 1) * P], rows[:, i, k * P:(k + 1) * P],
                                                 const.ident[:])
                    mm.then_inc(filled, 1)
                ps = take(n_t)
                pe.wait_ge(s_b2, 1)
                pe.wait_ge(freed["dve"], c * per["dve"] + per["dve"] + n_t)
                for i in range(n_t):
                    ri, pr = i // NP, i % NP
                    for k in range(KD):
                        cols = slice(ri * N * KD + k, (ri + 1) * N * KD, KD)
                        mm = three(nc, ps[:, i * N:(i + 1) * N],
                                   [w[:, ri, k, pr * P:(pr + 1) * P] for w in wT], [b[:, cols] for b in b2T],
                                   k == 0, k == KD - 1)
                mm.then_inc(filled, 1)
                for j, (ri, n, kh) in enumerate(FJ):
                    ps = take(n_t + 1 + j)
                    for k in range(KD):
                        mm = three(nc, ps[:, 0:FOLD],
                                   [w[:, ri, n * KD + k, kh * P:(kh + 1) * P] for w in w2],
                                   [w[:, ri, k] for w in wT], k == 0, k == KD - 1)
                    mm.then_inc(filled, 1)

        def out_slot(j):
            ri, n, kh = FJ[j]
            return ri, stage[:, ri, n * KH + kh, :]

        @block.scalar
        def _(act):
            nc.scalar.activation(b2T[0][:], biasT[:, 0:RI * N * KD], ACT.Identity).then_inc(s_b2hi, 1)
            nc.scalar.activation(const.scratch[:, 0:1], const.eps[:], ACT.Identity).then_inc(freed["act"], per["act"])
            with act.Fori(0, KD) as c:
                for i in range(n_t):
                    ri, pr = i // NP, i % NP
                    act.wait_ge(filled, ring.filled(i, c))
                    if i == 0:
                        act.wait_ge(freed["dve"], (c + 1) * per["dve"])
                    nc.scalar.activation(wT[0][:, ri, :, pr * P:(pr + 1) * P],
                                         banks[ring.bank(i)][:].rearrange("p (k f) -> p k f", k=KD),
                                         ACT.Identity).then_inc(s_hi, 1)
                for j, (ri, n, kh) in enumerate(FJ):
                    jj = n_t + 1 + j
                    if n == 0 and kh == 0:
                        act.wait_ge(s_stored[ri], (c + 1) * 16)
                    act.wait_ge(filled, ring.filled(jj, c))
                    nc.scalar.activation(stage[:, ri, n * KH + kh, :], banks[ring.bank(jj)][:, 0:FOLD],
                                         ACT.Identity).then_inc(freed["act"], 1)

        @block.vector
        def _(dve):
            dve.wait_ge(s_b2hi, 1)
            nc.vector.tensor_tensor(b2T[1][:], biasT[:, 0:RI * N * KD], f32(b2T[0][:]), ALU.subtract).then_inc(s_b2, 1)
            nc.vector.memset(const.scratch[:, 1:2], 0.0).then_inc(freed["dve"], per["dve"])
            for ri in range(RI):
                nc.vector.memset(const.scratch[:, 2 + ri:3 + ri], 0.0).then_inc(s_stored[ri], 16)
            with dve.Fori(0, KD) as c:
                for i in range(n_t):
                    ri, pr = i // NP, i % NP
                    dve.wait_ge(s_hi, c * n_t + i + 1)
                    cols = slice(pr * P, (pr + 1) * P)
                    nc.vector.tensor_tensor(wT[1][:, ri, :, cols], banks[ring.bank(i)][:].rearrange("p (k f) -> p k f", k=KD),
                                            f32(wT[0][:, ri, :, cols]), ALU.subtract).then_inc(freed["dve"], 1)
                dve.wait_ge(filled, ring.filled(n_t, c))
                own = biasT[:, RI * N * KD:RI * N * KD + n_t * KD].rearrange("p (i c) -> p i c", c=KD)[:, :, bass.ds(c, 1)]
                nc.vector.tensor_tensor(bias_cols[:, bass.ds(c, 1)].rearrange("p a i n -> p (a i) n"),
                                        banks[ring.bank(n_t)][:, 0:n_t * N].rearrange("p (i n) -> p i n", n=N),
                                        own.to_broadcast([P, n_t, N]), ALU.add).then_inc(freed["dve"], 1)


def stage_attend(nc, const, hT, banks, bias_cols, c_dram, o_dram):
    with ExitStack() as ctx:
        E = ctx.enter_context
        sb = lambda name, shape, dt=F32: E(nc.sbuf_tensor(name, shape, dt))
        pair = lambda name, shape: [sb(f"{name}_{s}", shape, F32R) for s in ("hi", "lo")]
        sem = lambda name: E(nc.semaphore(name))
        SLOTS = 4
        KI_, KR_, NKI_ = 0, 1, 2
        fold_in = sb("fold_in", [P, SLOTS, KH * FOLD])
        fold = pair("fold", [P, RI, N, KH * FOLD])
        bias = sb("bias_chunk", [P, RI, NP, N])
        k_ = pair("k", [P, G, 3, P])
        q_ = pair("q", [P, RI, G, P])
        vT = sb("vT", [P, RI, G, P])
        v_ = pair("v", [P, G, HC, RI, HD])
        sq = sb("squares", [P, 2, GH // 2, 2, P])
        mag2 = sb("masked_mag2", [P, GH // 2, P])
        magc = sb("mag2", [P, GH, N])
        root = sb("magnitude", [P, GH, N])
        top = sb("row_max", [P, GH])
        dif = sb("minus_max", [P, GH, N])
        ex = sb("exps", [P, GH, N])
        den = sb("exp_sum", [P, GH])
        rden = sb("exp_sum_inverse", [P, GH])
        w = sb("weights", [P, GH, N])
        wt = sb("weights_turned", [P, GH, N])
        wt_ = pair("weights_split", [P, GH, N])
        wT = pair("wT", [P, GH, P])
        oT = sb("oT", [P, HC, N, TQ])

        s_in = [sem(f"fold_in_{i}") for i in range(SLOTS)]
        s_fhi, s_flo, s_bias = sem("fold_hi_ready"), sem("fold_lo_ready"), sem("bias_ready")
        filled = sem("b_filled")
        freed = {"act": sem("b_freed_act"), "dve": sem("b_freed_dve")}
        s_hi, s_nki, s_sq = sem("b_hi_ready"), sem("minus_ki_ready"), sem("squares_ready")
        s_sum, s_msk = sem("mag2_summed"), sem("mag2_masked")
        s_mag, s_root, s_top, s_dif = sem("mag2_ready"), sem("magnitude_ready"), sem("max_ready"), sem("minus_max_ready")
        s_ex, s_den, s_rden, s_w, s_wt = (sem(n) for n in ("exps_ready", "exp_sum_ready", "inverse_ready", "weights_ready", "weights_turned_ready"))
        s_wthi, s_wtlo, s_wThi, s_wTlo = (sem(n) for n in ("weights_hi_ready", "weights_lo_ready", "wT_hi_ready", "wT_lo_ready"))
        s_out = sem("oT_stored")

        STEPS = KD * NQ
        VJ = [(ri, n) for ri in range(RI) for n in range(N)]
        KJ = [(ri, n) for ri in (1, 0) for n in range(N)]
        QJ = VJ
        OJ = [(h, gq) for h in range(HC) for gq in range(G // 4)]
        TJ = range(G // 2)
        SJ = range(GH // 2)
        kinds = (["act"] * len(VJ) + ["dve"] * len(KJ) + ["dve"] * len(QJ) + ["dve"] * len(OJ)
                 + ["dve"] * len(TJ) + ["act"] * len(SJ))
        ring = Ring(kinds)
        per, n_j = ring.per, len(kinds)
        j_k = len(VJ)
        j_q = j_k + len(KJ)
        j_o = j_q + len(QJ)
        j_t = j_o + len(OJ)
        j_s = j_t + len(TJ)
        n_hi = len(KJ) + len(QJ) + len(TJ)
        HB = GH // 4
        done = lambda j, it, r: (it + 1) * per[r] + ring.nth(j) + 1

        block = E(nc.Block())

        @block.sync
        def _(sp):
            def store(it):
                wait_apart(sp, freed["dve"], done(j_t - 1, it, "dve"))
                sp.dma_start(o_dram[bass.ds(it, 1)].rearrange("a p h n t -> (a p) (h n t)"),
                             oT[:].rearrange("p h n t -> p (h n t)")).then_inc(s_out, 16)

            with sp.Fori(0, KD) as c:
                for i, (ri, n) in enumerate(VJ):
                    wait_apart(sp, s_flo, (c + 1) * len(VJ) + i + 1 - SLOTS)
                    sp.dma_start(fold_in[:, i % SLOTS], c_dram[bass.ds(c, 1), :, ri, KH * n:KH * n + KH, :]
                                 .rearrange("a p k f -> (a p) (k f)")).then_inc(s_in[i % SLOTS], 16)
                with sp.Fori(0, NQ) as q:
                    store(c * NQ + q)
            sp.wait_ge(freed["dve"], (STEPS + 1) * per["dve"] + len(OJ))
            sp.dma_start(o_dram[STEPS].rearrange("p h n t -> p (h n t)"),
                         oT[:].rearrange("p h n t -> p (h n t)")).then_inc(s_out, 16)
            sp.wait_ge(s_out, 16 * (STEPS + 2))

        @block.gpsimd
        def _(pool):
            def expand(it):
                pool.wait_ge(s_wtlo, it + 1)
                nc.gpsimd.tensor_tensor(wT[1][:].rearrange("p a (n t) -> p (a n) t", t=32),
                                        f32(wt_[1][:]).rearrange("p a n -> p (a n)").unsqueeze(2).to_broadcast([P, GH * N, 32]),
                                        const.mask[:].unsqueeze(1).to_broadcast([P, GH * N, 32]),
                                        ALU.mult).then_inc(s_wTlo, 1)

            with pool.Fori(0, KD) as c:
                with pool.Fori(0, NQ) as q:
                    it = c * NQ + q
                    expand(it)
                    pool.wait_ge(freed["dve"], done(j_k + N - 1, it, "dve"))
                    for s in range(2):
                        nc.gpsimd.tensor_tensor(k_[s][:, :, NKI_, :], const.zero[:].unsqueeze(2).to_broadcast([P, G, P]),
                                                f32(k_[s][:, :, KI_, :]), ALU.subtract).then_inc(s_nki, 1)
            expand(STEPS)

        @block.tensor
        def _(pe):
            def weighted_sum(it, j0, take):
                pe.wait_ge(s_wThi, it + 1)
                pe.wait_ge(s_wTlo, it + 1)
                for j, (h, gq) in enumerate(OJ):
                    ps = take(j0 + j)
                    for g4 in range(4):
                        g = 4 * gq + g4
                        lhs = [v[:, g, h].rearrange("p r d -> p (r d)") for v in v_]
                        rhs = [x[:, h * G + g, :] for x in wT]
                        mm = three(nc, ps[:, g4 * P:(g4 + 1) * P], lhs, rhs, True, True)
                    mm.then_inc(filled, 1)

            with pe.Fori(0, KD) as c:
                with pe.Fori(0, NQ) as q:
                    it = c * NQ + q
                    toks = bass.ds(q * TQ, TQ)

                    def take(j):
                        r, v = ring.before(j, it)
                        pe.wait_ge(freed[r], v)
                        return banks[ring.bank(j)]

                    for j0, pr, jobs in ((0, 2, VJ), (j_k, 1, KJ), (j_q, 0, QJ)):
                        for j, (ri, n) in enumerate(jobs):
                            if pr == 2:
                                pe.wait_ge(s_flo, (c + 1) * len(VJ) + j + 1)
                            ps = take(j0 + j)
                            for kh in range(KH):
                                f0 = kh * FOLD + pr * P
                                mm = three(nc, ps[:, 0:TQ], [f[:, ri, n, f0:f0 + P] for f in fold],
                                           [x[:, ri, kh, toks] for x in hT], kh == 0, kh == KH - 1)
                            mm.then_inc(filled, 1)
                    weighted_sum(it, j_o, take)
                    pe.wait_ge(freed["act"], done(j_k - 1, it, "act"))
                    for j in TJ:
                        ps = take(j_t + j)
                        for g2 in range(2):
                            for ri in range(RI):
                                o = (ri * 2 + g2) * P
                                mm = nc.tensor.transpose(ps[:, o:o + P], vT[:, ri, 2 * j + g2, :], const.ident[:])
                        mm.then_inc(filled, 1)
                    pe.wait_ge(freed["dve"], done(j_o - 1, it, "dve"))
                    pe.wait_ge(s_nki, 2 * it + 2)
                    for j in SJ:
                        ps = take(j_s + j)
                        for x in range(2):
                            gh = 2 * j + x
                            h, g = gh // G, gh % G
                            rows = slice(h * HD, (h + 1) * HD)
                            out = ps[:, x * 2 * P:(x + 1) * 2 * P]
                            for ri, ks in ((0, slice(KR_, NKI_ + 1)), (1, slice(KI_, KR_ + 1))):
                                mm = three(nc, out, [t[rows, ri, g, :] for t in q_],
                                           [t[rows, g, ks, :].rearrange("p s f -> p (s f)") for t in k_],
                                           ri == 0, ri == 1)
                        mm.then_inc(filled, 1)
            pe.wait_ge(freed["act"], (STEPS + 1) * per["act"])
            weighted_sum(STEPS, 0, lambda j: banks[j])

        @block.scalar
        def _(act):
            nc.scalar.activation(const.scratch[:, 0:1], const.eps[:], ACT.Identity).then_inc(freed["act"], per["act"])

            def magnitudes(it):
                act.wait_ge(s_mag, 2 * it + 2)
                nc.scalar.activation(root[:], magc[:], ACT.Sqrt, bias=const.eps[:]).then_inc(s_root, 1)

            def exponentials(it):
                act.wait_ge(s_dif, it + 1)
                nc.scalar.activation(ex[:], dif[:], ACT.Exp, scale=float(HD) ** -0.5).then_inc(s_ex, 1)

            with act.Fori(0, KD) as c:
                for i, (ri, n) in enumerate(VJ):
                    act.wait_ge(s_in[i % SLOTS], (c * (len(VJ) // SLOTS) + i // SLOTS + 1) * 16)
                    nc.scalar.activation(fold[0][:, ri, n], fold_in[:, i % SLOTS], ACT.Identity).then_inc(s_fhi, 1)
                act.wait_ge(s_bias, c + 1)
                with act.Fori(0, NQ) as q:
                    it = c * NQ + q
                    for j, (ri, n) in enumerate(VJ):
                        if j == 2:
                            magnitudes(it)
                        if j == 4:
                            exponentials(it)
                        act.wait_ge(filled, ring.filled(j, it))
                        nc.scalar.activation(vT[:, ri, :, n * 32:(n + 1) * 32],
                                             banks[ring.bank(j)][:, 0:TQ].rearrange("p (g t) -> p g t", t=32),
                                             ACT.Identity, bias=bias[:, ri, 2, n:n + 1]).then_inc(freed["act"], 1)
                    for j0, pr, jobs in ((j_k, 1, KJ), (j_q, 0, QJ)):
                        for j, (ri, n) in enumerate(jobs):
                            act.wait_ge(filled, ring.filled(j0 + j, it))
                            dst = k_[0][:, :, 1 - ri, :] if pr == 1 else q_[0][:, ri]
                            nc.scalar.activation(dst[:, :, n * 32:(n + 1) * 32],
                                                 banks[ring.bank(j0 + j)][:, 0:TQ].rearrange("p (g t) -> p g t", t=32),
                                                 ACT.Identity, bias=bias[:, ri, pr, n:n + 1]).then_inc(s_hi, 1)
                    for j in TJ:
                        act.wait_ge(filled, ring.filled(j_t + j, it))
                        nc.scalar.activation(v_[0][:, 2 * j:2 * j + 2].rearrange("p g h r d -> p r (g h) d"),
                                             banks[ring.bank(j_t + j)][:].rearrange("p (r a d) -> p r a d", r=RI, d=HD),
                                             ACT.Identity).then_inc(s_hi, 1)
                    for j in SJ:
                        act.wait_ge(filled, ring.filled(j_s + j, it))
                        nc.scalar.activation(sq[:, j // HB, 2 * (j % HB):2 * (j % HB) + 2].rearrange("p a r f -> p (a r f)"),
                                             banks[ring.bank(j_s + j)][:], ACT.Square).then_inc(freed["act"], 1)
            magnitudes(STEPS)
            exponentials(STEPS)

        @block.vector
        def _(dve):
            nc.vector.memset(const.scratch[:, 1:2], 0.0).then_inc(freed["dve"], per["dve"])
            nc.vector.memset(const.scratch[:, 2:3], 0.0).then_inc(s_flo, len(VJ))
            nc.vector.memset(const.scratch[:, 3:4], 0.0).then_inc(s_out, 16)
            nc.vector.memset(f32(v_[0][:]), 0.0)
            nc.vector.memset(f32(v_[1][:]), 0.0)
            nc.vector.memset(magc[:], 0.0).then_inc(s_mag, 2)

            def softmax_a(it):
                dve.wait_ge(s_root, it + 1)
                nc.vector.tensor_reduce(top[:], root[:], AX_X, ALU.max).then_inc(s_top, 1)
                dve.wait_ge(s_top, it + 1)
                nc.vector.tensor_tensor(dif[:], root[:], top[:].unsqueeze(2).to_broadcast([P, GH, N]),
                                        ALU.subtract).then_inc(s_dif, 1)

            def softmax_b(it):
                dve.wait_ge(s_ex, it + 1)
                nc.vector.tensor_reduce(den[:], ex[:], AX_X, ALU.add).then_inc(s_den, 1)
                dve.wait_ge(s_den, it + 1)
                nc.vector.reciprocal(rden[:], den[:]).then_inc(s_rden, 1)
                dve.wait_ge(s_rden, it + 1)
                nc.vector.tensor_tensor(w[:], ex[:], rden[:].unsqueeze(2).to_broadcast([P, GH, N]),
                                        ALU.mult).then_inc(s_w, 1)
                dve.wait_ge(s_w, it + 1)
                for n in range(N):
                    for m in range(N):
                        ins = nc.vector.tensor_copy(wt[m * 32:(m + 1) * 32, :, n], w[n * 32:(n + 1) * 32, :, m])
                        ins.then_inc(s_wt, 1)
                dve.wait_ge(s_wt, N * N * (it + 1))
                nc.vector.tensor_copy(wt_[0][:], wt[:]).then_inc(s_wthi, 1)
                dve.wait_ge(s_wthi, it + 1)
                nc.vector.tensor_tensor(wt_[1][:], wt[:], f32(wt_[0][:]), ALU.subtract).then_inc(s_wtlo, 1)
                nc.vector.tensor_tensor(wT[0][:].rearrange("p a (n t) -> p (a n) t", t=32),
                                        f32(wt_[0][:]).rearrange("p a n -> p (a n)").unsqueeze(2).to_broadcast([P, GH * N, 32]),
                                        const.mask[:].unsqueeze(1).to_broadcast([P, GH * N, 32]),
                                        ALU.mult).then_inc(s_wThi, 1)

            def outputs(j0, fill):
                for j, (h, gq) in enumerate(OJ):
                    dve.wait_ge(filled, fill + j + 1)
                    nc.vector.tensor_copy(oT[:, h, :, gq * BANK // N:(gq + 1) * BANK // N].rearrange("p n (g t) -> p g n t", t=32),
                                          banks[(j0 + j) % NB][:].rearrange("p (g n t) -> p g n t", n=N, t=32)
                                          ).then_inc(freed["dve"], 1)

            with dve.Fori(0, KD) as c:
                nc.vector.tensor_copy(bias[:].rearrange("p r a n -> p (r a) n"),
                                      bias_cols[:, bass.ds(c, 1)].rearrange("p a i n -> p (a i) n")).then_inc(s_bias, 1)
                for i, (ri, n) in enumerate(VJ):
                    dve.wait_ge(s_fhi, c * len(VJ) + i + 1)
                    nc.vector.tensor_tensor(fold[1][:, ri, n], fold_in[:, i % SLOTS], f32(fold[0][:, ri, n]),
                                            ALU.subtract).then_inc(s_flo, 1)
                with dve.Fori(0, NQ) as q:
                    it = c * NQ + q
                    softmax_a(it)
                    softmax_b(it)
                    for i, (j0, pr, jobs) in enumerate(((j_k, 1, KJ), (j_q, 0, QJ))):
                        for j, (ri, n) in enumerate(jobs):
                            dve.wait_ge(s_hi, it * n_hi + i * len(KJ) + j + 1)
                            cols = slice(n * 32, (n + 1) * 32)
                            hi, lo = [k_[s][:, :, 1 - ri, cols] if pr == 1 else q_[s][:, ri, :, cols] for s in range(2)]
                            nc.vector.scalar_tensor_tensor(out=lo, in0=banks[ring.bank(j0 + j)][:, 0:TQ].rearrange("p (g t) -> p g t", t=32),
                                                           scalar=bias[:, ri, pr, n:n + 1], in1=f32(hi),
                                                           op0=ALU.add, op1=ALU.subtract).then_inc(freed["dve"], 1)
                    dve.wait_ge(s_out, (it + 1) * 16)
                    outputs(j_o, it * n_j + j_o)
                    for j in TJ:
                        dve.wait_ge(s_hi, it * n_hi + len(KJ) + len(QJ) + j + 1)
                        hi, lo = [v_[s][:, 2 * j:2 * j + 2].rearrange("p g h r d -> p r (g h) d") for s in range(2)]
                        nc.vector.tensor_tensor(lo, banks[ring.bank(j_t + j)][:].rearrange("p (r a d) -> p r a d", r=RI, d=HD),
                                                f32(hi), ALU.subtract).then_inc(freed["dve"], 1)
                    for b in range(2):
                        dve.wait_ge(freed["act"], done(j_s + (b + 1) * HB - 1, it, "act"))
                        dve.wait_ge(s_mag, 2 * it + b + 2)
                        nc.vector.tensor_tensor(mag2[:], sq[:, b, :, 0, :], sq[:, b, :, 1, :], ALU.add).then_inc(s_sum, 1)
                        dve.wait_ge(s_sum, 2 * it + b + 1)
                        m2 = mag2[:].rearrange("p a (n t) -> p (a n) t", t=32)
                        nc.vector.tensor_tensor(m2, m2, const.mask[:].unsqueeze(1).to_broadcast([P, GH * N // 2, 32]),
                                                ALU.mult).then_inc(s_msk, 1)
                        dve.wait_ge(s_msk, 2 * it + b + 1)
                        nc.vector.tensor_reduce(magc[:, b * GH // 2:(b + 1) * GH // 2].rearrange("p a n -> p (a n)"),
                                                m2, AX_X, ALU.add).then_inc(s_mag, 1)
            softmax_a(STEPS)
            softmax_b(STEPS)
            dve.wait_ge(s_out, (STEPS + 1) * 16)
            outputs(0, STEPS * n_j)


def at_least(eng, sem, count):
    if not isinstance(count, int) or count > 0:
        eng.wait_ge(sem, count)


def stage_interact(nc, const, banks, wo, int_r, int_i, bo_cols, o_dram, z_dram):
    with ExitStack() as ctx:
        E = ctx.enter_context
        sb = lambda name, shape, dt=F32: E(nc.sbuf_tensor(name, shape, dt))
        pair = lambda name, shape: [sb(f"{name}_{s}", shape, F32R) for s in ("hi", "lo")]
        sem = lambda name: E(nc.semaphore(name))
        TT = TQ // P
        rows = sb("int_rows", [P, 3, KD, D])
        woT = pair("woT", [P, RI, KD, D])
        wT = pair("intT", [P, 3, KD, D])
        o_in = sb("out_in", [P, RI, KD, TQ])
        o_ = pair("out", [P, RI, KD, TQ])
        a_f = sb("attn_f", [P, 2, 3, KD, TQ])
        a_ = pair("attn", [P, 3, KD, TQ])
        k1 = sb("k1", [P, TT, D])
        z = sb("z_out", [P, TT, RI, D])

        s_wo, s_int, s_oin = sem("wo_in"), sem("int_in"), sem("out_in_ready")
        s_sums = sem("int_sums_ready")
        s_tf, s_thi, s_tlo = sem("turn_filled"), sem("turn_hi"), sem("turn_lo")
        s_af, s_ahi0, s_as = sem("attn_filled"), sem("attn_evacuated"), sem("attn_sum_ready")
        s_ahi, s_alo = sem("attn_hi"), sem("attn_lo")
        s_ohi, s_olo = sem("out_hi"), sem("out_lo")
        s_zf, s_k1, s_z, s_st = sem("z_filled"), sem("k1_ready"), sem("z_ready"), sem("z_stored")

        STEPS = N * NQ
        WJ = [(ri, m) for ri in range(RI) for m in range(KD)]
        TJ = [(w, m) for w in range(3) for m in range(KD)]
        AJ = [(ri, m) for ri in range(RI) for m in range(KD)]
        ZB = 2
        n_t, n_a, n_z = len(TJ), len(AJ), 3 * TT
        SRC = (0, 1, 2)
        o_view = o_dram[1:].rearrange("(c q) p h n t -> q c p h n t", q=NQ)
        z_view = z_dram.rearrange("n (q k p) r d -> n q p k (r d)", p=P, k=TT)

        def turned(n):
            return len(WJ) + (n + 1) * n_t

        block = E(nc.Block())

        @block.sync
        def _(sp):
            def load_out(n, q):
                for ri in range(RI):
                    for hh in range(HC):
                        src = o_view[q, :, ri * HD:(ri + 1) * HD, hh, bass.ds(n, 1), :].rearrange("c p a t -> p (a c) t")
                        sp.dma_start(o_in[hh * HD:(hh + 1) * HD, ri], src).then_inc(s_oin, 16)

            def store(n, q):
                wait_apart(sp, s_z, RI * TT * (n * NQ + q + 1))
                sp.dma_start(z_view[bass.ds(n, 1), q].rearrange("a p k f -> (a p) k f"),
                             z[:].rearrange("p k r d -> p k (r d)")).then_inc(s_st, 16)

            def state(n, first, last):
                for q in range(NQ):
                    if not (last and q == NQ - 1):
                        wait_apart(sp, s_olo, n * NQ + q + 1)
                        load_out(n + (q + 1) // NQ, (q + 1) % NQ)
                    if not (first and q == 0):
                        store(n - (q == 0), (q - 1) % NQ)

            for ri in range(RI):
                sp.dma_start(rows[:, ri], wo[ri].rearrange("(m p) d -> p m d", p=P)).then_inc(s_wo, 16)
            load_out(0, 0)
            state(0, True, False)
            with sp.Fori(1, N - 1) as n:
                state(n, False, False)
            state(N - 1, False, True)
            store(N - 1, NQ - 1)
            sp.wait_ge(s_st, 16 * STEPS)

        @block.gpsimd
        def _(pool):
            def state(n):
                pool.wait_ge(s_tf, len(WJ) + n * n_t)
                for i, src in enumerate((int_r, int_i)):
                    pool.dma_start(rows[:, i], src[bass.ds(n, 1)].rearrange("a (m p) d -> p (a m) d", p=P)).then_inc(s_int, 16)
                pool.wait_ge(s_int, 32 * (n + 1))
                nc.gpsimd.tensor_tensor(rows[:, 2], rows[:, 0], rows[:, 1], ALU.add).then_inc(s_sums, 1)
                pool.wait_ge(s_sums, 2 * n + 1)
                nc.gpsimd.tensor_tensor(rows[:, 1], rows[:, 1], rows[:, 0], ALU.subtract).then_inc(s_sums, 1)

            state(0)
            with pool.Fori(1, N) as n:
                state(n)

        @block.tensor
        def _(pe):
            def turns(jobs, j0):
                for j, (w, m) in enumerate(jobs):
                    ps = banks[ZB + j % 6]
                    at_least(pe, s_tlo, j0 + j - 5)
                    for k in range(KD):
                        mm = nc.tensor.transpose(ps[:, k * P:(k + 1) * P], rows[:, w, m, k * P:(k + 1) * P],
                                                 const.ident[:])
                    mm.then_inc(s_tf, 1)

            def attn(n, q):
                s = n * NQ + q
                pe.wait_ge(s_olo, s + 1)
                for j, (ri, m) in enumerate(AJ):
                    ps = banks[j % ZB]
                    at_least(pe, s_ahi0, s * n_a + j - ZB + 1)
                    for k in range(KD):
                        mm = three(nc, ps[:, 0:TQ], [w[:, ri, k, m * P:(m + 1) * P] for w in woT],
                                   [o[:, ri, k] for o in o_], k == 0, k == KD - 1)
                    mm.then_inc(s_af, 1)

            def product(n, s):
                pe.wait_ge(s_alo, s + 1)
                pe.wait_ge(s_tlo, turned(n))
                at_least(pe, s_z, RI * TT * s)
                for t in range(TT):
                    for i in range(3):
                        ps = banks[ZB + 3 * t + i]
                        for k in range(KD):
                            mm = three(nc, ps[:], [a[:, i, k, t * P:(t + 1) * P] for a in a_],
                                       [w[:, i, k] for w in wT], k == 0, k == KD - 1)
                        mm.then_inc(s_zf, 1)

            def turn_state(n):
                pe.wait_ge(s_sums, 2 * n + 2)
                at_least(pe, s_z, RI * TT * NQ * n)
                turns(TJ, len(WJ) + n * n_t)

            pe.wait_ge(s_wo, 16 * RI)
            turns(WJ, 0)
            def state(n, first=False):
                for q in range(NQ):
                    attn(n, q)
                    if q:
                        product(n, n * NQ + q - 1)
                    elif not first:
                        product(n - 1, n * NQ - 1)
                    if q == 0:
                        turn_state(n)

            state(0, True)
            with pe.Fori(1, N - 1) as n:
                state(n)
            state(N - 1)
            product(N - 1, STEPS - 1)

        @block.scalar
        def _(act):
            def turns(jobs, j0, dst):
                for j, (w, m) in enumerate(jobs):
                    act.wait_ge(s_tf, j0 + j + 1)
                    nc.scalar.activation(dst[0][:, w, :, m * P:(m + 1) * P],
                                         banks[ZB + j % 6][:].rearrange("p (k f) -> p k f", k=KD),
                                         ACT.Identity).then_inc(s_thi, 1)

            def split_out(s):
                act.wait_ge(s_oin, 16 * RI * HC * (s + 1))
                nc.scalar.activation(o_[0][:], o_in[:], ACT.Identity).then_inc(s_ohi, 1)

            def attn(s, par):
                for j, (ri, m) in enumerate(AJ):
                    act.wait_ge(s_af, s * n_a + j + 1)
                    if j == 0:
                        at_least(act, s_alo, s - 1)
                    nc.scalar.activation(a_f[:, par, 1 + ri, m], banks[j % ZB][:, 0:TQ], ACT.Identity,
                                         bias=bo_cols[:, ri, m:m + 1]).then_inc(s_ahi0, 1)

            def split_attn(s, par):
                act.wait_ge(s_as, s + 1)
                at_least(act, s_zf, n_z * s)
                nc.scalar.activation(a_[0][:], a_f[:, par], ACT.Identity).then_inc(s_ahi, 1)

            def product(s):
                for t in range(TT):
                    act.wait_ge(s_zf, s * n_z + 3 * t + 1)
                    at_least(act, s_z, RI * TT * s)
                    nc.scalar.activation(k1[:, t], banks[ZB + 3 * t][:], ACT.Identity).then_inc(s_k1, 1)

            def state(n, first=False, last=False):
                for q in range(NQ):
                    s = n * NQ + q
                    attn(s, q % 2)
                    if not (last and q == NQ - 1):
                        split_out(s + 1)
                    if not (first and q == 0):
                        product(s - 1)
                    split_attn(s, q % 2)
                    if q == 0:
                        turns(TJ, len(WJ) + n * n_t, wT)

            turns(WJ, 0, woT)
            split_out(0)
            state(0, first=True)
            with act.Fori(1, N - 1) as n:
                state(n)
            state(N - 1, last=True)
            product(STEPS - 1)

        @block.vector
        def _(dve):
            def turns(jobs, j0, dst):
                for j, (w, m) in enumerate(jobs):
                    dve.wait_ge(s_thi, j0 + j + 1)
                    cols = slice(m * P, (m + 1) * P)
                    nc.vector.tensor_tensor(dst[1][:, w, :, cols], banks[ZB + j % 6][:].rearrange("p (k f) -> p k f", k=KD),
                                            f32(dst[0][:, w, :, cols]), ALU.subtract).then_inc(s_tlo, 1)

            def split_out(s):
                dve.wait_ge(s_ohi, s + 1)
                nc.vector.tensor_tensor(o_[1][:], o_in[:], f32(o_[0][:]), ALU.subtract).then_inc(s_olo, 1)

            def attn_sum(s, par):
                dve.wait_ge(s_ahi0, n_a * (s + 1))
                nc.vector.tensor_tensor(a_f[:, par, 0], a_f[:, par, 1], a_f[:, par, 2], ALU.add).then_inc(s_as, 1)

            def split_attn(s, par):
                dve.wait_ge(s_ahi, s + 1)
                nc.vector.tensor_tensor(a_[1][:], a_f[:, par], f32(a_[0][:]), ALU.subtract).then_inc(s_alo, 1)

            def product(s):
                for t in range(TT):
                    if t == 0:
                        at_least(dve, s_st, 16 * s)
                    dve.wait_ge(s_k1, s * TT + t + 1)
                    dve.wait_ge(s_zf, s * n_z + 3 * t + 2)
                    nc.vector.tensor_tensor(z[:, t, 1], k1[:, t], banks[ZB + 3 * t + 1][:], ALU.add).then_inc(s_z, 1)
                    dve.wait_ge(s_zf, s * n_z + 3 * t + 3)
                    nc.vector.tensor_tensor(z[:, t, 0], k1[:, t], banks[ZB + 3 * t + 2][:], ALU.subtract).then_inc(s_z, 1)

            def state(n, first=False, last=False):
                for q in range(NQ):
                    s = n * NQ + q
                    attn_sum(s, q % 2)
                    if not (last and q == NQ - 1):
                        split_out(s + 1)
                    if not (first and q == 0):
                        product(s - 1)
                    split_attn(s, q % 2)
                    if q == 0:
                        turns(TJ, len(WJ) + n * n_t, wT)

            turns(WJ, 0, woT)
            split_out(0)
            state(0, first=True)
            with dve.Fori(1, N - 1) as n:
                state(n)
            state(N - 1, last=True)
            product(STEPS - 1)


def stage_measure(nc, const, banks, strength, meas_r, meas_i, post_w, post_vectors, z_dram, y_dram, out):
    TINY = 1e-17
    SHIFTS = ((1, 0, 3), (2, 3, 2), (3, 5, 1))
    PAIRS = [(i, i + d) for d, _, n in SHIFTS for i in range(n)]
    NPAIR = len(PAIRS)
    of = lambda i, j: PAIRS.index((min(i, j), max(i, j)))
    HALVES = (slice(0, 3), slice(3, 6))
    ZBUF = 3
    with ExitStack() as ctx:
        E = ctx.enter_context
        sb = lambda name, shape, dt=F32: E(nc.sbuf_tensor(name, shape, dt))
        pair = lambda name, shape: [sb(f"{name}_{s}", shape, F32R) for s in ("hi", "lo")]
        sem = lambda name: E(nc.semaphore(name))
        z = sb("z_in", [P, ZBUF, N, RI, D])
        st = sb("strengths", [P, TILES, N, N])
        st_neg = sb("strengths_negated", [P, TILES, N, N])
        sq = sb("z_squares", [P, N, RI, D])
        root = sb("root", [P, NPAIR, D])
        seed = sb("seed", [P, NPAIR, D])
        inv = sb("root_inverse_negated", [P, NPAIR, D])
        x = sb("cosines", [P, NPAIR, D])
        gz = sb("weighted_z", [P, N, RI, D])
        gain = sq[:, :, 1]
        nrm = sb("norm", [P, 1])
        rn = sb("norm_inverse", [P, 1])
        ones = sb("ones", [P, 1])
        supT = pair("supT", [P, RI + 1, KD, P])
        squares = sb("sup_squares", [P, RI, KD * P])
        amp = squares[:, 0]
        ampT = pair("ampT", [P, KD, P])
        mT = pair("measT", [P, RI, KD, OUT])
        pT = pair("postT", [P, KD, OUT])
        post_b = sb("post_b_bcast", [P, OUT])
        y_row = sb("y_rows", [P, OUT])
        stats = sb("post_stats", [P, TILES, 6])
        mv = sb("post_mean_var", [P, TILES, 2])
        std = sb("post_std", [P, TILES])
        rstd = sb("post_rstd", [P, TILES])
        eps_ln = sb("eps_post", [P, 1])
        tiny2 = sb("tiny_squared", [P, 1])

        im = gz[:].rearrange("p n r d -> p (n r) d")[:, 0:NPAIR]
        post_g, post_be = gain[:, 0], gain[:, 1]
        y = z[:, 0].rearrange("p n r d -> p (n r) d")
        w_rows = [gz[:, 0:2].rearrange("p n r d -> p (n r) d"), gz[:, 2:4].rearrange("p n r d -> p (n r) d"), x[:, 0:KD]]
        w_dst = [[t[:, 0] for t in mT], [t[:, 1] for t in mT], [t[:] for t in pT]]
        TJ = [(w, m) for w in range(3) for m in range(KD)]

        s_w, s_st, s_vec, s_gbe = sem("meas_rows_in"), sem("strength_in"), sem("post_b_in"), sem("post_g_be_in")
        s_zin = [sem(f"z_in_ready_{i}") for i in range(ZBUF)]
        s_eps, s_neg_st = sem("d_constants_ready"), sem("strengths_negated_ready")
        s_tf, s_thi, s_tlo = sem("d_turn_filled"), sem("d_turn_hi"), sem("d_turn_lo")
        s_sq, s_m2, s_mm, s_root, s_ln, s_seed, s_newt = (sem(n) for n in (
            "z_squares_ready", "z_mag2_ready", "z_mag2_products", "roots_ready", "ln_ready", "seed_ready", "root_times_seed"))
        s_inv, s_re, s_im, s_x, s_cos = (sem(n) for n in ("root_inverse_ready", "real_products", "imag_products", "dots_ready", "cosines_ready"))
        s_g0, s_g, s_gz, s_gz3 = (sem(n) for n in ("gains_begun", "gains_step", "weighted_z_ready", "weighted_z3_ready"))
        s_nf, s_n, s_rn = sem("norm2_filled"), sem("norm_ready"), sem("norm_inverse_ready")
        s_sf, s_shi, s_slo, s_sneg = sem("supT_filled"), sem("supT_hi"), sem("supT_lo"), sem("supT_negated_lo")
        s_mf, s_a2, s_asum, s_amp = sem("meas_filled"), sem("amp_squares"), sem("amp2_ready"), sem("amp_ready")
        s_pf, s_phi, s_plo = sem("ampT_filled"), sem("ampT_hi"), sem("ampT_lo")
        s_yf, s_y, s_yst, s_var, s_std, s_rstd, s_yn, s_yg, s_yb = (sem(n) for n in ("post_filled", "y_rows", "y_stats", "y_variance", "y_std", "y_rstd", "y_normed", "y_scaled", "y_ready"))
        s_ystored, s_yin = sem("y_rows_stored"), sem("y_rows_back")
        s_out, s_gelu = sem("out_stored"), sem("gelu_ready")
        B_SUP, B_M, B_AMP, B_Y, B_N = 0, 2, 4, 5, 6

        block = E(nc.Block())

        @block.sync
        def _(sp):
            def load(t):
                sp.dma_start(z[:, t % ZBUF], z_dram[:, t * P:(t + 1) * P].rearrange("n p r d -> p n r d")).then_inc(s_zin[t % ZBUF], 16)

            load(0)
            for w, src in zip(w_rows, (meas_r, meas_i, post_w)):
                sp.dma_start(w, src.rearrange("(m p) d -> p m d", p=P)).then_inc(s_w, 16)
            sp.dma_start(st[:], strength.rearrange("(t p) i j -> p t (i j)", p=P)
                         .rearrange("p t (i j) -> p t i j", i=N)).then_inc(s_st, 16)
            sp.dma_start(post_b[:], post_vectors[0].partition_broadcast(P)).then_inc(s_vec, 16)
            load(1)
            load(2)

            def store_rows(t):
                sp.wait_ge(s_y, t + 1)
                sp.dma_start(y_dram[t], y_row[:]).then_inc(s_ystored, 16)

            for t in range(ZBUF, TILES):
                sp.wait_ge(s_gz, t - ZBUF + 1)
                sp.wait_ge(s_gz3, t - ZBUF + 1)
                load(t)
                store_rows(t - ZBUF)
            for t in range(TILES - ZBUF, TILES - 1):
                store_rows(t)
            sp.wait_ge(s_ystored, 16 * (TILES - 1))
            sp.dma_start(y[:, 0:TILES - 1], y_dram.rearrange("t p f -> p t f")).then_inc(s_yin, 16)
            sp.wait_ge(s_gz, TILES)
            sp.wait_ge(s_gz3, TILES)
            for dst, v in ((post_g, post_vectors[1]), (post_be, post_vectors[2])):
                sp.dma_start(dst, v.partition_broadcast(P)).then_inc(s_gbe, 16)
            for t in range(TILES):
                sp.wait_ge(s_gelu, t + 1)
                sp.dma_start(out[t * P:(t + 1) * P, :], y[:, t]).then_inc(s_out, 16)
            sp.wait_ge(s_out, 16 * TILES)

        @block.gpsimd
        def _(pool):
            def mag2(t):
                for h in range(2):
                    pool.wait_ge(s_sq, 2 * t + h + 1)
                    s = sq[:, 2 * h:2 * h + 2]
                    nc.gpsimd.tensor_tensor(s[:, :, 0], s[:, :, 0], s[:, :, 1], ALU.add).then_inc(s_m2, 1)
                pool.wait_ge(s_m2, 2 * t + 2)

            def mag2_products(t, half):
                for d, p0, n in SHIFTS[:1] if half == 0 else SHIFTS[1:]:
                    at_least(pool, s_inv, 2 * t + half - 1)
                    nc.gpsimd.tensor_tensor(root[:, p0:p0 + n], sq[:, 0:n, 0], sq[:, d:d + n, 0], ALU.mult).then_inc(s_mm, 1)

            def newton(t):
                for h, s in enumerate(HALVES):
                    pool.wait_ge(s_seed, 2 * t + h + 1)
                    nc.gpsimd.tensor_tensor(root[:, s], root[:, s], seed[:, s], ALU.mult).then_inc(s_newt, 1)

            def negate(t):
                pool.wait_ge(s_slo, RI * (t + 1))
                nc.gpsimd.tensor_tensor(supT[1][:, 2].rearrange("p k f -> p (k f)"), const.zero[:].to_broadcast([P, KD * P]),
                                        f32(supT[1][:, 1]).rearrange("p k f -> p (k f)"), ALU.subtract).then_inc(s_sneg, 1)

            def weight_last(t, par):
                pool.wait_ge(s_g, (N - 2) * N * (t + 1))
                at_least(pool, s_sf, RI * t)
                nc.gpsimd.tensor_tensor(gz[:, N - 1], z[:, par, N - 1], gain[:, N - 1].unsqueeze(1).to_broadcast([P, RI, D]),
                                        ALU.mult).then_inc(s_gz3, 1)

            def body(t, par, first=False, last=False):
                if not last:
                    mag2(t + 1)
                    mag2_products(t + 1, 0)
                    mag2_products(t + 1, 1)
                if not first:
                    negate(t - 1)
                if not last:
                    newton(t + 1)
                weight_last(t, par)

            mag2(0)
            mag2_products(0, 0)
            mag2_products(0, 1)
            newton(0)
            body(0, 0, first=True)
            with pool.Fori(0, (TILES - 2) // ZBUF) as i:
                for k in range(1, ZBUF + 1):
                    body(ZBUF * i + k, k % ZBUF)
            body(TILES - 1, (TILES - 1) % ZBUF, last=True)
            negate(TILES - 1)
            pool.wait_ge(s_gbe, 16 * 2)
            for t in range(TILES):
                pool.wait_ge(s_yg, t + 1)
                nc.gpsimd.tensor_tensor(y[:, t], y[:, t], post_be, ALU.add).then_inc(s_yb, 1)

        @block.tensor
        def _(pe):
            pe.wait_ge(s_w, 16 * 3)
            for j, (w, m) in enumerate(TJ):
                ps = banks[j % NB]
                at_least(pe, s_tlo, j - NB + 1)
                for k in range(KD):
                    mm = nc.tensor.transpose(ps[:, k * P:(k + 1) * P], w_rows[w][:, m, k * P:(k + 1) * P], const.ident[:])
                mm.then_inc(s_tf, 1)
            pe.wait_ge(s_tlo, len(TJ))

            def superpose(t):
                pe.wait_ge(s_gz, t + 1)
                pe.wait_ge(s_gz3, t + 1)
                for ri in range(RI):
                    for k in range(KD):
                        for n in range(N):
                            mm = nc.tensor.matmul(banks[B_SUP + ri][:, k * P:(k + 1) * P], gz[:, n, ri, k * P:(k + 1) * P],
                                                  const.ident[:], start=n == 0, stop=n == N - 1)
                    mm.then_inc(s_sf, 1)
                pe.wait_ge(s_shi, RI * (t + 1))
                at_least(pe, s_n, t)
                for ri in range(RI):
                    for k in range(KD):
                        mm = nc.tensor.matmul(banks[B_N][:, 0:1], squares[:, ri, k * P:(k + 1) * P], ones[:],
                                              start=ri == 0 and k == 0, stop=ri == 1 and k == KD - 1)
                mm.then_inc(s_nf, 1)

            def last_layer(t):
                pe.wait_ge(s_plo, t + 1)
                at_least(pe, s_y, t)
                for k in range(KD):
                    mm = three(nc, banks[B_Y][:], [a[:, k] for a in ampT], [w[:, k] for w in pT], k == 0, k == KD - 1)
                mm.then_inc(s_yf, 1)

            def measure(t):
                pe.wait_ge(s_slo, RI * (t + 1))
                for o, terms in enumerate((((0, 1), (1, 0)), ((0, 0), (2, 1)))):
                    for i, (s, m) in enumerate(terms):
                        if s == 2:
                            pe.wait_ge(s_sneg, t + 1)
                        for k in range(KD):
                            mm = three(nc, banks[B_M + o][:], [v[:, s, k] for v in supT], [v[:, m, k] for v in mT],
                                       i == 0 and k == 0, i == 1 and k == KD - 1)
                    mm.then_inc(s_mf, 1)
                pe.wait_ge(s_amp, t + 1)
                for k in range(KD):
                    mm = nc.tensor.transpose(banks[B_AMP][:, k * P:(k + 1) * P], amp[:, k * P:(k + 1) * P], const.ident[:])
                mm.then_inc(s_pf, 1)

            superpose(0)
            measure(0)
            with pe.Fori(1, TILES) as t:
                superpose(t)
                last_layer(t - 1)
                measure(t)
            last_layer(TILES - 1)

        @block.scalar
        def _(act):
            def z_squares(t, par, nth):
                act.wait_ge(s_zin[par], 16 * nth)
                at_least(act, s_mm, len(SHIFTS) * t)
                at_least(act, s_gz, t - 1)
                at_least(act, s_gz3, t - 1)
                for h in range(2):
                    s = slice(2 * h, 2 * h + 2)
                    nc.scalar.activation(sq[:, s], z[:, par, s], ACT.Square).then_inc(s_sq, 1)

            def roots(t, h):
                act.wait_ge(s_mm, len(SHIFTS) * t + (1, 3)[h])
                s = HALVES[h]
                nc.scalar.activation(root[:, s], root[:, s], ACT.Sqrt, bias=tiny2[:]).then_inc(s_root, 1)

            def seeds(t):
                for h, s in enumerate(HALVES):
                    act.wait_ge(s_root, 2 * t + h + 1)
                    at_least(act, s_inv, 2 * t + h - 1)
                    nc.scalar.activation(seed[:, s], root[:, s], ACT.Ln).then_inc(s_ln, 1)
                for h, s in enumerate(HALVES):
                    act.wait_ge(s_ln, 2 * t + h + 1)
                    nc.scalar.activation(seed[:, s], seed[:, s], ACT.Exp, scale=-1.0).then_inc(s_seed, 1)

            def begin_gains(t, last):
                act.wait_ge(s_m2, 2 * t + (2 if last else 4))
                for j in (0, 1, 2, 3):
                    i = (j + 1) % N
                    act.wait_ge(s_cos, 2 * t + (1 if j < N - 1 else 2))
                    nc.scalar.activation(gain[:, j], x[:, of(i, j)], ACT.Identity, bias=cur(st, t, j, j),
                                         scale=cur(st_neg, t, i, j)).then_inc(s_g0, 1)

            def cur(s, t, i, j):
                return s[:, bass.ds(t, 1), i, j]

            def supT_hi(t):
                at_least(act, s_pf, t)
                for ri in range(RI):
                    act.wait_ge(s_sf, RI * t + ri + 1)
                    bank = banks[B_SUP + ri][:]
                    nc.scalar.activation(supT[0][:, ri].rearrange("p k f -> p (k f)"), bank, ACT.Identity)
                    if ri == 1:
                        nc.scalar.activation(supT[0][:, 2].rearrange("p k f -> p (k f)"), bank, ACT.Identity, scale=-1.0)
                    nc.scalar.activation(squares[:, ri], bank, ACT.Square).then_inc(s_shi, 1)

            def amplitude(t):
                for o in range(2):
                    act.wait_ge(s_mf, 2 * t + o + 1)
                    nc.scalar.activation(squares[:, o], banks[B_M + o][:], ACT.Square).then_inc(s_a2, 1)
                act.wait_ge(s_asum, t + 1)
                nc.scalar.activation(amp, amp, ACT.Sqrt).then_inc(s_amp, 1)

            def norm(t):
                at_least(act, s_rn, t)
                act.wait_ge(s_nf, t + 1)
                nc.scalar.activation(nrm[:], banks[B_N][:, 0:1], ACT.Sqrt, bias=const.eps[:]).then_inc(s_n, 1)

            def ampT_hi(t):
                act.wait_ge(s_pf, t + 1)
                nc.scalar.activation(ampT[0][:].rearrange("p k f -> p (k f)"), banks[B_AMP][:], ACT.Identity).then_inc(s_phi, 1)

            def body(t, par, nth, first=False, last=False):
                if not last:
                    z_squares(t + 1, (par + 1) % ZBUF, nth + (par == ZBUF - 1))
                if not first:
                    supT_hi(t - 1)
                if first:
                    begin_gains(t, last)
                if not last:
                    roots(t + 1, 0)
                    roots(t + 1, 1)
                    seeds(t + 1)
                if not first:
                    begin_gains(t, last)
                if not first:
                    norm(t - 1)
                    amplitude(t - 1)
                    ampT_hi(t - 1)

            def turns():
                for j, (w, m) in enumerate(TJ):
                    act.wait_ge(s_tf, j + 1)
                    nc.scalar.activation(w_dst[w][0][:, :, m * P:(m + 1) * P],
                                         banks[j % NB][:].rearrange("p (k f) -> p k f", k=KD), ACT.Identity).then_inc(s_thi, 1)

            z_squares(0, 0, 1)
            turns()
            act.wait_ge(s_eps, 3)
            roots(0, 0)
            roots(0, 1)
            seeds(0)
            act.wait_ge(s_st, 16)
            act.wait_ge(s_neg_st, 1)
            body(0, 0, 1, first=True)
            with act.Fori(0, (TILES - 2) // ZBUF) as i:
                for k in range(1, ZBUF + 1):
                    body(ZBUF * i + k, k % ZBUF, i + 1 + k // ZBUF)
            body(TILES - 1, (TILES - 1) % ZBUF, (TILES - 1) // ZBUF + 1, last=True)
            supT_hi(TILES - 1)
            norm(TILES - 1)
            amplitude(TILES - 1)
            ampT_hi(TILES - 1)
            act.wait_ge(s_var, TILES)
            nc.scalar.activation(std[:], mv[:, :, 1], ACT.Sqrt, bias=eps_ln[:]).then_inc(s_std, 1)
            for t in range(TILES):
                act.wait_ge(s_yb, t + 1)
                nc.scalar.activation(y[:, t], y[:, t], ACT.Gelu).then_inc(s_gelu, 1)

        @block.vector
        def _(dve):
            nc.vector.memset(eps_ln[:], EPS_LN).then_inc(s_eps, 1)
            nc.vector.memset(tiny2[:], TINY * TINY).then_inc(s_eps, 1)
            nc.vector.memset(ones[:], 1.0).then_inc(s_eps, 1)
            for j, (w, m) in enumerate(TJ):
                dve.wait_ge(s_thi, j + 1)
                cols = slice(m * P, (m + 1) * P)
                nc.vector.tensor_tensor(w_dst[w][1][:, :, cols], banks[j % NB][:].rearrange("p (k f) -> p k f", k=KD),
                                        f32(w_dst[w][0][:, :, cols]), ALU.subtract).then_inc(s_tlo, 1)
            dve.wait_ge(s_st, 16)
            nc.vector.tensor_scalar(st_neg[:], st[:], -1.0, None, ALU.mult).then_inc(s_neg_st, 1)
            dve.wait_ge(s_vec, 16)
            dve.wait_ge(s_neg_st, 1)

            def real_products(t, par, nth):
                zt = z[:, par]
                dve.wait_ge(s_zin[par], 16 * nth)
                for d, p0, n in SHIFTS:
                    nc.vector.tensor_tensor(x[:, p0:p0 + n], zt[:, 0:n, 0], zt[:, d:d + n, 0], ALU.mult).then_inc(s_re, 1)

            def dots(t, par):
                zt = z[:, par]
                at_least(dve, s_sf, RI * t)
                for d, p0, n in SHIFTS:
                    nc.vector.tensor_tensor(im[:, p0:p0 + n], zt[:, 0:n, 1], zt[:, d:d + n, 1], ALU.mult).then_inc(s_im, 1)
                dve.wait_ge(s_re, len(SHIFTS) * (t + 1))
                dve.wait_ge(s_im, len(SHIFTS) * (t + 1))
                nc.vector.scalar_tensor_tensor(out=x[:], in0=x[:], scalar=TINY, in1=im, op0=ALU.add,
                                               op1=ALU.add).then_inc(s_x, 1)

            def inverses(t):
                for h, s in enumerate(HALVES):
                    dve.wait_ge(s_newt, 2 * t + h + 1)
                    nc.vector.scalar_tensor_tensor(out=inv[:, s], in0=root[:, s], scalar=2.0, in1=seed[:, s],
                                                   op0=ALU.subtract, op1=ALU.mult).then_inc(s_inv, 1)

            def cosines(t):
                dve.wait_ge(s_x, t + 1)
                dve.wait_ge(s_inv, 2 * t + 2)
                for h, s in enumerate(HALVES):
                    nc.vector.tensor_tensor(x[:, s], x[:, s], inv[:, s], ALU.mult).then_inc(s_cos, 1)

            def gains(t):
                dve.wait_ge(s_cos, 2 * (t + 1))
                for k in range(2, N):
                    for j in range(N):
                        i = (j + k) % N
                        if k == 2:
                            dve.wait_ge(s_g0, N * t + j + 1)
                        nc.vector.scalar_tensor_tensor(out=gain[:, j], in0=x[:, of(i, j)], scalar=st_neg[:, bass.ds(t, 1), i, j],
                                                       in1=gain[:, j], op0=ALU.mult, op1=ALU.add).then_inc(s_g, 1)
                    dve.wait_ge(s_g, (N - 2) * N * t + (k - 1) * N)

            def weight(t, par):
                m = N - 1
                nc.vector.tensor_tensor(gz[:, 0:m], z[:, par, 0:m], gain[:, 0:m].unsqueeze(2).to_broadcast([P, m, RI, D]),
                                        ALU.mult).then_inc(s_gz, 1)

            def supT_lo(t):
                at_least(dve, s_mf, 2 * t)
                for ri in range(RI):
                    dve.wait_ge(s_shi, RI * t + ri + 1)
                    nc.vector.tensor_tensor(supT[1][:, ri].rearrange("p k f -> p (k f)"), banks[B_SUP + ri][:],
                                            f32(supT[0][:, ri]).rearrange("p k f -> p (k f)"), ALU.subtract).then_inc(s_slo, 1)

            def ampT_lo(t):
                dve.wait_ge(s_phi, t + 1)
                nc.vector.tensor_tensor(ampT[1][:].rearrange("p k f -> p (k f)"), banks[B_AMP][:],
                                        f32(ampT[0][:]).rearrange("p k f -> p (k f)"), ALU.subtract).then_inc(s_plo, 1)

            def norm(t):
                dve.wait_ge(s_n, t + 1)
                nc.vector.reciprocal(rn[:], nrm[:]).then_inc(s_rn, 1)

            def layer(t, yt=y_row[:]):
                at_least(dve, s_ystored, 16 * t)
                dve.wait_ge(s_rn, t + 1)
                dve.wait_ge(s_yf, t + 1)
                nc.vector.scalar_tensor_tensor(out=yt, in0=banks[B_Y][:], scalar=rn[:], in1=post_b[:],
                                               op0=ALU.mult, op1=ALU.add).then_inc(s_y, 1)
                wait_apart(dve, s_y, t + 1)
                nc.vector.bn_stats(stats[:, bass.ds(t, 1)].rearrange("p a f -> p (a f)"), yt).then_inc(s_yst, 1)

            def amp_sum(t):
                dve.wait_ge(s_a2, 2 * (t + 1))
                nc.vector.tensor_tensor(amp, amp, squares[:, 1], ALU.add).then_inc(s_asum, 1)

            def body(t, par, nth, before=2):
                if before:
                    inverses(t)
                real_products(t, par, nth)
                if before > 1:
                    ampT_lo(t - 2)
                if before:
                    supT_lo(t - 1)
                dots(t, par)
                if not before:
                    inverses(t)
                cosines(t)
                if before > 1:
                    layer(t - 2)
                gains(t)
                if before:
                    norm(t - 1)
                    amp_sum(t - 1)
                weight(t, par)

            body(0, 0, 1, before=0)
            body(1, 1, 1, before=1)
            with dve.Fori(0, (TILES - 2) // ZBUF) as i:
                for k in range(2, ZBUF + 2):
                    body(ZBUF * i + k, k % ZBUF, i + 1 + k // ZBUF)
            ampT_lo(TILES - 2)
            supT_lo(TILES - 1)
            layer(TILES - 2)
            norm(TILES - 1)
            amp_sum(TILES - 1)
            ampT_lo(TILES - 1)
            layer(TILES - 1, y[:, TILES - 1])
            dve.wait_ge(s_yst, TILES)
            for t in range(TILES):
                nc.vector.bn_aggr(mv[:, t], stats[:, t]).then_inc(s_var, 1)
            dve.wait_ge(s_std, 1)
            nc.vector.reciprocal(rstd[:], std[:]).then_inc(s_rstd, 1)
            dve.wait_ge(s_rstd, 1)
            dve.wait_ge(s_gbe, 16 * 2)
            dve.wait_ge(s_yin, 16)
            for t in range(TILES):
                nc.vector.tensor_scalar(y[:, t], y[:, t], mv[:, t, 0:1], rstd[:, t:t + 1], ALU.subtract,
                                        ALU.mult).then_inc(s_yn, 1)
                dve.wait_ge(s_yn, t + 1)
                nc.vector.tensor_tensor(y[:, t], y[:, t], post_g, ALU.mult).then_inc(s_yg, 1)


def program(nc, t, out):
    w = lambda name: t["L0_rec_" + name]
    sides = ("r", "i")
    folded = nc.dram_tensor("folded_weights", (KD, P, RI, N * KH, FOLD), F32, kind="Internal").ap()
    attended = nc.dram_tensor("attended", (KD * NQ + 1, P, HC, N, TQ), F32, kind="Internal").ap()
    y_rows = nc.dram_tensor("y_rows_of_tiles", (TILES - 1, P, OUT), F32, kind="Internal").ap()
    states = nc.dram_tensor("states", (N, B, RI, D), F32, kind="Internal").ap()
    bias_rows = [w(f"e{s}_b2") for s in sides] + [w(f"b{p}_{s}") for s in sides for p in "qkv"] + [w(f"bo_{s}") for s in sides]
    n_bias = sum(v.shape[0] for v in bias_rows) // P
    with ExitStack() as ctx:
        E = ctx.enter_context

        class const:
            ident = E(nc.sbuf_tensor("identity", [P, P], F32))
            mask = E(nc.sbuf_tensor("same_token", [P, 32], F32))
            eps = E(nc.sbuf_tensor("eps", [P, 1], F32))
            zero = E(nc.sbuf_tensor("zero", [P, 1], F32))
            scratch = E(nc.sbuf_tensor("scratch", [P, 8], F32))

        banks = [E(nc.psum_tensor(f"bank_{i}", [P, BANK], F32)) for i in range(NB)]
        biasT = E(nc.sbuf_tensor("biasT", [P, n_bias], F32))
        bias_cols = E(nc.sbuf_tensor("bias_cols", [P, KD, RI * NP, N], F32))
        with ExitStack() as attention:
            hT = [attention.enter_context(nc.sbuf_tensor(f"hT_{s}", [P, RI, KH, B], F32R)) for s in ("hi", "lo")]
            with ExitStack() as folding:
                w2 = [folding.enter_context(nc.sbuf_tensor(f"w2_{s}", [P, RI, N * KD, HID], F32R)) for s in ("hi", "lo")]
                both = lambda name: [w(f"e{s}_{name}") for s in sides]
                stage_encode(nc, const, hT, w2, banks, t["r_x"], both("W1"), both("b1"), both("g1"), both("be1"),
                             both("W2"), bias_rows, biasT)
                stage_fold(nc, const, w2, banks, [[w(f"W{p}_{s}") for p in "qkv"] for s in sides], biasT, bias_cols, folded)
            stage_attend(nc, const, hT, banks, bias_cols, folded, attended)
        bo_cols = biasT[:, n_bias - RI * KD:n_bias].rearrange("p (r m) -> p r m", r=RI)
        stage_interact(nc, const, banks, [w(f"Wo_{s}") for s in sides], w("int_Wr"), w("int_Wi"), bo_cols, attended, states)
        stage_measure(nc, const, banks, t["r_strength"], w("meas_Mr"), w("meas_Mi"), w("post_W"),
                      [w("post_b"), w("post_g"), w("post_be")], states, y_rows, out)


_INS = ["r_strength", "r_x"] + ["L0_rec_" + n for n in (
    "er_W1", "er_b1", "er_g1", "er_be1", "er_W2", "er_b2", "ei_W1", "ei_b1", "ei_g1", "ei_be1", "ei_W2", "ei_b2",
    "Wq_r", "bq_r", "Wq_i", "bq_i", "Wk_r", "bk_r", "Wk_i", "bk_i", "Wv_r", "bv_r", "Wv_i", "bv_i",
    "Wo_r", "bo_r", "Wo_i", "bo_i", "int_Wr", "int_Wi", "meas_Mr", "meas_Mi", "post_W", "post_b", "post_g", "post_be")]


def kernel(**inputs):
    import numpy as np
    import concourse.bacc as bacc
    from concourse.bass_utils import run_bass_kernel_spmd

    nc = bacc.Bacc("TRN2", target_bir_lowering=False, num_devices=1)
    arrays = {f"in_{n}": np.ascontiguousarray(inputs[n]) for n in _INS}
    tensors = {n: nc.dram_tensor(f"in_{n}", arrays[f"in_{n}"].shape, F32, kind="ExternalInput").ap() for n in _INS}
    out = nc.dram_tensor("out", (B, OUT), F32, kind="ExternalOutput").ap()
    program(nc, tensors, out)
    return run_bass_kernel_spmd(nc, [arrays], core_ids=[0]).results[0]["out"]
```

```python
from contextlib import ExitStack

import concourse.bass as bass
from concourse import mybir

P = 128
BANK = 512
NB = 8

F32 = mybir.dt.float32
F32R = mybir.dt.float32r
ACT = mybir.ActivationFunctionType
ALU = mybir.AluOpType
AX_X = mybir.AxisListType.X

B, IN, HID, D, N, OUT, H = 1024, 256, 256, 512, 4, 512, 8
HD = D // H
TILES = B // P
KI = IN // P
KH = HID // P
KD = D // P
HC = P // HD
TQ = 256
NQ = B // TQ
G = TQ // 32
GH = G * HC
EPS_LN = 1e-5
EPS = 1e-8
RI = 2
NP = 3
FOLD = NP * P


class Ring:

    def __init__(self, readers):
        self.readers = readers
        self.per = {r: readers.count(r) for r in set(readers)}

    def nth(self, j):
        return self.readers[:j].count(self.readers[j])

    def bank(self, j):
        return j % NB

    def filled(self, j, it):
        return it * len(self.readers) + j + 1

    def before(self, j, it):
        if j >= NB:
            r = self.readers[j - NB]
            return r, it * self.per[r] + self.nth(j - NB) + 1 + self.per[r]
        last = max(k for k in range(len(self.readers)) if k % NB == j)
        r = self.readers[last]
        return r, it * self.per[r] + self.nth(last) + 1


def three(nc, out, lhs, rhs, first, last):
    (lh, ll), (rh, rl) = lhs, rhs
    nc.tensor.matmul(out, lh, rh, start=first, stop=False)
    nc.tensor.matmul(out, lh, rl, start=False, stop=False)
    return nc.tensor.matmul(out, ll, rh, start=False, stop=last)


def wait_apart(eng, sem, count):
    eng.wait_ge(sem, 1)
    eng.wait_ge(sem, count)


def at_least(eng, sem, count):
    if not isinstance(count, int) or count > 0:
        eng.wait_ge(sem, count)


def f32(ap):
    return ap.bitcast(F32)


class Carry:
    SLOTS = 4

    def __init__(self, nc, E):
        self.buf = E(nc.sbuf_tensor("carry", [P, N * RI * D], F32))
        self.fold_in = self.buf[:, 0:self.SLOTS * KH * FOLD].rearrange("p (s f) -> p s f", s=self.SLOTS)
        self.s_in = [E(nc.semaphore(f"fold_in_{i}")) for i in range(self.SLOTS)]
        self.s_wo = E(nc.semaphore("wo_in"))
        self.s_z0 = E(nc.semaphore("z_in_ready_0"))
        self.wo_rows = self.buf[:].rearrange("p (r m d) -> p r m d", r=RI, m=KD)
        self.z0 = self.buf[:].rearrange("p (n r d) -> p n r d", n=N, r=RI)

    def load_folded(self, sp, c_dram, c, i):
        ri, n = i // N, i % N
        sp.dma_start(self.fold_in[:, i % self.SLOTS], c_dram[bass.ds(c, 1), :, ri, KH * n:KH * n + KH, :]
                     .rearrange("a p k f -> (a p) (k f)")).then_inc(self.s_in[i % self.SLOTS], 16)


class Encoded:

    def __init__(self, nc, E):
        sb = lambda name, shape, dt=F32: E(nc.sbuf_tensor(name, shape, dt))
        self.h = sb("h_rows", [P, TILES, RI, HID])
        self.w2_rows = sb("w2_rows", [P, RI, N * KD, HID])
        self.w2 = [sb(f"w2_{s}", [P, RI, N * KD, HID], F32R) for s in ("hi", "lo")]
        self.g1 = sb("g1_bcast", [P, RI, HID])
        self.be1 = sb("be1_bcast", [P, RI, HID])
        self.mv = sb("ln_mean_var", [P, TILES * RI, 2])
        self.eps = sb("eps_ln", [P, 1])
        self.proj_rows = sb("proj_rows", [P, RI, NP, D])
        self.s_w2 = [E(nc.semaphore(f"w2_in_{ri}")) for ri in range(RI)]
        self.s_vec = E(nc.semaphore("ln_scale_shift_in"))
        self.s_rows = [E(nc.semaphore(f"proj_rows_in_{ri}")) for ri in range(RI)]


def stage_encode(nc, const, carry, enc, banks, x, w1, b1, g1, be1, W2, proj, bias_rows, biasT):
    with ExitStack() as ctx:
        E = ctx.enter_context
        sb = lambda name, shape, dt=F32: E(nc.sbuf_tensor(name, shape, dt))
        sem = lambda name: E(nc.semaphore(name))
        x_rows = carry.buf[:, 0:TILES * IN].rearrange("p (t f) -> p t f", t=TILES)
        xT = [sb(f"xT_{s}", [P, KI, B], F32R) for s in ("hi", "lo")]
        w1_rows = carry.buf[:, TILES * IN:TILES * IN + RI * KH * IN].rearrange("p (r k f) -> p r k f", r=RI, k=KH)
        w1T = [sb(f"w1T_{s}", [P, KI, RI, HID], F32R) for s in ("hi", "lo")]
        h, mv = enc.h, enc.mv
        b1b = sb("b1_bcast", [P, RI, HID])
        brows = sb("bias_rows", [P, P])
        stats = sb("ln_stats", [P, TILES * RI, 6])

        s_x, s_w1, s_brow, s_b1 = (sem(n) for n in ("x_in", "w1_in", "bias_rows_in", "b1_in"))
        s_id0, s_id, s_mask = sem("identity_zeroed"), sem("identity_ready"), sem("mask_ready")
        filled = sem("a_filled")
        freed = {"act": sem("a_freed_act"), "dve": sem("a_freed_dve")}
        s_hi = sem("a_hi_ready")
        s_w2hi = sem("w2_hi_ready")
        s_step = sem("a_dve_step")

        XJ = [(k, q) for k in range(KI) for q in range(TILES // 4)]
        n_x, n_w1 = len(XJ), RI
        first_h = n_x + n_w1 + 1
        ring = Ring(["dve"] * (first_h + TILES))

        block = E(nc.Block())

        @block.sync
        def _(sp):
            sp.dma_start(x_rows, x.rearrange("(t p) f -> p t f", p=P)).then_inc(s_x, 16)
            for ri in range(RI):
                sp.dma_start(w1_rows[:, ri], w1[ri].rearrange("(k p) f -> p k f", p=P)).then_inc(s_w1, 16)
            row = 0
            for v in bias_rows:
                n = v.shape[0] // P
                sp.dma_start(brows[row:row + n, :], v.rearrange("(r p) -> r p", p=P)).then_inc(s_brow, 16)
                row += n
            for ri in range(RI):
                sp.dma_start(b1b[:, ri], b1[ri].partition_broadcast(P)).then_inc(s_b1, 16)
            for ri in range(RI):
                sp.dma_start(enc.w2_rows[:, ri], W2[ri].rearrange("(k p) f -> p k f", p=P)).then_inc(enc.s_w2[ri], 16)
                for i in range(NP):
                    sp.dma_start(enc.proj_rows[:, ri, i, :], proj[ri][i][0:P, :]).then_inc(enc.s_rows[ri], 16)
            for t, v in ((enc.g1, g1), (enc.be1, be1)):
                for ri in range(RI):
                    sp.dma_start(t[:, ri], v[ri].partition_broadcast(P)).then_inc(enc.s_vec, 16)

        @block.gpsimd
        def _(pool):
            nc.gpsimd.memset(const.ident[:], 0.0).then_inc(s_id0, 1)
            pool.wait_ge(s_id0, 1)
            nc.gpsimd.affine_select(out=const.ident[:], in_=const.ident[:], compare_op=ALU.not_equal, fill=1.0,
                                    base=0, pattern=[[-1, P]], channel_multiplier=1).then_inc(s_id, 1)
            pool.wait_ge(s_w2hi, 1)
            nc.gpsimd.tensor_tensor(enc.w2[1][:, 0], enc.w2_rows[:, 0], f32(enc.w2[0][:, 0]), ALU.subtract)

        @block.tensor
        def _(pe):
            def take(j):
                if j >= NB:
                    pe.wait_ge(freed["dve"], j - NB + 1)
                return banks[ring.bank(j)]

            pe.wait_ge(s_id, 1)
            pe.wait_ge(s_x, 16)
            for j, (k, q) in enumerate(XJ):
                ps = take(j)
                for t in range(4):
                    mm = nc.tensor.transpose(ps[:, t * P:(t + 1) * P], x_rows[:, 4 * q + t, k * P:(k + 1) * P],
                                             const.ident[:])
                mm.then_inc(filled, 1)
            pe.wait_ge(s_w1, 16 * RI)
            for ri in range(RI):
                ps = take(n_x + ri)
                for k in range(KI):
                    for m in range(KH):
                        mm = nc.tensor.transpose(ps[:, (k * KH + m) * P:(k * KH + m + 1) * P],
                                                 w1_rows[:, ri, m, k * P:(k + 1) * P], const.ident[:])
                mm.then_inc(filled, 1)
            pe.wait_ge(s_brow, 16 * len(bias_rows))
            ps = take(n_x + n_w1)
            nrow = biasT.shape[1]
            nc.tensor.transpose(ps[:, 0:nrow], brows[0:nrow, :], const.ident[0:nrow, 0:nrow]).then_inc(filled, 1)
            pe.wait_ge(freed["dve"], n_x + n_w1)
            for t in range(TILES):
                ps = take(first_h + t)
                for k in range(KI):
                    mm = three(nc, ps[:], [v[:, k, t * P:(t + 1) * P] for v in xT],
                               [v[:, k].rearrange("p r f -> p (r f)") for v in w1T], k == 0, k == KI - 1)
                mm.then_inc(filled, 1)

        @block.scalar
        def _(act):
            for j, (k, q) in enumerate(XJ):
                act.wait_ge(filled, j + 1)
                nc.scalar.activation(xT[0][:, k, q * BANK:(q + 1) * BANK], banks[ring.bank(j)][:],
                                     ACT.Identity).then_inc(s_hi, 1)
            for ri in range(RI):
                act.wait_ge(filled, n_x + ri + 1)
                nc.scalar.activation(w1T[0][:, :, ri, :],
                                     banks[ring.bank(n_x + ri)][:].rearrange("p (k f) -> p k f", k=KI),
                                     ACT.Identity).then_inc(s_hi, 1)
            act.wait_ge(enc.s_w2[0], 16)
            nc.scalar.activation(enc.w2[0][:, 0], enc.w2_rows[:, 0], ACT.Identity).then_inc(s_w2hi, 1)

        @block.vector
        def _(dve):
            steps = [0]

            def link(ins):
                steps[0] += 1
                ins.then_inc(s_step, 1)
                dve.wait_ge(s_step, steps[0])

            nc.vector.memset(enc.eps[:], EPS_LN)
            nc.vector.memset(const.zero[:], 0.0)
            nc.vector.memset(const.eps[:], EPS)
            for j, (k, q) in enumerate(XJ):
                dve.wait_ge(s_hi, j + 1)
                cols = slice(q * BANK, (q + 1) * BANK)
                nc.vector.tensor_tensor(xT[1][:, k, cols], banks[ring.bank(j)][:], f32(xT[0][:, k, cols]),
                                        ALU.subtract).then_inc(freed["dve"], 1)
            for ri in range(RI):
                dve.wait_ge(s_hi, n_x + ri + 1)
                nc.vector.tensor_tensor(w1T[1][:, :, ri, :],
                                        banks[ring.bank(n_x + ri)][:].rearrange("p (k f) -> p k f", k=KI),
                                        f32(w1T[0][:, :, ri, :]), ALU.subtract).then_inc(freed["dve"], 1)
            dve.wait_ge(filled, n_x + n_w1 + 1)
            nc.vector.tensor_copy(biasT[:], banks[ring.bank(n_x + n_w1)][:, 0:biasT.shape[1]]).then_inc(freed["dve"], 1)
            dve.wait_ge(s_id, 1)
            nc.vector.tensor_reduce(const.mask[:], const.ident[:].rearrange("p (n t) -> p t n", t=32), AX_X, ALU.add)
            dve.wait_ge(s_b1, 16 * RI)
            for t in range(TILES):
                dve.wait_ge(filled, first_h + t + 1)
                link(nc.vector.tensor_tensor(h[:, t].rearrange("p r f -> p (r f)"), banks[ring.bank(first_h + t)][:],
                                             b1b[:].rearrange("p r f -> p (r f)"), ALU.add))
                nc.vector.bn_stats(stats[:, RI * t, :], h[:, t, 0]).then_inc(freed["dve"], 1)
                link(nc.vector.bn_stats(stats[:, RI * t + 1, :], h[:, t, 1]))
                nc.vector.bn_aggr(mv[:, RI * t, :], stats[:, RI * t, :])
                nc.vector.bn_aggr(mv[:, RI * t + 1, :], stats[:, RI * t + 1, :])


def stage_fold(nc, const, carry, enc, hT, banks, proj, biasT, bias_cols, c_dram):
    with ExitStack() as ctx:
        E = ctx.enter_context
        sb = lambda name, shape, dt=F32: E(nc.sbuf_tensor(name, shape, dt))
        sem = lambda name: E(nc.semaphore(name))
        rows, s_rows, w2, h, mv = enc.proj_rows, enc.s_rows, enc.w2, enc.h, enc.mv
        after = carry.SLOTS * KH * FOLD
        std = carry.buf[:, after:after + TILES * RI]
        rstd = carry.buf[:, after + TILES * RI:after + 2 * TILES * RI]
        wT = [sb(f"projT_{s}", [P, RI, KD, FOLD], F32R) for s in ("hi", "lo")]
        b2T = [sb(f"b2T_{s}", [P, RI * N * KD], F32R) for s in ("hi", "lo")]
        b2_rows = enc.w2_rows[0:N, 0].rearrange("n a f -> n (a f)")[:, 0:KD * RI * FOLD].rearrange(
            "n (c r f) -> n c r f", c=KD, r=RI)
        STAGES = 2
        stage = sb("fold_out", [P, STAGES, KH, FOLD])

        s_w2hi, s_w2lo = sem("w2_imag_hi"), sem("w2_imag_lo")
        s_std, s_rstd, s_norm, s_scaled, s_ln, s_h = (sem(n) for n in (
            "ln_std_ready", "ln_rstd_ready", "h_normed", "h_scaled", "ln_rows_ready", "h_rows_ready"))
        s_hf, s_hhi, s_hlo = sem("hT_filled"), sem("hT_hi"), sem("hT_lo")
        s_stored = [sem(f"folded_stored_{i}") for i in range(STAGES)]
        s_tf, s_thi, s_tlo = sem("proj_turn_filled"), sem("proj_hi"), sem("proj_lo")
        s_ff, s_fout = sem("fold_filled"), sem("fold_out_ready")
        s_b2hi, s_b2 = sem("b2_hi_ready"), sem("b2_split")
        s_bf, s_brow, s_bT = sem("folded_bias_filled"), sem("folded_bias_rows_ready"), sem("folded_bias_turned")

        HJ = [(ri, k, q) for ri in range(RI) for k in range(KH) for q in range(TILES // 4)]
        FJ = [(n, kh) for n in range(N) for kh in range(KH)]
        n_f = len(FJ)
        TB, BB, FB, NFB = 0, 3, 4, 4
        turns_before = lambda ri, c: (2 * c + ri) * NP
        folds_before = lambda ri, c: (2 * c + ri) * n_f

        block = E(nc.Block())

        @block.sync
        def _(sp):
            def load(ri, c):
                wait_apart(sp, s_tf, turns_before(ri, c) - (RI - 1) * NP)
                for i in range(NP):
                    sp.dma_start(rows[:, ri, i, :], proj[ri][i][bass.ds(c * P, P), :]).then_inc(s_rows[ri], 16)

            def stores(ri, c):
                for n in range(N):
                    wait_apart(sp, s_fout, NFB + folds_before(ri, c) + (n + 1) * KH)
                    sp.dma_start(c_dram[bass.ds(c, 1), :, ri, n * KH:(n + 1) * KH].rearrange("a p k f -> (a p) (k f)"),
                                 stage[:, n % STAGES].rearrange("p k f -> p (k f)")).then_inc(s_stored[n % STAGES], 16)

            with sp.Fori(0, KD - 1) as c:
                load(0, c + 1)
                stores(0, c)
                load(1, c + 1)
                stores(1, c)
            for i in range(STAGES):
                sp.wait_ge(s_stored[i], 16 * (RI * N // STAGES + 1))
            for i in range(carry.SLOTS):
                carry.load_folded(sp, c_dram, 0, i)
            stores(0, KD - 1)
            stores(1, KD - 1)
            for s in s_stored:
                sp.wait_ge(s, 16 * (KD * RI * N // STAGES + 1))

        @block.gpsimd
        def _(pool):
            pool.wait_ge(s_w2hi, 1)
            nc.gpsimd.tensor_tensor(w2[1][:, 1], enc.w2_rows[:, 1], f32(w2[0][:, 1]), ALU.subtract).then_inc(s_w2lo, 1)
            pool.wait_ge(enc.s_vec, 16 * 2 * RI)
            for t in range(TILES):
                pool.wait_ge(s_scaled, t + 1)
                nc.gpsimd.tensor_tensor(h[:, t], h[:, t], enc.be1[:], ALU.add).then_inc(s_ln, 1)

        @block.tensor
        def _(pe):
            def turns(ri, c):
                pe.wait_ge(s_rows[ri], (c + 1) * 16 * NP)
                for i in range(NP):
                    at_least(pe, s_tlo, turns_before(ri, c) - NP + i + 1)
                    for k in range(KD):
                        mm = nc.tensor.transpose(banks[TB + i][:, k * P:(k + 1) * P], rows[:, ri, i, k * P:(k + 1) * P],
                                                 const.ident[:])
                    mm.then_inc(s_tf, 1)

            def folds(ri, c):
                pe.wait_ge(s_tlo, turns_before(ri, c) + NP)
                if ri == 1:
                    pe.wait_ge(s_w2lo, 1)
                for j, (n, kh) in enumerate(FJ):
                    pe.wait_ge(s_fout, folds_before(ri, c) + j + 1)
                    for k in range(KD):
                        mm = three(nc, banks[FB + j % NFB][:, 0:FOLD],
                                   [w[:, ri, n * KD + k, kh * P:(kh + 1) * P] for w in w2],
                                   [w[:, ri, k] for w in wT], k == 0, k == KD - 1)
                    mm.then_inc(s_ff, 1)
                at_least(pe, s_brow, 2 * c + ri)
                for k in range(KD):
                    cols = slice(ri * N * KD + k, (ri + 1) * N * KD, KD)
                    mm = three(nc, banks[BB][0:N, 0:FOLD], [b[:, cols] for b in b2T], [w[:, ri, k] for w in wT],
                               k == 0, k == KD - 1)
                mm.then_inc(s_bf, 1)

            turns(0, 0)
            pe.wait_ge(s_b2, 1)
            with pe.Fori(0, KD - 1) as c:
                turns(1, c)
                folds(0, c)
                turns(0, c + 1)
                folds(1, c)
            turns(1, KD - 1)
            folds(0, KD - 1)
            pe.wait_ge(s_h, TILES)
            for j, (ri, k, q) in enumerate(HJ):
                if j < NP:
                    pe.wait_ge(s_tlo, 2 * KD * NP)
                else:
                    pe.wait_ge(s_hlo, j - NP + 1)
                for t in range(4):
                    mm = nc.tensor.transpose(banks[TB + j % NP][:, t * P:(t + 1) * P],
                                             h[:, 4 * q + t, ri, k * P:(k + 1) * P], const.ident[:])
                mm.then_inc(s_hf, 1)
            folds(1, KD - 1)
            pe.wait_ge(s_hlo, len(HJ))
            pe.wait_ge(s_brow, RI * KD)
            for c in range(KD):
                for i in range(RI * NP):
                    ri, pr = i // NP, i % NP
                    mm = nc.tensor.transpose(banks[TB][:, (c * RI * NP + i) * N:(c * RI * NP + i + 1) * N],
                                             b2_rows[:, c, ri, pr * P:(pr + 1) * P], const.ident[0:N, 0:N])
            mm.then_inc(s_bT, 1)

        @block.scalar
        def _(act):
            nc.scalar.activation(b2T[0][:], biasT[:, 0:RI * N * KD], ACT.Identity).then_inc(s_b2hi, 1)
            nc.scalar.activation(const.scratch[:, 0:1], const.eps[:], ACT.Identity).then_inc(s_fout, NFB)

            def turns(ri, c):
                for i in range(NP):
                    act.wait_ge(s_tf, turns_before(ri, c) + i + 1)
                    if i == 0:
                        at_least(act, s_bf, 2 * c + ri - 1)
                    nc.scalar.activation(wT[0][:, ri, :, i * P:(i + 1) * P],
                                         banks[TB + i][:].rearrange("p (k f) -> p k f", k=KD), ACT.Identity).then_inc(s_thi, 1)

            def folds(ri, c):
                for j, (n, kh) in enumerate(FJ):
                    if kh == 0:
                        act.wait_ge(s_stored[n % STAGES], 16 * ((2 * c + ri) * N // STAGES + n // STAGES + 1))
                    act.wait_ge(s_ff, folds_before(ri, c) + j + 1)
                    nc.scalar.activation(stage[:, n % STAGES, kh, :], banks[FB + j % NFB][:, 0:FOLD],
                                         ACT.Identity).then_inc(s_fout, 1)
                act.wait_ge(s_bf, 2 * c + ri + 1)
                nc.scalar.activation(b2_rows[:, bass.ds(c, 1), ri].rearrange("n a f -> n (a f)"), banks[BB][0:N, 0:FOLD],
                                     ACT.Identity).then_inc(s_brow, 1)

            turns(0, 0)
            turns(1, 0)
            act.wait_ge(enc.s_w2[1], 16)
            nc.scalar.activation(w2[0][:, 1], enc.w2_rows[:, 1], ACT.Identity).then_inc(s_w2hi, 1)
            nc.scalar.activation(std, mv[:, :, 1], ACT.Sqrt, bias=enc.eps[:]).then_inc(s_std, 1)
            folds(0, 0)
            for t in range(TILES):
                act.wait_ge(s_ln, t + 1)
                nc.scalar.activation(h[:, t], h[:, t], ACT.Gelu).then_inc(s_h, 1)
            turns(0, 1)
            folds(1, 0)
            with act.Fori(1, KD - 1) as c:
                turns(1, c)
                folds(0, c)
                turns(0, c + 1)
                folds(1, c)
            turns(1, KD - 1)
            folds(0, KD - 1)
            for j, (ri, k, q) in enumerate(HJ):
                act.wait_ge(s_hf, j + 1)
                nc.scalar.activation(hT[0][:, ri, k, q * BANK:(q + 1) * BANK], banks[TB + j % NP][:],
                                     ACT.Identity).then_inc(s_hhi, 1)
            folds(1, KD - 1)

        @block.vector
        def _(dve):
            dve.wait_ge(s_b2hi, 1)
            nc.vector.tensor_tensor(b2T[1][:], biasT[:, 0:RI * N * KD], f32(b2T[0][:]), ALU.subtract).then_inc(s_b2, 1)
            for i in range(STAGES):
                nc.vector.memset(const.scratch[:, 2 + i:3 + i], 0.0).then_inc(s_stored[i], 16)

            def turns(ri, c):
                for i in range(NP):
                    dve.wait_ge(s_thi, turns_before(ri, c) + i + 1)
                    cols = slice(i * P, (i + 1) * P)
                    nc.vector.tensor_tensor(wT[1][:, ri, :, cols], banks[TB + i][:].rearrange("p (k f) -> p k f", k=KD),
                                            f32(wT[0][:, ri, :, cols]), ALU.subtract).then_inc(s_tlo, 1)

            turns(0, 0)
            turns(1, 0)
            dve.wait_ge(s_std, 1)
            nc.vector.reciprocal(rstd, std).then_inc(s_rstd, 1)
            dve.wait_ge(s_rstd, 1)
            dve.wait_ge(enc.s_vec, 16 * 2 * RI)
            for t in range(TILES):
                for ri in range(RI):
                    i = RI * t + ri
                    nc.vector.tensor_scalar(h[:, t, ri], h[:, t, ri], mv[:, i, 0:1], rstd[:, i:i + 1],
                                            ALU.subtract, ALU.mult).then_inc(s_norm, 1)
                dve.wait_ge(s_norm, RI * (t + 1))
                nc.vector.tensor_tensor(h[:, t], h[:, t], enc.g1[:], ALU.mult).then_inc(s_scaled, 1)
            turns(0, 1)
            with dve.Fori(1, KD - 1) as c:
                turns(1, c)
                turns(0, c + 1)
            turns(1, KD - 1)
            for j, (ri, k, q) in enumerate(HJ):
                dve.wait_ge(s_hhi, j + 1)
                cols = slice(q * BANK, (q + 1) * BANK)
                nc.vector.tensor_tensor(hT[1][:, ri, k, cols], banks[TB + j % NP][:], f32(hT[0][:, ri, k, cols]),
                                        ALU.subtract).then_inc(s_hlo, 1)
            dve.wait_ge(s_bT, 1)
            n_i = RI * NP
            own = biasT[:, RI * N * KD:RI * N * KD + n_i * KD].rearrange("p (i c) -> p i c", c=KD)
            for c in range(KD):
                nc.vector.tensor_tensor(bias_cols[:, c], banks[TB][:, c * n_i * N:(c + 1) * n_i * N]
                                        .rearrange("p (i n) -> p i n", n=N),
                                        own[:, :, c:c + 1].to_broadcast([P, n_i, N]), ALU.add)


def stage_attend(nc, const, carry, hT, banks, bias_cols, c_dram, o_dram, wo):
    with ExitStack() as ctx:
        E = ctx.enter_context
        sb = lambda name, shape, dt=F32: E(nc.sbuf_tensor(name, shape, dt))
        pair = lambda name, shape: [sb(f"{name}_{s}", shape, F32R) for s in ("hi", "lo")]
        sem = lambda name: E(nc.semaphore(name))
        SLOTS, fold_in, s_in = carry.SLOTS, carry.fold_in, carry.s_in
        KI_, KR_, NKI_ = 0, 1, 2
        fold = pair("fold", [P, RI, N, KH * FOLD])
        bias = sb("bias_chunk", [P, RI, NP, N])
        k_ = pair("k", [P, G, 3, P])
        q_ = pair("q", [P, RI, G, P])
        vT = sb("vT", [P, RI, G, P])
        v_ = pair("v", [P, G, HC, RI, HD])
        sq = sb("squares", [P, 2, GH // 2, 2, P])
        mag2 = sb("masked_mag2", [P, GH // 2, P])
        magc = sb("mag2", [P, GH, N])
        root = sb("magnitude", [P, GH, N])
        top = sb("row_max", [P, GH])
        dif = sb("minus_max", [P, GH, N])
        ex = sb("exps", [P, GH, N])
        den = sb("exp_sum", [P, GH])
        rden = sb("exp_sum_inverse", [P, GH])
        w = sb("weights", [P, GH, N])
        wt = sb("weights_turned", [P, GH, N])
        wt_ = pair("weights_split", [P, GH, N])
        wT = pair("wT", [P, GH, P])
        oT = sb("oT", [P, HC, N, TQ])

        s_fhi, s_flo, s_bias = sem("fold_hi_ready"), sem("fold_lo_ready"), sem("bias_ready")
        filled = sem("b_filled")
        freed = {"act": sem("b_freed_act"), "dve": sem("b_freed_dve")}
        s_hi, s_nki, s_sq = sem("b_hi_ready"), sem("minus_ki_ready"), sem("squares_ready")
        s_sum, s_msk = sem("mag2_summed"), sem("mag2_masked")
        s_mag, s_root, s_top, s_dif = sem("mag2_ready"), sem("magnitude_ready"), sem("max_ready"), sem("minus_max_ready")
        s_ex, s_den, s_rden, s_w, s_wt = (sem(n) for n in ("exps_ready", "exp_sum_ready", "inverse_ready", "weights_ready", "weights_turned_ready"))
        s_wthi, s_wtlo, s_wThi, s_wTlo = (sem(n) for n in ("weights_hi_ready", "weights_lo_ready", "wT_hi_ready", "wT_lo_ready"))
        s_out = sem("oT_stored")

        STEPS = KD * NQ
        VJ = [(ri, n) for ri in range(RI) for n in range(N)]
        KJ = [(ri, n) for ri in (1, 0) for n in range(N)]
        QJ = VJ
        OJ = [(h, gq) for h in range(HC) for gq in range(G // 4)]
        TJ = range(G // 2)
        SJ = range(GH // 2)
        kinds = (["act"] * len(VJ) + ["dve"] * len(KJ) + ["dve"] * len(QJ) + ["dve"] * len(OJ)
                 + ["dve"] * len(TJ) + ["act"] * len(SJ))
        ring = Ring(kinds)
        per, n_j = ring.per, len(kinds)
        j_k = len(VJ)
        j_q = j_k + len(KJ)
        j_o = j_q + len(QJ)
        j_t = j_o + len(OJ)
        j_s = j_t + len(TJ)
        n_hi = len(KJ) + len(QJ) + len(TJ)
        HB = GH // 4
        done = lambda j, it, r: (it + 1) * per[r] + ring.nth(j) + 1

        block = E(nc.Block())

        @block.sync
        def _(sp):
            def store(it):
                wait_apart(sp, freed["dve"], done(j_t - 1, it, "dve"))
                sp.dma_start(o_dram[bass.ds(it, 1)].rearrange("a p h n t -> (a p) (h n t)"),
                             oT[:].rearrange("p h n t -> p (h n t)")).then_inc(s_out, 16)

            def load(c, pieces):
                for i in pieces:
                    wait_apart(sp, s_flo, (c + 1) * len(VJ) + i + 1 - SLOTS)
                    carry.load_folded(sp, c_dram, c, i)

            load(0, range(SLOTS, len(VJ)))
            with sp.Fori(0, KD - 1) as c:
                with sp.Fori(0, NQ - 1) as q:
                    store(c * NQ + q)
                load(c + 1, range(len(VJ)))
                store(c * NQ + NQ - 1)
            sp.wait_ge(s_flo, (KD + 1) * len(VJ))
            for ri in range(RI):
                sp.dma_start(carry.wo_rows[:, ri], wo[ri].rearrange("(m p) d -> p m d", p=P)).then_inc(carry.s_wo, 16)
            with sp.Fori(0, NQ) as q:
                store((KD - 1) * NQ + q)
            sp.wait_ge(freed["dve"], (STEPS + 1) * per["dve"] + len(OJ))
            sp.dma_start(o_dram[STEPS].rearrange("p h n t -> p (h n t)"),
                         oT[:].rearrange("p h n t -> p (h n t)")).then_inc(s_out, 16)
            sp.wait_ge(s_out, 16 * (STEPS + 2))

        @block.gpsimd
        def _(pool):
            def expand(it):
                pool.wait_ge(s_wtlo, it + 1)
                nc.gpsimd.tensor_tensor(wT[1][:].rearrange("p a (n t) -> p (a n) t", t=32),
                                        f32(wt_[1][:]).rearrange("p a n -> p (a n)").unsqueeze(2).to_broadcast([P, GH * N, 32]),
                                        const.mask[:].unsqueeze(1).to_broadcast([P, GH * N, 32]),
                                        ALU.mult).then_inc(s_wTlo, 1)

            for v in v_:
                nc.gpsimd.memset(f32(v[:]), 0.0)
            with pool.Fori(0, KD) as c:
                with pool.Fori(0, NQ) as q:
                    it = c * NQ + q
                    expand(it)
                    pool.wait_ge(freed["dve"], done(j_k + N - 1, it, "dve"))
                    for s in range(2):
                        nc.gpsimd.tensor_tensor(k_[s][:, :, NKI_, :], const.zero[:].unsqueeze(2).to_broadcast([P, G, P]),
                                                f32(k_[s][:, :, KI_, :]), ALU.subtract).then_inc(s_nki, 1)
            expand(STEPS)

        @block.tensor
        def _(pe):
            def weighted_sum(it, j0, take):
                pe.wait_ge(s_wThi, it + 1)
                pe.wait_ge(s_wTlo, it + 1)
                for j, (h, gq) in enumerate(OJ):
                    ps = take(j0 + j)
                    for g4 in range(4):
                        g = 4 * gq + g4
                        lhs = [v[:, g, h].rearrange("p r d -> p (r d)") for v in v_]
                        rhs = [x[:, h * G + g, :] for x in wT]
                        mm = three(nc, ps[:, g4 * P:(g4 + 1) * P], lhs, rhs, True, True)
                    mm.then_inc(filled, 1)

            with pe.Fori(0, KD) as c:
                with pe.Fori(0, NQ) as q:
                    it = c * NQ + q
                    toks = bass.ds(q * TQ, TQ)

                    def take(j):
                        r, v = ring.before(j, it)
                        pe.wait_ge(freed[r], v)
                        return banks[ring.bank(j)]

                    for j0, pr, jobs in ((0, 2, VJ), (j_k, 1, KJ), (j_q, 0, QJ)):
                        for j, (ri, n) in enumerate(jobs):
                            if pr == 2:
                                pe.wait_ge(s_flo, (c + 1) * len(VJ) + j + 1)
                            ps = take(j0 + j)
                            for kh in range(KH):
                                f0 = kh * FOLD + pr * P
                                mm = three(nc, ps[:, 0:TQ], [f[:, ri, n, f0:f0 + P] for f in fold],
                                           [x[:, ri, kh, toks] for x in hT], kh == 0, kh == KH - 1)
                            mm.then_inc(filled, 1)
                    weighted_sum(it, j_o, take)
                    pe.wait_ge(freed["act"], done(j_k - 1, it, "act"))
                    for j in TJ:
                        ps = take(j_t + j)
                        for g2 in range(2):
                            for ri in range(RI):
                                o = (ri * 2 + g2) * P
                                mm = nc.tensor.transpose(ps[:, o:o + P], vT[:, ri, 2 * j + g2, :], const.ident[:])
                        mm.then_inc(filled, 1)
                    pe.wait_ge(freed["dve"], done(j_o - 1, it, "dve"))
                    pe.wait_ge(s_nki, 2 * it + 2)
                    for j in SJ:
                        ps = take(j_s + j)
                        for x in range(2):
                            gh = 2 * j + x
                            h, g = gh // G, gh % G
                            rows = slice(h * HD, (h + 1) * HD)
                            out = ps[:, x * 2 * P:(x + 1) * 2 * P]
                            for ri, ks in ((0, slice(KR_, NKI_ + 1)), (1, slice(KI_, KR_ + 1))):
                                mm = three(nc, out, [t[rows, ri, g, :] for t in q_],
                                           [t[rows, g, ks, :].rearrange("p s f -> p (s f)") for t in k_],
                                           ri == 0, ri == 1)
                        mm.then_inc(filled, 1)
            pe.wait_ge(freed["act"], (STEPS + 1) * per["act"])
            weighted_sum(STEPS, 0, lambda j: banks[j])

        @block.scalar
        def _(act):
            nc.scalar.activation(const.scratch[:, 0:1], const.eps[:], ACT.Identity).then_inc(freed["act"], per["act"])

            def magnitudes(it):
                act.wait_ge(s_mag, 2 * it + 2)
                nc.scalar.activation(root[:], magc[:], ACT.Sqrt, bias=const.eps[:]).then_inc(s_root, 1)

            def exponentials(it):
                act.wait_ge(s_dif, it + 1)
                nc.scalar.activation(ex[:], dif[:], ACT.Exp, scale=float(HD) ** -0.5).then_inc(s_ex, 1)

            def split_weights(c, pieces):
                for i in pieces:
                    ri, n = VJ[i]
                    act.wait_ge(s_in[i % SLOTS], (c * (len(VJ) // SLOTS) + i // SLOTS + 1) * 16)
                    nc.scalar.activation(fold[0][:, ri, n], fold_in[:, i % SLOTS], ACT.Identity).then_inc(s_fhi, 1)

            def step(c, q, last):
                it = c * NQ + q
                act.wait_ge(s_bias, c + 1)
                for j, (ri, n) in enumerate(VJ):
                    if j == 2:
                        magnitudes(it)
                    if j == 4:
                        exponentials(it)
                    act.wait_ge(filled, ring.filled(j, it))
                    nc.scalar.activation(vT[:, ri, :, n * 32:(n + 1) * 32],
                                         banks[ring.bank(j)][:, 0:TQ].rearrange("p (g t) -> p g t", t=32),
                                         ACT.Identity, bias=bias[:, ri, 2, n:n + 1]).then_inc(freed["act"], 1)
                for j0, pr, jobs in ((j_k, 1, KJ), (j_q, 0, QJ)):
                    for j, (ri, n) in enumerate(jobs):
                        act.wait_ge(filled, ring.filled(j0 + j, it))
                        dst = k_[0][:, :, 1 - ri, :] if pr == 1 else q_[0][:, ri]
                        nc.scalar.activation(dst[:, :, n * 32:(n + 1) * 32],
                                             banks[ring.bank(j0 + j)][:, 0:TQ].rearrange("p (g t) -> p g t", t=32),
                                             ACT.Identity, bias=bias[:, ri, pr, n:n + 1]).then_inc(s_hi, 1)
                if last:
                    split_weights(c + 1, range(SLOTS))
                for j in TJ:
                    act.wait_ge(filled, ring.filled(j_t + j, it))
                    nc.scalar.activation(v_[0][:, 2 * j:2 * j + 2].rearrange("p g h r d -> p r (g h) d"),
                                         banks[ring.bank(j_t + j)][:].rearrange("p (r a d) -> p r a d", r=RI, d=HD),
                                         ACT.Identity).then_inc(s_hi, 1)
                for j in SJ:
                    act.wait_ge(filled, ring.filled(j_s + j, it))
                    nc.scalar.activation(sq[:, j // HB, 2 * (j % HB):2 * (j % HB) + 2].rearrange("p a r f -> p (a r f)"),
                                         banks[ring.bank(j_s + j)][:], ACT.Square).then_inc(freed["act"], 1)
                    if last and j % 2 == 0 and SLOTS + j // 2 < len(VJ):
                        split_weights(c + 1, [SLOTS + j // 2])

            split_weights(0, range(len(VJ)))
            with act.Fori(0, KD - 1) as c:
                with act.Fori(0, NQ - 1) as q:
                    step(c, q, False)
                step(c, NQ - 1, True)
            with act.Fori(0, NQ) as q:
                step(KD - 1, q, False)
            magnitudes(STEPS)
            exponentials(STEPS)

        @block.vector
        def _(dve):
            nc.vector.memset(const.scratch[:, 1:2], 0.0).then_inc(freed["dve"], per["dve"])
            nc.vector.memset(const.scratch[:, 2:3], 0.0).then_inc(s_flo, len(VJ))
            nc.vector.memset(const.scratch[:, 3:4], 0.0).then_inc(s_out, 16)
            nc.vector.memset(magc[:], 0.0).then_inc(s_mag, 2)

            def softmax_a(it):
                dve.wait_ge(s_root, it + 1)
                nc.vector.tensor_reduce(top[:], root[:], AX_X, ALU.max).then_inc(s_top, 1)
                dve.wait_ge(s_top, it + 1)
                nc.vector.tensor_tensor(dif[:], root[:], top[:].unsqueeze(2).to_broadcast([P, GH, N]),
                                        ALU.subtract).then_inc(s_dif, 1)

            def softmax_b(it):
                dve.wait_ge(s_ex, it + 1)
                nc.vector.tensor_reduce(den[:], ex[:], AX_X, ALU.add).then_inc(s_den, 1)
                dve.wait_ge(s_den, it + 1)
                nc.vector.reciprocal(rden[:], den[:]).then_inc(s_rden, 1)
                dve.wait_ge(s_rden, it + 1)
                nc.vector.tensor_tensor(w[:], ex[:], rden[:].unsqueeze(2).to_broadcast([P, GH, N]),
                                        ALU.mult).then_inc(s_w, 1)
                dve.wait_ge(s_w, it + 1)
                for n in range(N):
                    for m in range(N):
                        ins = nc.vector.tensor_copy(wt[m * 32:(m + 1) * 32, :, n], w[n * 32:(n + 1) * 32, :, m])
                        ins.then_inc(s_wt, 1)
                dve.wait_ge(s_wt, N * N * (it + 1))
                nc.vector.tensor_copy(wt_[0][:], wt[:]).then_inc(s_wthi, 1)
                dve.wait_ge(s_wthi, it + 1)
                nc.vector.tensor_tensor(wt_[1][:], wt[:], f32(wt_[0][:]), ALU.subtract).then_inc(s_wtlo, 1)

            def expand(it):
                nc.vector.tensor_tensor(wT[0][:].rearrange("p a (n t) -> p (a n) t", t=32),
                                        f32(wt_[0][:]).rearrange("p a n -> p (a n)").unsqueeze(2).to_broadcast([P, GH * N, 32]),
                                        const.mask[:].unsqueeze(1).to_broadcast([P, GH * N, 32]),
                                        ALU.mult).then_inc(s_wThi, 1)

            def outputs(j0, fill, jobs):
                for j in jobs:
                    h, gq = OJ[j]
                    dve.wait_ge(filled, fill + j + 1)
                    nc.vector.tensor_copy(oT[:, h, :, gq * BANK // N:(gq + 1) * BANK // N].rearrange("p n (g t) -> p g n t", t=32),
                                          banks[(j0 + j) % NB][:].rearrange("p (g n t) -> p g n t", n=N, t=32)
                                          ).then_inc(freed["dve"], 1)

            def chunk_bias(c):
                nc.vector.tensor_copy(bias[:].rearrange("p r a n -> p (r a) n"),
                                      bias_cols[:, bass.ds(c, 1)].rearrange("p a i n -> p (a i) n")).then_inc(s_bias, 1)

            def split_weights(c, pieces):
                for i in pieces:
                    ri, n = VJ[i]
                    dve.wait_ge(s_fhi, c * len(VJ) + i + 1)
                    nc.vector.tensor_tensor(fold[1][:, ri, n], fold_in[:, i % SLOTS], f32(fold[0][:, ri, n]),
                                            ALU.subtract).then_inc(s_flo, 1)

            def step(c, q, last):
                it = c * NQ + q
                softmax_a(it)
                softmax_b(it)
                for i, (j0, pr, jobs) in enumerate(((j_k, 1, KJ), (j_q, 0, QJ))):
                    for j, (ri, n) in enumerate(jobs):
                        dve.wait_ge(s_hi, it * n_hi + i * len(KJ) + j + 1)
                        cols = slice(n * 32, (n + 1) * 32)
                        hi, lo = [k_[s][:, :, 1 - ri, cols] if pr == 1 else q_[s][:, ri, :, cols] for s in range(2)]
                        nc.vector.scalar_tensor_tensor(out=lo, in0=banks[ring.bank(j0 + j)][:, 0:TQ].rearrange("p (g t) -> p g t", t=32),
                                                       scalar=bias[:, ri, pr, n:n + 1], in1=f32(hi),
                                                       op0=ALU.add, op1=ALU.subtract).then_inc(freed["dve"], 1)
                    if pr == 1:
                        expand(it)
                if last:
                    dve.wait_ge(freed["dve"], done(j_o - 1, it, "dve"))
                    chunk_bias(c + 1)
                    split_weights(c + 1, range(2))
                dve.wait_ge(s_out, (it + 1) * 16)
                outputs(j_o, it * n_j + j_o, range(2))
                if last:
                    split_weights(c + 1, range(2, SLOTS))
                outputs(j_o, it * n_j + j_o, range(2, len(OJ)))
                for j in TJ:
                    dve.wait_ge(s_hi, it * n_hi + len(KJ) + len(QJ) + j + 1)
                    hi, lo = [v_[s][:, 2 * j:2 * j + 2].rearrange("p g h r d -> p r (g h) d") for s in range(2)]
                    nc.vector.tensor_tensor(lo, banks[ring.bank(j_t + j)][:].rearrange("p (r a d) -> p r a d", r=RI, d=HD),
                                            f32(hi), ALU.subtract).then_inc(freed["dve"], 1)
                for b in range(2):
                    if last:
                        split_weights(c + 1, range(SLOTS + 2 * b, SLOTS + 2 * b + 2))
                    dve.wait_ge(freed["act"], done(j_s + (b + 1) * HB - 1, it, "act"))
                    dve.wait_ge(s_mag, 2 * it + b + 2)
                    nc.vector.tensor_tensor(mag2[:], sq[:, b, :, 0, :], sq[:, b, :, 1, :], ALU.add).then_inc(s_sum, 1)
                    dve.wait_ge(s_sum, 2 * it + b + 1)
                    m2 = mag2[:].rearrange("p a (n t) -> p (a n) t", t=32)
                    nc.vector.tensor_tensor(m2, m2, const.mask[:].unsqueeze(1).to_broadcast([P, GH * N // 2, 32]),
                                            ALU.mult).then_inc(s_msk, 1)
                    dve.wait_ge(s_msk, 2 * it + b + 1)
                    nc.vector.tensor_reduce(magc[:, b * GH // 2:(b + 1) * GH // 2].rearrange("p a n -> p (a n)"),
                                            m2, AX_X, ALU.add).then_inc(s_mag, 1)

            chunk_bias(0)
            split_weights(0, range(len(VJ)))
            with dve.Fori(0, KD - 1) as c:
                with dve.Fori(0, NQ - 1) as q:
                    step(c, q, False)
                step(c, NQ - 1, True)
            with dve.Fori(0, NQ) as q:
                step(KD - 1, q, False)
            softmax_a(STEPS)
            softmax_b(STEPS)
            expand(STEPS)
            dve.wait_ge(s_out, (STEPS + 1) * 16)
            outputs(0, STEPS * n_j, range(len(OJ)))


def stage_interact(nc, const, carry, banks, int_r, int_i, bo_cols, o_dram, z_dram):
    with ExitStack() as ctx:
        E = ctx.enter_context
        sb = lambda name, shape, dt=F32: E(nc.sbuf_tensor(name, shape, dt))
        pair = lambda name, shape: [sb(f"{name}_{s}", shape, F32R) for s in ("hi", "lo")]
        sem = lambda name: E(nc.semaphore(name))
        TT = TQ // P
        rows = sb("int_rows", [P, 3, KD, D])
        woT = pair("woT", [P, RI, KD, D])
        wT = pair("intT", [P, 3, KD, D])
        o_in = sb("out_in", [P, RI, KD, TQ])
        o_ = pair("out", [P, RI, KD, TQ])
        a_f = sb("attn_f", [P, 2, 3, KD, TQ])
        a_ = pair("attn", [P, 3, KD, TQ])
        k1 = sb("k1", [P, TT, D])
        z = sb("z_out", [P, TT, RI, D])

        s_int, s_oin = sem("int_in"), sem("out_in_ready")
        s_sums = sem("int_sums_ready")
        s_tf, s_thi, s_tlo = sem("turn_filled"), sem("turn_hi"), sem("turn_lo")
        s_af, s_ahi0, s_as = sem("attn_filled"), sem("attn_evacuated"), sem("attn_sum_ready")
        s_ahi, s_alo = sem("attn_hi"), sem("attn_lo")
        s_ohi, s_olo = sem("out_hi"), sem("out_lo")
        s_zf, s_k1, s_z, s_st = sem("z_filled"), sem("k1_ready"), sem("z_ready"), sem("z_stored")

        STEPS = N * NQ
        WJ = [(ri, m) for ri in range(RI) for m in range(KD)]
        TJ = [(w, m) for w in range(3) for m in range(KD)]
        AJ = [(ri, m) for ri in range(RI) for m in range(KD)]
        ZB = 2
        n_t, n_a, n_z = len(TJ), len(AJ), 3 * TT
        BESIDE = [range(i * n_t // n_a, (i + 1) * n_t // n_a) for i in range(n_a)]
        SRC = (0, 1, 2)
        o_view = o_dram[1:].rearrange("(c q) p h n t -> q c p h n t", q=NQ)
        z_view = z_dram.rearrange("n (q k p) r d -> n q p k (r d)", p=P, k=TT)

        def turned(n):
            return len(WJ) + (n + 1) * n_t

        block = E(nc.Block())

        @block.sync
        def _(sp):
            def load_out(n, q):
                for ri in range(RI):
                    for hh in range(HC):
                        src = o_view[q, :, ri * HD:(ri + 1) * HD, hh, bass.ds(n, 1), :].rearrange("c p a t -> p (a c) t")
                        sp.dma_start(o_in[hh * HD:(hh + 1) * HD, ri], src).then_inc(s_oin, 16)

            def store(n, q):
                wait_apart(sp, s_z, RI * TT * (n * NQ + q + 1))
                sp.dma_start(z_view[bass.ds(n, 1), q].rearrange("a p k f -> (a p) k f"),
                             z[:].rearrange("p k r d -> p k (r d)")).then_inc(s_st, 16)

            def state(n, first, last):
                for q in range(NQ):
                    if not (last and q == NQ - 1):
                        wait_apart(sp, s_olo, n * NQ + q + 1)
                        load_out(n + (q + 1) // NQ, (q + 1) % NQ)
                    if not (first and q == 0):
                        store(n - (q == 0), (q - 1) % NQ)
                    if last and q == 2:
                        sp.wait_ge(s_st, 16 * ((N - 1) * NQ + 1))
                        sp.wait_ge(s_tf, len(WJ))
                        sp.dma_start(carry.z0, z_dram[:, 0:P].rearrange("n p r d -> p n r d")).then_inc(carry.s_z0, 16)

            load_out(0, 0)
            state(0, True, False)
            with sp.Fori(1, N - 1) as n:
                state(n, False, False)
            state(N - 1, False, True)
            store(N - 1, NQ - 1)
            sp.wait_ge(s_st, 16 * STEPS)

        @block.gpsimd
        def _(pool):
            def state(n):
                if not isinstance(n, int):
                    pool.wait_ge(s_tf, len(WJ) + n * n_t)
                else:
                    pool.wait_ge(s_oin, 16 * RI * HC)
                for i, src in enumerate((int_r, int_i)):
                    pool.dma_start(rows[:, i], src[bass.ds(n, 1)].rearrange("a (m p) d -> p (a m) d", p=P)).then_inc(s_int, 16)
                pool.wait_ge(s_int, 32 * (n + 1))
                nc.gpsimd.tensor_tensor(rows[:, 2], rows[:, 0], rows[:, 1], ALU.add).then_inc(s_sums, 1)
                pool.wait_ge(s_sums, 2 * n + 1)
                nc.gpsimd.tensor_tensor(rows[:, 1], rows[:, 1], rows[:, 0], ALU.subtract).then_inc(s_sums, 1)

            state(0)
            with pool.Fori(1, N) as n:
                state(n)

        @block.tensor
        def _(pe):
            def turns(jobs, j0, rows, some=None):
                for j, (w, m) in enumerate(jobs):
                    if some is not None and j not in some:
                        continue
                    ps = banks[ZB + j % 6]
                    at_least(pe, s_tlo, j0 + j - 5)
                    for k in range(KD):
                        mm = nc.tensor.transpose(ps[:, k * P:(k + 1) * P], rows[:, w, m, k * P:(k + 1) * P],
                                                 const.ident[:])
                    mm.then_inc(s_tf, 1)

            def attn(n, q):
                s = n * NQ + q
                pe.wait_ge(s_olo, s + 1)
                for j, (ri, m) in enumerate(AJ):
                    if q == 1:
                        turns(TJ, len(WJ) + n * n_t, rows, BESIDE[j])
                    ps = banks[j % ZB]
                    at_least(pe, s_ahi0, s * n_a + j - ZB + 1)
                    for k in range(KD):
                        mm = three(nc, ps[:, 0:TQ], [w[:, ri, k, m * P:(m + 1) * P] for w in woT],
                                   [o[:, ri, k] for o in o_], k == 0, k == KD - 1)
                    mm.then_inc(s_af, 1)

            def product(n, s):
                pe.wait_ge(s_alo, s + 1)
                pe.wait_ge(s_tlo, turned(n))
                at_least(pe, s_z, RI * TT * s)
                for t in range(TT):
                    for i in range(3):
                        ps = banks[ZB + 3 * t + i]
                        for k in range(KD):
                            mm = three(nc, ps[:], [a[:, i, k, t * P:(t + 1) * P] for a in a_],
                                       [w[:, i, k] for w in wT], k == 0, k == KD - 1)
                        mm.then_inc(s_zf, 1)

            def turn_state(n):
                pe.wait_ge(s_sums, 2 * n + 2)
                at_least(pe, s_z, RI * TT * NQ * n)

            pe.wait_ge(carry.s_wo, 16 * RI)
            turns(WJ, 0, carry.wo_rows)
            def state(n, first=False):
                for q in range(NQ):
                    attn(n, q)
                    if q:
                        product(n, n * NQ + q - 1)
                    elif not first:
                        product(n - 1, n * NQ - 1)
                    if q == 0:
                        turn_state(n)

            state(0, True)
            with pe.Fori(1, N - 1) as n:
                state(n)
            state(N - 1)
            product(N - 1, STEPS - 1)

        @block.scalar
        def _(act):
            def turns(jobs, j0, dst, some=None):
                for j, (w, m) in enumerate(jobs):
                    if some is not None and j not in some:
                        continue
                    act.wait_ge(s_tf, j0 + j + 1)
                    nc.scalar.activation(dst[0][:, w, :, m * P:(m + 1) * P],
                                         banks[ZB + j % 6][:].rearrange("p (k f) -> p k f", k=KD),
                                         ACT.Identity).then_inc(s_thi, 1)

            def split_out(s):
                act.wait_ge(s_oin, 16 * RI * HC * (s + 1))
                nc.scalar.activation(o_[0][:], o_in[:], ACT.Identity).then_inc(s_ohi, 1)

            def attn(n, q, par):
                s = n * NQ + q
                for j, (ri, m) in enumerate(AJ):
                    if q == 1:
                        turns(TJ, len(WJ) + n * n_t, wT, BESIDE[j])
                    act.wait_ge(s_af, s * n_a + j + 1)
                    if j == 0:
                        at_least(act, s_alo, s - 1)
                    nc.scalar.activation(a_f[:, par, 1 + ri, m], banks[j % ZB][:, 0:TQ], ACT.Identity,
                                         bias=bo_cols[:, ri, m:m + 1]).then_inc(s_ahi0, 1)

            def split_attn(s, par):
                act.wait_ge(s_as, s + 1)
                at_least(act, s_zf, n_z * s)
                nc.scalar.activation(a_[0][:], a_f[:, par], ACT.Identity).then_inc(s_ahi, 1)

            def product(s):
                for t in range(TT):
                    act.wait_ge(s_zf, s * n_z + 3 * t + 1)
                    at_least(act, s_z, RI * TT * s)
                    nc.scalar.activation(k1[:, t], banks[ZB + 3 * t][:], ACT.Identity).then_inc(s_k1, 1)

            def state(n, first=False, last=False):
                for q in range(NQ):
                    s = n * NQ + q
                    attn(n, q, q % 2)
                    if not (last and q == NQ - 1):
                        split_out(s + 1)
                    if not (first and q == 0):
                        product(s - 1)
                    split_attn(s, q % 2)

            turns(WJ, 0, woT)
            split_out(0)
            state(0, first=True)
            with act.Fori(1, N - 1) as n:
                state(n)
            state(N - 1, last=True)
            product(STEPS - 1)

        @block.vector
        def _(dve):
            def turns(jobs, j0, dst):
                for j, (w, m) in enumerate(jobs):
                    dve.wait_ge(s_thi, j0 + j + 1)
                    cols = slice(m * P, (m + 1) * P)
                    nc.vector.tensor_tensor(dst[1][:, w, :, cols], banks[ZB + j % 6][:].rearrange("p (k f) -> p k f", k=KD),
                                            f32(dst[0][:, w, :, cols]), ALU.subtract).then_inc(s_tlo, 1)

            def split_out(s):
                dve.wait_ge(s_ohi, s + 1)
                nc.vector.tensor_tensor(o_[1][:], o_in[:], f32(o_[0][:]), ALU.subtract).then_inc(s_olo, 1)

            def attn_sum(s, par):
                dve.wait_ge(s_ahi0, n_a * (s + 1))
                nc.vector.tensor_tensor(a_f[:, par, 0], a_f[:, par, 1], a_f[:, par, 2], ALU.add).then_inc(s_as, 1)

            def split_attn(s, par):
                dve.wait_ge(s_ahi, s + 1)
                nc.vector.tensor_tensor(a_[1][:], a_f[:, par], f32(a_[0][:]), ALU.subtract).then_inc(s_alo, 1)

            def product(s):
                for t in range(TT):
                    if t == 0:
                        at_least(dve, s_st, 16 * s)
                    dve.wait_ge(s_k1, s * TT + t + 1)
                    dve.wait_ge(s_zf, s * n_z + 3 * t + 2)
                    nc.vector.tensor_tensor(z[:, t, 1], k1[:, t], banks[ZB + 3 * t + 1][:], ALU.add).then_inc(s_z, 1)
                    dve.wait_ge(s_zf, s * n_z + 3 * t + 3)
                    nc.vector.tensor_tensor(z[:, t, 0], k1[:, t], banks[ZB + 3 * t + 2][:], ALU.subtract).then_inc(s_z, 1)

            def state(n, first=False, last=False):
                for q in range(NQ):
                    s = n * NQ + q
                    attn_sum(s, q % 2)
                    if not (last and q == NQ - 1):
                        split_out(s + 1)
                    if not (first and q == 0):
                        product(s - 1)
                    split_attn(s, q % 2)
                    if q == 0:
                        turns(TJ, len(WJ) + n * n_t, wT)

            turns(WJ, 0, woT)
            split_out(0)
            state(0, first=True)
            with dve.Fori(1, N - 1) as n:
                state(n)
            state(N - 1, last=True)
            product(STEPS - 1)


def stage_measure(nc, const, carry, banks, strength, meas_r, meas_i, post_w, post_vectors, z_dram, y_dram, out):
    TINY = 1e-17
    SHIFTS = ((1, 0, 3), (2, 3, 2), (3, 5, 1))
    PAIRS = [(i, i + d) for d, _, n in SHIFTS for i in range(n)]
    NPAIR = len(PAIRS)
    of = lambda i, j: PAIRS.index((min(i, j), max(i, j)))
    HALVES = (slice(0, 3), slice(3, 6))
    ZBUF = 3
    FAR = N - 1
    ORDER = [(FAR + k) % N for k in range(N)]
    EARLY = TILES - 2
    with ExitStack() as ctx:
        E = ctx.enter_context
        sb = lambda name, shape, dt=F32: E(nc.sbuf_tensor(name, shape, dt))
        pair = lambda name, shape: [sb(f"{name}_{s}", shape, F32R) for s in ("hi", "lo")]
        sem = lambda name: E(nc.semaphore(name))
        z_more = sb("z_in", [P, ZBUF - 1, N, RI, D])
        z = [carry.z0] + [z_more[:, i] for i in range(ZBUF - 1)]
        st = sb("strengths", [P, TILES, N, N])
        st_neg = sb("strengths_negated", [P, TILES, N, N])
        sq = sb("z_squares", [P, N, RI, D])
        root = sb("root", [P, NPAIR, D])
        seed = sb("seed", [P, NPAIR, D])
        im = sb("imag_products", [P, NPAIR, D])
        x = sb("cosines", [P, NPAIR, D])
        gz = sb("weighted_z", [P, N, RI, D])
        gain = sq[:, :, 1]
        nrm = sb("norm", [P, 1])
        rn = sb("norm_inverse", [P, 1])
        ones = sb("ones", [P, 1])
        supT = pair("supT", [P, RI + 1, KD, P])
        squares = sb("sup_squares", [P, RI, KD * P])
        amp = squares[:, 0]
        ampT = pair("ampT", [P, KD, P])
        mT = pair("measT", [P, RI, KD, OUT])
        pT = pair("postT", [P, KD, OUT])
        post_b = sb("post_b_bcast", [P, OUT])
        y_row = sb("y_rows", [P, OUT])
        stats = sb("post_stats", [P, TILES, 6])
        mv = sb("post_mean_var", [P, TILES, 2])
        std = sb("post_std", [P, TILES])
        rstd = sb("post_rstd", [P, TILES])
        eps_ln = sb("eps_post", [P, 1])
        tiny2 = sb("tiny_squared", [P, 1])

        post_g, post_be = gain[:, 0], gain[:, 1]
        y = z[0].rearrange("p n r d -> p (n r) d")
        w_rows = [v.rearrange("p n r d -> p (n r) d") for v in (z[2][:, 0:2], z[2][:, 2:4], gz[:, 0:2])]
        w_dst = [[t[:, 0] for t in mT], [t[:, 1] for t in mT], [t[:] for t in pT]]
        TJ = [(w, m) for w in range(3) for m in range(KD)]

        s_w, s_st, s_vec, s_gbe = sem("meas_rows_in"), sem("strength_in"), sem("post_b_in"), sem("post_g_be_in")
        s_zin = [carry.s_z0] + [sem(f"z_in_ready_{i}") for i in range(1, ZBUF)]
        s_eps, s_neg_st = sem("d_constants_ready"), sem("strengths_negated_ready")
        s_tf, s_thi, s_tlo = sem("d_turn_filled"), sem("d_turn_hi"), sem("d_turn_lo")
        s_sq, s_m2, s_mm, s_root, s_ln, s_seed, s_newt = (sem(n) for n in (
            "z_squares_ready", "z_mag2_ready", "z_mag2_products", "roots_ready", "ln_ready", "seed_ready", "root_times_seed"))
        s_inv, s_re, s_im_far, s_im, s_x, s_cos = (sem(n) for n in ("root_inverse_ready", "real_products", "imag_products_far", "imag_products", "dots_ready", "cosines_ready"))
        s_g0, s_g0_act, s_g, s_gz, s_gz_last = (sem(n) for n in ("gains_begun", "gains_begun_act", "gains_step", "weighted_z_ready", "weighted_last_z_ready"))
        s_nf, s_n, s_rn = sem("norm2_filled"), sem("norm_ready"), sem("norm_inverse_ready")
        s_sf, s_shi, s_slo, s_sneg = sem("supT_filled"), sem("supT_hi"), sem("supT_lo"), sem("supT_negated_lo")
        s_mf, s_a2, s_asum, s_amp = sem("meas_filled"), sem("amp_squares"), sem("amp2_ready"), sem("amp_ready")
        s_pf, s_phi, s_plo = sem("ampT_filled"), sem("ampT_hi"), sem("ampT_lo")
        s_yf, s_y, s_yst, s_var, s_std, s_rstd, s_yn, s_yg, s_yb = (sem(n) for n in ("post_filled", "y_rows", "y_stats", "y_variance", "y_std", "y_rstd", "y_normed", "y_scaled", "y_ready"))
        s_ystored, s_yin = sem("y_rows_stored"), sem("y_rows_back")
        s_out, s_gelu = sem("out_stored"), sem("gelu_ready")
        B_SUP, B_M, B_AMP, B_Y, B_N = 0, 2, 4, 5, 6
        TB, NTB = 2, NB - 2

        block = E(nc.Block())

        @block.sync
        def _(sp):
            def load(t):
                sp.dma_start(z[t % ZBUF], z_dram[:, t * P:(t + 1) * P].rearrange("n p r d -> p n r d")).then_inc(s_zin[t % ZBUF], 16)

            for w, src in zip(w_rows, (meas_r, meas_i, post_w)):
                sp.dma_start(w, src.rearrange("(m p) d -> p m d", p=P)).then_inc(s_w, 16)
            sp.dma_start(st[:], strength.rearrange("(t p) i j -> p t (i j)", p=P)
                         .rearrange("p t (i j) -> p t i j", i=N)).then_inc(s_st, 16)
            sp.dma_start(post_b[:], post_vectors[0].partition_broadcast(P)).then_inc(s_vec, 16)
            load(1)
            sp.wait_ge(s_tf, 2 * KD)
            load(2)

            def store_rows(t):
                sp.wait_ge(s_y, t + 1)
                sp.dma_start(y_dram[t], y_row[:]).then_inc(s_ystored, 16)

            for t in range(ZBUF, TILES):
                sp.wait_ge(s_gz, t - ZBUF + 1)
                sp.wait_ge(s_gz_last, t - ZBUF + 1)
                load(t)
                if t > ZBUF:
                    store_rows(t - ZBUF - 1)
            for t in range(TILES - ZBUF - 1, EARLY):
                store_rows(t)
            sp.wait_ge(s_ystored, 16 * EARLY)
            sp.wait_ge(s_gz, TILES - 1)
            sp.wait_ge(s_gz_last, TILES - 1)
            sp.dma_start(y[:, 0:EARLY], y_dram[0:EARLY].rearrange("t p f -> p t f")).then_inc(s_yin, 16)
            sp.wait_ge(s_gz, TILES)
            sp.wait_ge(s_gz_last, TILES)
            for dst, v in ((post_g, post_vectors[1]), (post_be, post_vectors[2])):
                sp.dma_start(dst, v.partition_broadcast(P)).then_inc(s_gbe, 16)
            for t in range(TILES):
                sp.wait_ge(s_gelu, t + 1)
                sp.dma_start(out[t * P:(t + 1) * P, :], y[:, t]).then_inc(s_out, 16)
            sp.wait_ge(s_out, 16 * TILES)

        @block.gpsimd
        def _(pool):
            def mag2(t):
                for h in range(2):
                    pool.wait_ge(s_sq, 2 * t + h + 1)
                    s = sq[:, 2 * h:2 * h + 2]
                    nc.gpsimd.tensor_tensor(s[:, :, 0], s[:, :, 0], s[:, :, 1], ALU.add).then_inc(s_m2, 1)
                pool.wait_ge(s_m2, 2 * t + 2)

            def mag2_products(t, half):
                for d, p0, n in SHIFTS[:1] if half == 0 else SHIFTS[1:]:
                    at_least(pool, s_inv, 2 * t + half - 1)
                    nc.gpsimd.tensor_tensor(root[:, p0:p0 + n], sq[:, 0:n, 0], sq[:, d:d + n, 0], ALU.mult).then_inc(s_mm, 1)

            def newton(t):
                for h, s in enumerate(HALVES):
                    pool.wait_ge(s_seed, 2 * t + h + 1)
                    nc.gpsimd.tensor_tensor(root[:, s], root[:, s], seed[:, s], ALU.mult).then_inc(s_newt, 1)

            def imag_products(t, par, nth):
                pool.wait_ge(s_zin[par], 16 * nth)
                at_least(pool, s_x, t)
                zt = z[par]
                for d, p0, n in SHIFTS[1:]:
                    nc.gpsimd.tensor_tensor(im[:, p0:p0 + n], zt[:, 0:n, 1], zt[:, d:d + n, 1], ALU.mult).then_inc(s_im_far, 1)

            def weight(t, par):
                at_least(pool, s_sf, RI * t)
                pool.wait_ge(s_g, (N - 2) * N * t + (N - 3) * N + 1)
                nc.gpsimd.tensor_tensor(gz[:, FAR:], z[par][:, FAR:], gain[:, FAR:].unsqueeze(2).to_broadcast([P, N - FAR, RI, D]),
                                        ALU.mult).then_inc(s_gz_last, 1)

            def negate(t):
                pool.wait_ge(s_slo, RI * (t + 1))
                nc.gpsimd.tensor_tensor(supT[1][:, 2].rearrange("p k f -> p (k f)"), const.zero[:].to_broadcast([P, KD * P]),
                                        f32(supT[1][:, 1]).rearrange("p k f -> p (k f)"), ALU.subtract).then_inc(s_sneg, 1)

            def body(t, par, nth, first=False, last=False):
                if last:
                    nc.gpsimd.memset(const.scratch[:, 4:5], 0.0).then_inc(s_m2, 2)
                else:
                    mag2(t + 1)
                    mag2_products(t + 1, 0)
                    mag2_products(t + 1, 1)
                if not first:
                    negate(t - 1)
                if not last:
                    imag_products(t + 1, (par + 1) % ZBUF, nth + (par == ZBUF - 1))
                weight(t, par)
                if not last:
                    newton(t + 1)

            imag_products(0, 0, 1)
            body(0, 0, 1, first=True)
            with pool.Fori(0, (TILES - 2) // ZBUF) as i:
                for k in range(1, ZBUF + 1):
                    body(ZBUF * i + k, k % ZBUF, i + 1 + k // ZBUF)
            body(TILES - 1, (TILES - 1) % ZBUF, (TILES - 1) // ZBUF + 1, last=True)
            negate(TILES - 1)
            pool.wait_ge(s_gbe, 16 * 2)
            for t in range(TILES):
                pool.wait_ge(s_yg, t + 1)
                nc.gpsimd.tensor_tensor(y[:, t], y[:, t], post_be, ALU.add).then_inc(s_yb, 1)

        @block.tensor
        def _(pe):
            pe.wait_ge(s_w, 16 * 3)
            for j, (w, m) in enumerate(TJ):
                ps = banks[TB + j % NTB]
                at_least(pe, s_tlo, j - NTB + 1)
                for k in range(KD):
                    mm = nc.tensor.transpose(ps[:, k * P:(k + 1) * P], w_rows[w][:, m, k * P:(k + 1) * P], const.ident[:])
                mm.then_inc(s_tf, 1)
            def superpose(t, first=False):
                pe.wait_ge(s_gz, t + 1)
                pe.wait_ge(s_gz_last, t + 1)
                for ri in range(RI):
                    for k in range(KD):
                        for n in range(N):
                            mm = nc.tensor.matmul(banks[B_SUP + ri][:, k * P:(k + 1) * P], gz[:, n, ri, k * P:(k + 1) * P],
                                                  const.ident[:], start=n == 0, stop=n == N - 1)
                    mm.then_inc(s_sf, 1)
                if first:
                    pe.wait_ge(s_tlo, len(TJ))
                pe.wait_ge(s_shi, RI * (t + 1))
                at_least(pe, s_n, t)
                for ri in range(RI):
                    for k in range(KD):
                        mm = nc.tensor.matmul(banks[B_N][:, 0:1], squares[:, ri, k * P:(k + 1) * P], ones[:],
                                              start=ri == 0 and k == 0, stop=ri == 1 and k == KD - 1)
                mm.then_inc(s_nf, 1)

            def last_layer(t):
                pe.wait_ge(s_plo, t + 1)
                at_least(pe, s_y, t)
                for k in range(KD):
                    mm = three(nc, banks[B_Y][:], [a[:, k] for a in ampT], [w[:, k] for w in pT], k == 0, k == KD - 1)
                mm.then_inc(s_yf, 1)

            def measure(t):
                pe.wait_ge(s_slo, RI * (t + 1))
                for o, terms in enumerate((((0, 1), (1, 0)), ((0, 0), (2, 1)))):
                    for i, (s, m) in enumerate(terms):
                        if s == 2:
                            pe.wait_ge(s_sneg, t + 1)
                        for k in range(KD):
                            mm = three(nc, banks[B_M + o][:], [v[:, s, k] for v in supT], [v[:, m, k] for v in mT],
                                       i == 0 and k == 0, i == 1 and k == KD - 1)
                    mm.then_inc(s_mf, 1)
                pe.wait_ge(s_amp, t + 1)
                for k in range(KD):
                    mm = nc.tensor.transpose(banks[B_AMP][:, k * P:(k + 1) * P], amp[:, k * P:(k + 1) * P], const.ident[:])
                mm.then_inc(s_pf, 1)

            superpose(0, first=True)
            measure(0)
            with pe.Fori(1, TILES) as t:
                superpose(t)
                last_layer(t - 1)
                measure(t)
            last_layer(TILES - 1)

        @block.scalar
        def _(act):
            def z_squares(t, par, nth):
                act.wait_ge(s_zin[par], 16 * nth)
                at_least(act, s_mm, len(SHIFTS) * t)
                at_least(act, s_gz, t - 1)
                at_least(act, s_gz_last, t - 1)
                for h in range(2):
                    s = slice(2 * h, 2 * h + 2)
                    nc.scalar.activation(sq[:, s], z[par][:, s], ACT.Square).then_inc(s_sq, 1)

            def roots(t, h):
                act.wait_ge(s_mm, len(SHIFTS) * t + (1, 3)[h])
                s = HALVES[h]
                nc.scalar.activation(root[:, s], root[:, s], ACT.Sqrt, bias=tiny2[:]).then_inc(s_root, 1)

            def gains(t):
                cur = lambda s, i, j: s[:, bass.ds(t, 1), i, j]
                act.wait_ge(s_cos, 2 * t + 1)
                act.wait_ge(s_m2, 2 * t + 4)
                for j in range(FAR):
                    nc.scalar.activation(gain[:, j], x[:, of(j + 1, j)], ACT.Identity, bias=cur(st, j, j),
                                         scale=cur(st_neg, j + 1, j)).then_inc(s_g0_act, 1)

            def seeds(t):
                for h, s in enumerate(HALVES):
                    act.wait_ge(s_root, 2 * t + h + 1)
                    at_least(act, s_cos, 2 * t)
                    nc.scalar.activation(seed[:, s], root[:, s], ACT.Ln).then_inc(s_ln, 1)
                for h, s in enumerate(HALVES):
                    act.wait_ge(s_ln, 2 * t + h + 1)
                    nc.scalar.activation(seed[:, s], seed[:, s], ACT.Exp, scale=-1.0).then_inc(s_seed, 1)

            def supT_hi(t):
                at_least(act, s_pf, t)
                for ri in range(RI):
                    act.wait_ge(s_sf, RI * t + ri + 1)
                    bank = banks[B_SUP + ri][:]
                    nc.scalar.activation(supT[0][:, ri].rearrange("p k f -> p (k f)"), bank, ACT.Identity)
                    if ri == 1:
                        nc.scalar.activation(supT[0][:, 2].rearrange("p k f -> p (k f)"), bank, ACT.Identity, scale=-1.0)
                    nc.scalar.activation(squares[:, ri], bank, ACT.Square).then_inc(s_shi, 1)

            def amplitude_squares(t):
                for o in range(2):
                    act.wait_ge(s_mf, 2 * t + o + 1)
                    nc.scalar.activation(squares[:, o], banks[B_M + o][:], ACT.Square).then_inc(s_a2, 1)

            def amplitude(t):
                act.wait_ge(s_asum, t + 1)
                nc.scalar.activation(amp, amp, ACT.Sqrt).then_inc(s_amp, 1)

            def norm(t):
                at_least(act, s_rn, t)
                act.wait_ge(s_nf, t + 1)
                nc.scalar.activation(nrm[:], banks[B_N][:, 0:1], ACT.Sqrt, bias=const.eps[:]).then_inc(s_n, 1)

            def ampT_hi(t):
                act.wait_ge(s_pf, t + 1)
                nc.scalar.activation(ampT[0][:].rearrange("p k f -> p (k f)"), banks[B_AMP][:], ACT.Identity).then_inc(s_phi, 1)

            def body(t, par, nth, first=False, last=False):
                if not first and not last:
                    z_squares(t + 1, (par + 1) % ZBUF, nth + (par == ZBUF - 1))
                if not first:
                    supT_hi(t - 1)
                if not last:
                    roots(t + 1, 0)
                gains(t)
                if not last:
                    roots(t + 1, 1)
                    seeds(t + 1)
                if not first:
                    amplitude_squares(t - 1)
                    norm(t - 1)
                    amplitude(t - 1)
                    ampT_hi(t - 1)

            def turns():
                for j, (w, m) in enumerate(TJ):
                    act.wait_ge(s_tf, j + 1)
                    nc.scalar.activation(w_dst[w][0][:, :, m * P:(m + 1) * P],
                                         banks[TB + j % NTB][:].rearrange("p (k f) -> p k f", k=KD), ACT.Identity).then_inc(s_thi, 1)

            z_squares(0, 0, 1)
            act.wait_ge(s_eps, 3)
            roots(0, 0)
            roots(0, 1)
            seeds(0)
            z_squares(1, 1, 1)
            turns()
            act.wait_ge(s_neg_st, 1)
            body(0, 0, 1, first=True)
            with act.Fori(0, (TILES - 2) // ZBUF) as i:
                for k in range(1, ZBUF + 1):
                    body(ZBUF * i + k, k % ZBUF, i + 1 + k // ZBUF)
            body(TILES - 1, (TILES - 1) % ZBUF, (TILES - 1) // ZBUF + 1, last=True)
            supT_hi(TILES - 1)
            norm(TILES - 1)
            act.wait_ge(s_var, EARLY)
            nc.scalar.activation(std[:, 0:EARLY], mv[:, 0:EARLY, 1], ACT.Sqrt, bias=eps_ln[:]).then_inc(s_std, 1)
            amplitude_squares(TILES - 1)
            amplitude(TILES - 1)
            ampT_hi(TILES - 1)
            act.wait_ge(s_var, TILES)
            nc.scalar.activation(std[:, EARLY:], mv[:, EARLY:, 1], ACT.Sqrt, bias=eps_ln[:]).then_inc(s_std, 1)
            for t in range(TILES):
                act.wait_ge(s_yb, t + 1)
                nc.scalar.activation(y[:, t], y[:, t], ACT.Gelu).then_inc(s_gelu, 1)

        @block.vector
        def _(dve):
            nc.vector.memset(eps_ln[:], EPS_LN).then_inc(s_eps, 1)
            nc.vector.memset(tiny2[:], TINY * TINY).then_inc(s_eps, 1)
            nc.vector.memset(ones[:], 1.0).then_inc(s_eps, 1)
            for h in range(2):
                dve.wait_ge(s_sq, h + 1)
                s = sq[:, 2 * h:2 * h + 2]
                nc.vector.tensor_tensor(s[:, :, 0], s[:, :, 0], s[:, :, 1], ALU.add).then_inc(s_m2, 1)
            dve.wait_ge(s_m2, 2)
            for d, p0, n in SHIFTS:
                nc.vector.tensor_tensor(root[:, p0:p0 + n], sq[:, 0:n, 0], sq[:, d:d + n, 0], ALU.mult).then_inc(s_mm, 1)
            def real_products(t, par, nth):
                zt = z[par]
                dve.wait_ge(s_zin[par], 16 * nth)
                for d, p0, n in SHIFTS:
                    nc.vector.tensor_tensor(x[:, p0:p0 + n], zt[:, 0:n, 0], zt[:, d:d + n, 0], ALU.mult).then_inc(s_re, 1)

            def imag_products(t, par):
                at_least(dve, s_x, t)
                zt = z[par]
                for d, p0, n in SHIFTS[:1]:
                    nc.vector.tensor_tensor(im[:, p0:p0 + n], zt[:, 0:n, 1], zt[:, d:d + n, 1], ALU.mult).then_inc(s_im, 1)

            def dots(t):
                dve.wait_ge(s_re, len(SHIFTS) * (t + 1))
                dve.wait_ge(s_im_far, (len(SHIFTS) - 1) * (t + 1))
                dve.wait_ge(s_im, t + 1)
                nc.vector.scalar_tensor_tensor(out=x[:], in0=x[:], scalar=TINY, in1=im[:], op0=ALU.add,
                                               op1=ALU.add).then_inc(s_x, 1)

            def inverses(t):
                for h, s in enumerate(HALVES):
                    dve.wait_ge(s_newt, 2 * t + h + 1)
                    nc.vector.scalar_tensor_tensor(out=seed[:, s], in0=root[:, s], scalar=2.0, in1=seed[:, s],
                                                   op0=ALU.subtract, op1=ALU.mult).then_inc(s_inv, 1)

            def cosines(t):
                dve.wait_ge(s_x, t + 1)
                dve.wait_ge(s_inv, 2 * t + 2)
                for h, s in enumerate(HALVES):
                    nc.vector.tensor_tensor(x[:, s], x[:, s], seed[:, s], ALU.mult).then_inc(s_cos, 1)

            def gains(t):
                cur = lambda s, i, j: s[:, bass.ds(t, 1), i, j]
                dve.wait_ge(s_cos, 2 * (t + 1))
                dve.wait_ge(s_m2, 2 * t + 4)
                for j in range(FAR, N):
                    i = (j + 1) % N
                    nc.vector.tensor_scalar(gain[:, j], x[:, of(i, j)], cur(st_neg, i, j), cur(st, j, j), ALU.mult,
                                            ALU.add).then_inc(s_g0, 1)
                for k in range(2, N):
                    for nth, j in enumerate(ORDER):
                        i = (j + k) % N
                        if k == 2:
                            if j >= FAR:
                                dve.wait_ge(s_g0, (N - FAR) * t + j - FAR + 1)
                            else:
                                dve.wait_ge(s_g0_act, FAR * t + j + 1)
                        elif nth == 0:
                            dve.wait_ge(s_g, (N - 2) * N * t + N)
                        nc.vector.scalar_tensor_tensor(out=gain[:, j], in0=x[:, of(i, j)], scalar=cur(st_neg, i, j),
                                                       in1=gain[:, j], op0=ALU.mult, op1=ALU.add).then_inc(s_g, 1)

            def weight(t, par):
                at_least(dve, s_sf, RI * t)
                dve.wait_ge(s_g, (N - 2) * N * (t + 1))
                nc.vector.tensor_tensor(gz[:, 0:FAR], z[par][:, 0:FAR], gain[:, 0:FAR].unsqueeze(2).to_broadcast([P, FAR, RI, D]),
                                        ALU.mult).then_inc(s_gz, 1)

            def supT_lo(t):
                at_least(dve, s_mf, 2 * t)
                for ri in range(RI):
                    dve.wait_ge(s_shi, RI * t + ri + 1)
                    nc.vector.tensor_tensor(supT[1][:, ri].rearrange("p k f -> p (k f)"), banks[B_SUP + ri][:],
                                            f32(supT[0][:, ri]).rearrange("p k f -> p (k f)"), ALU.subtract).then_inc(s_slo, 1)

            def ampT_lo(t):
                dve.wait_ge(s_phi, t + 1)
                nc.vector.tensor_tensor(ampT[1][:].rearrange("p k f -> p (k f)"), banks[B_AMP][:],
                                        f32(ampT[0][:]).rearrange("p k f -> p (k f)"), ALU.subtract).then_inc(s_plo, 1)

            def norm(t):
                dve.wait_ge(s_n, t + 1)
                nc.vector.reciprocal(rn[:], nrm[:]).then_inc(s_rn, 1)

            def layer(t, yt=y_row[:]):
                if not isinstance(t, int):
                    dve.wait_ge(s_ystored, 16 * t)
                dve.wait_ge(s_rn, t + 1)
                dve.wait_ge(s_yf, t + 1)
                nc.vector.scalar_tensor_tensor(out=yt, in0=banks[B_Y][:], scalar=rn[:], in1=post_b[:],
                                               op0=ALU.mult, op1=ALU.add).then_inc(s_y, 1)
                wait_apart(dve, s_y, t + 1)
                nc.vector.bn_stats(stats[:, bass.ds(t, 1)].rearrange("p a f -> p (a f)"), yt).then_inc(s_yst, 1)

            def amp_sum(t):
                dve.wait_ge(s_a2, 2 * (t + 1))
                nc.vector.tensor_tensor(amp, amp, squares[:, 1], ALU.add).then_inc(s_asum, 1)

            def body(t, par, nth, before=2):
                real_products(t, par, nth)
                inverses(t)
                imag_products(t, par)
                if before > 1:
                    ampT_lo(t - 2)
                dots(t)
                supT_lo(t - 1)
                cosines(t)
                gains(t)
                weight(t, par)
                if before > 1:
                    norm(t - 2)
                    layer(t - 2)
                amp_sum(t - 1)

            real_products(0, 0, 1)
            imag_products(0, 0)
            dots(0)
            dve.wait_ge(s_st, 16)
            nc.vector.tensor_scalar(st_neg[:], st[:], -1.0, None, ALU.mult).then_inc(s_neg_st, 1)
            dve.wait_ge(s_neg_st, 1)
            for h, s in enumerate(HALVES):
                dve.wait_ge(s_seed, h + 1)
                nc.vector.tensor_tensor(root[:, s], root[:, s], seed[:, s], ALU.mult).then_inc(s_newt, 1)
            dve.wait_ge(s_x, 1)
            inverses(0)
            cosines(0)
            def turns(jobs):
                for j in jobs:
                    w, m = TJ[j]
                    dve.wait_ge(s_thi, j + 1)
                    cols = slice(m * P, (m + 1) * P)
                    nc.vector.tensor_tensor(w_dst[w][1][:, :, cols],
                                            banks[TB + j % NTB][:].rearrange("p (k f) -> p k f", k=KD),
                                            f32(w_dst[w][0][:, :, cols]), ALU.subtract).then_inc(s_tlo, 1)

            turns(range(NTB))
            gains(0)
            dve.wait_ge(s_tf, len(TJ))
            weight(0, 0)
            turns(range(NTB, len(TJ)))
            dve.wait_ge(s_vec, 16)
            body(1, 1, 1, before=1)
            with dve.Fori(0, (TILES - 2) // ZBUF) as i:
                for k in range(2, ZBUF + 2):
                    body(ZBUF * i + k, k % ZBUF, i + 1 + k // ZBUF)
            def variances(tiles):
                dve.wait_ge(s_yst, tiles.stop)
                for t in tiles:
                    nc.vector.bn_aggr(mv[:, t], stats[:, t]).then_inc(s_var, 1)

            def layernorm(tiles):
                group = slice(tiles.start, tiles.stop)
                dve.wait_ge(s_std, 1 if tiles.start == 0 else 2)
                nc.vector.reciprocal(rstd[:, group], std[:, group]).then_inc(s_rstd, 1)
                dve.wait_ge(s_rstd, 1 if tiles.start == 0 else 2)
                for t in tiles:
                    nc.vector.tensor_scalar(y[:, t], y[:, t], mv[:, t, 0:1], rstd[:, t:t + 1], ALU.subtract,
                                            ALU.mult).then_inc(s_yn, 1)
                    dve.wait_ge(s_yn, t + 1)
                    nc.vector.tensor_tensor(y[:, t], y[:, t], post_g, ALU.mult).then_inc(s_yg, 1)

            norm(TILES - 2)
            ampT_lo(TILES - 2)
            variances(range(EARLY))
            supT_lo(TILES - 1)
            layer(TILES - 2, y[:, TILES - 2])
            norm(TILES - 1)
            dve.wait_ge(s_gbe, 16 * 2)
            dve.wait_ge(s_yin, 16)
            layernorm(range(EARLY))
            amp_sum(TILES - 1)
            ampT_lo(TILES - 1)
            layer(TILES - 1, y[:, TILES - 1])
            variances(range(EARLY, TILES))
            layernorm(range(EARLY, TILES))


def program(nc, t, out):
    w = lambda name: t["L0_rec_" + name]
    sides = ("r", "i")
    folded = nc.dram_tensor("folded_weights", (KD, P, RI, N * KH, FOLD), F32, kind="Internal").ap()
    attended = nc.dram_tensor("attended", (KD * NQ + 1, P, HC, N, TQ), F32, kind="Internal").ap()
    y_rows = nc.dram_tensor("y_rows_of_tiles", (TILES - 2, P, OUT), F32, kind="Internal").ap()
    states = nc.dram_tensor("states", (N, B, RI, D), F32, kind="Internal").ap()
    bias_rows = [w(f"e{s}_b2") for s in sides] + [w(f"b{p}_{s}") for s in sides for p in "qkv"] + [w(f"bo_{s}") for s in sides]
    n_bias = sum(v.shape[0] for v in bias_rows) // P
    with ExitStack() as ctx:
        E = ctx.enter_context

        class const:
            ident = E(nc.sbuf_tensor("identity", [P, P], F32))
            mask = E(nc.sbuf_tensor("same_token", [P, 32], F32))
            eps = E(nc.sbuf_tensor("eps", [P, 1], F32))
            zero = E(nc.sbuf_tensor("zero", [P, 1], F32))
            scratch = E(nc.sbuf_tensor("scratch", [P, 8], F32))

        banks = [E(nc.psum_tensor(f"bank_{i}", [P, BANK], F32)) for i in range(NB)]
        biasT = E(nc.sbuf_tensor("biasT", [P, n_bias], F32))
        bias_cols = E(nc.sbuf_tensor("bias_cols", [P, KD, RI * NP, N], F32))
        carry = Carry(nc, E)
        with ExitStack() as attention:
            hT = [attention.enter_context(nc.sbuf_tensor(f"hT_{s}", [P, RI, KH, B], F32R)) for s in ("hi", "lo")]
            with ExitStack() as folding:
                enc = Encoded(nc, folding.enter_context)
                proj = [[w(f"W{p}_{s}") for p in "qkv"] for s in sides]
                both = lambda name: [w(f"e{s}_{name}") for s in sides]
                stage_encode(nc, const, carry, enc, banks, t["r_x"], both("W1"), both("b1"), both("g1"), both("be1"),
                             both("W2"), proj, bias_rows, biasT)
                stage_fold(nc, const, carry, enc, hT, banks, proj, biasT, bias_cols, folded)
            stage_attend(nc, const, carry, hT, banks, bias_cols, folded, attended, [w(f"Wo_{s}") for s in sides])
        bo_cols = biasT[:, n_bias - RI * KD:n_bias].rearrange("p (r m) -> p r m", r=RI)
        stage_interact(nc, const, carry, banks, w("int_Wr"), w("int_Wi"), bo_cols, attended, states)
        stage_measure(nc, const, carry, banks, t["r_strength"], w("meas_Mr"), w("meas_Mi"), w("post_W"),
                      [w("post_b"), w("post_g"), w("post_be")], states, y_rows, out)


_INS = ["r_strength", "r_x"] + ["L0_rec_" + n for n in (
    "er_W1", "er_b1", "er_g1", "er_be1", "er_W2", "er_b2", "ei_W1", "ei_b1", "ei_g1", "ei_be1", "ei_W2", "ei_b2",
    "Wq_r", "bq_r", "Wq_i", "bq_i", "Wk_r", "bk_r", "Wk_i", "bk_i", "Wv_r", "bv_r", "Wv_i", "bv_i",
    "Wo_r", "bo_r", "Wo_i", "bo_i", "int_Wr", "int_Wi", "meas_Mr", "meas_Mi", "post_W", "post_b", "post_g", "post_be")]


def kernel(**inputs):
    import numpy as np
    import concourse.bacc as bacc
    from concourse.bass_utils import run_bass_kernel_spmd

    nc = bacc.Bacc("TRN2", target_bir_lowering=False, num_devices=1)
    arrays = {f"in_{n}": np.ascontiguousarray(inputs[n]) for n in _INS}
    tensors = {n: nc.dram_tensor(f"in_{n}", arrays[f"in_{n}"].shape, F32, kind="ExternalInput").ap() for n in _INS}
    out = nc.dram_tensor("out", (B, OUT), F32, kind="ExternalOutput").ap()
    program(nc, tensors, out)
    return run_bass_kernel_spmd(nc, [arrays], core_ids=[0]).results[0]["out"]
```
